# Optimizing a Trainium2 kernel written in Bass

```python
import numpy as np
import jax
import jax.numpy as jnp

def _softmax(x, axis=-1):
    return jax.nn.softmax(x, axis=axis)

def _gelu(x):
    return jax.nn.gelu(x, approximate=True)

def _silu(x):
    return jax.nn.silu(x)

def _sigmoid(x):
    return jax.nn.sigmoid(x)

def _layernorm(x, axis=-1, eps=1e-05):
    m = jnp.mean(x, axis=axis, keepdims=True)
    v = jnp.var(x, axis=axis, keepdims=True)
    return (x - m) / jnp.sqrt(v + eps)

def _scatter_add(tgt, idx, src, axis=0):
    return tgt.at[idx].add(src)

def _segment_sum(src, seg, n):
    return jax.ops.segment_sum(src, seg, n)
kernel_name = 'mk_vit_tower_cls_d1_tok_img1024_r4_82cc04'

def setup_inputs(seed: int=0):
    np.random.seed(seed)
    _w = jnp.asarray

    def _rec_inputs():
        import jax
        import jax.numpy as jnp
        _rk = jax.random.key(seed)
        x = 7.22013e-05 + 1.00017 * jax.random.normal(jax.random.fold_in(_rk, 1), (8, 1, 512, 256), jnp.float32)
        cls_tok = 0.02 * jax.random.normal(jax.random.fold_in(_rk, 5), (1, 1, 256), jnp.float32)
        return (x, cls_tok)
    x, cls_tok = _rec_inputs()

    def _L0_tok_setup():
        import jax, jax.numpy as jnp
        import numpy as np
        import math
        EMBED_DIM = 256
        NUM_HEADS = 16
        HEAD_DIM = EMBED_DIM // NUM_HEADS
        INPUT_DIM = 256
        key = jax.random.key(seed)
        k_x, k_wqkv, k_wout = jax.random.split(key, 3)
        x = jax.random.normal(k_x, (4, 1, 512, INPUT_DIM), dtype=jnp.float32)

        def xavier(k, shape):
            fan_out, fan_in = shape
            bound = math.sqrt(6.0 / (fan_in + fan_out))
            return jax.random.uniform(k, shape, jnp.float32, -bound, bound)
        w_qkv = xavier(k_wqkv, (3 * EMBED_DIM, INPUT_DIM))
        b_qkv = jnp.zeros((3 * EMBED_DIM,), jnp.float32)
        w_out = xavier(k_wout, (EMBED_DIM, EMBED_DIM))
        b_out = jnp.zeros((EMBED_DIM,), jnp.float32)
        return {'x': x, 'w_qkv': w_qkv, 'b_qkv': b_qkv, 'w_out': w_out, 'b_out': b_out}
    _L0_tok_all = _L0_tok_setup()
    _L0_tok_in = {k: v for k, v in _L0_tok_all.items() if k in ('w_qkv', 'b_qkv', 'w_out', 'b_out')}
    del _L0_tok_all

    def _L0_attn_setup():
        import jax, jax.numpy as jnp
        import numpy as np
        BATCH, SEQ, D_MODEL, STATE_DIM = (8, 512, 256, 256)

        def _cayley_circulant_eigenvalues(a_params, n):
            half_n = n // 2
            a_full = jnp.zeros((n,), dtype=a_params.dtype)
            a_full = a_full.at[1:half_n].set(a_params[:half_n - 1])
            a_full = a_full.at[half_n + 1:].set(-a_params[:half_n - 1][::-1])
            omega = jnp.fft.fft(a_full).imag
            w2 = omega * omega
            denom = 1.0 + w2
            return ((1.0 - w2) / denom + 1j * (-2.0 * omega / denom)).astype(jnp.complex64)
        key = jax.random.key(seed)
        k1, k2, k3, k4 = jax.random.split(key, 4)
        u = jax.random.normal(k1, (BATCH, SEQ, D_MODEL), dtype=jnp.float32)
        a_params = jax.random.normal(k2, (STATE_DIM // 2,), dtype=jnp.float32) * 0.1
        B_w = jax.random.normal(k3, (STATE_DIM, D_MODEL), dtype=jnp.float32) / np.sqrt(D_MODEL).astype(np.float32)
        C_w = jax.random.normal(k4, (D_MODEL, STATE_DIM), dtype=jnp.float32) / np.sqrt(STATE_DIM).astype(np.float32)
        D = jnp.zeros((D_MODEL,), dtype=jnp.float32)
        return {'u': u, 'a_params': a_params, 'B_w': B_w, 'C_w': C_w, 'D': D}
    _L0_attn_all = _L0_attn_setup()
    _L0_attn_in = {k: v for k, v in _L0_attn_all.items() if k in ('a_params', 'B_w', 'C_w', 'D')}
    del _L0_attn_all

    def _L0_ffn_setup():
        import jax, jax.numpy as jnp
        import numpy as np
        B, S, H, I, E_ROUTED, TOP_K = (8, 512, 256, 512, 8, 2)

        def _expert(x, Wg, Wu, Wd):
            return jax.nn.silu(x @ Wg.T) * (x @ Wu.T) @ Wd.T
        key = jax.random.key(seed)
        ks = jax.random.split(key, 9)
        s = 0.02
        return {'x': jax.random.normal(ks[0], (B, S, H), dtype=jnp.float32), 'Wg_s': jax.random.normal(ks[1], (I, H), dtype=jnp.float32) * s, 'Wu_s': jax.random.normal(ks[2], (I, H), dtype=jnp.float32) * s, 'Wd_s': jax.random.normal(ks[3], (H, I), dtype=jnp.float32) * s, 'Wg': jax.random.normal(ks[4], (E_ROUTED, I, H), dtype=jnp.float32) * s, 'Wu': jax.random.normal(ks[5], (E_ROUTED, I, H), dtype=jnp.float32) * s, 'Wd': jax.random.normal(ks[6], (E_ROUTED, H, I), dtype=jnp.float32) * s, 'Wr': jax.random.normal(ks[7], (E_ROUTED, H), dtype=jnp.float32) * s, 'rb': jnp.zeros((E_ROUTED,), dtype=jnp.float32)}
    _L0_ffn_all = _L0_ffn_setup()
    _L0_ffn_in = {k: v for k, v in _L0_ffn_all.items() if k in ('Wg_s', 'Wu_s', 'Wd_s', 'Wg', 'Wu', 'Wd', 'Wr', 'rb')}
    del _L0_ffn_all
    return {'x': x, 'cls_tok': cls_tok, 'L0_tok_w_qkv': _L0_tok_in['w_qkv'], 'L0_tok_b_qkv': _L0_tok_in['b_qkv'], 'L0_tok_w_out': _L0_tok_in['w_out'], 'L0_tok_b_out': _L0_tok_in['b_out'], 'L0_attn_a_params': _L0_attn_in['a_params'], 'L0_attn_B_w': _L0_attn_in['B_w'], 'L0_attn_C_w': _L0_attn_in['C_w'], 'L0_attn_D': _L0_attn_in['D'], 'L0_ffn_Wg_s': _L0_ffn_in['Wg_s'], 'L0_ffn_Wu_s': _L0_ffn_in['Wu_s'], 'L0_ffn_Wd_s': _L0_ffn_in['Wd_s'], 'L0_ffn_Wg': _L0_ffn_in['Wg'], 'L0_ffn_Wu': _L0_ffn_in['Wu'], 'L0_ffn_Wd': _L0_ffn_in['Wd'], 'L0_ffn_Wr': _L0_ffn_in['Wr'], 'L0_ffn_rb': _L0_ffn_in['rb']}

def reference(x, cls_tok, L0_tok_w_qkv, L0_tok_b_qkv, L0_tok_w_out, L0_tok_b_out, L0_attn_a_params, L0_attn_B_w, L0_attn_C_w, L0_attn_D, L0_ffn_Wg_s, L0_ffn_Wu_s, L0_ffn_Wd_s, L0_ffn_Wg, L0_ffn_Wu, L0_ffn_Wd, L0_ffn_Wr, L0_ffn_rb):
    import jax
    import jax.numpy as jnp

    def _L0_tok_ref(x, w_qkv, b_qkv, w_out, b_out):
        import jax, jax.numpy as jnp
        import numpy as np
        import math
        EMBED_DIM = 256
        NUM_HEADS = 16
        HEAD_DIM = EMBED_DIM // NUM_HEADS
        INPUT_DIM = 256
        B, y, S, _ = x.shape
        qkv = jnp.einsum('bysd,ed->byse', x, w_qkv) + b_qkv
        qkv = qkv.reshape(B, S, NUM_HEADS, 3 * HEAD_DIM).transpose(0, 2, 1, 3)
        q, k, v = jnp.split(qkv, 3, axis=-1)
        logits = jnp.einsum('bhqd,bhkd->bhqk', q, k) / math.sqrt(HEAD_DIM)
        attn = jax.nn.softmax(logits, axis=-1)
        vals = jnp.einsum('bhqk,bhkd->bhqd', attn, v)
        vals = vals.transpose(0, 2, 1, 3).reshape(B, S, EMBED_DIM)
        return jnp.einsum('bse,oe->bso', vals, w_out) + b_out

    def _L0_attn_ref(u, a_params, B_w, C_w, D):
        import jax, jax.numpy as jnp
        import numpy as np
        BATCH, SEQ, D_MODEL, STATE_DIM = (8, 512, 256, 256)

        def _cayley_circulant_eigenvalues(a_params, n):
            half_n = n // 2
            a_full = jnp.zeros((n,), dtype=a_params.dtype)
            a_full = a_full.at[1:half_n].set(a_params[:half_n - 1])
            a_full = a_full.at[half_n + 1:].set(-a_params[:half_n - 1][::-1])
            omega = jnp.fft.fft(a_full).imag
            w2 = omega * omega
            denom = 1.0 + w2
            return ((1.0 - w2) / denom + 1j * (-2.0 * omega / denom)).astype(jnp.complex64)
        n = B_w.shape[0]
        lambdas = _cayley_circulant_eigenvalues(a_params, n)
        Bu = jnp.einsum('bsd,nd->bsn', u, B_w)

        def step(h, bu_t):
            Wh = jnp.fft.ifft(lambdas * jnp.fft.fft(h.astype(jnp.float32))).real.astype(h.dtype)
            h_new = Wh + bu_t
            return (h_new, h_new)
        h0 = jnp.zeros((u.shape[0], n), dtype=u.dtype)
        _, hs = jax.lax.scan(step, h0, jnp.swapaxes(Bu, 0, 1))
        y = jnp.einsum('sbn,dn->bsd', hs, C_w) + D * u
        return y

    def _L0_ffn_ref(x, Wg_s, Wu_s, Wd_s, Wg, Wu, Wd, Wr, rb):
        import jax, jax.numpy as jnp
        import numpy as np
        B, S, H, I, E_ROUTED, TOP_K = (8, 512, 256, 512, 8, 2)

        def _expert(x, Wg, Wu, Wd):
            return jax.nn.silu(x @ Wg.T) * (x @ Wu.T) @ Wd.T
        shared = _expert(x, Wg_s, Wu_s, Wd_s)
        logits = jnp.einsum('bsh,eh->bse', x, Wr) + rb
        probs = jax.nn.sigmoid(logits)
        scores, idx = jax.lax.top_k(probs, TOP_K)
        cw = (jax.nn.one_hot(idx, E_ROUTED, dtype=x.dtype) * scores[..., None]).sum(-2)
        out = shared
        for e in range(E_ROUTED):
            out = out + cw[..., e:e + 1] * _expert(x, Wg[e], Wu[e], Wd[e])
        return out
    h = _L0_tok_ref(x, L0_tok_w_qkv, L0_tok_b_qkv, L0_tok_w_out, L0_tok_b_out)
    h = jnp.concatenate([jnp.broadcast_to(cls_tok, (h.shape[0], 1, h.shape[2])), h], axis=1)
    h = h + _L0_attn_ref(_layernorm(h, axis=-1), L0_attn_a_params, L0_attn_B_w, L0_attn_C_w, L0_attn_D)
    h = h + _L0_ffn_ref(_layernorm(h, axis=-1), L0_ffn_Wg_s, L0_ffn_Wu_s, L0_ffn_Wd_s, L0_ffn_Wg, L0_ffn_Wu, L0_ffn_Wd, L0_ffn_Wr, L0_ffn_rb)
    return h

_drawn_inputs = setup_inputs


def setup_inputs(seed=0):
    import zlib

    import numpy as np

    out = dict(_drawn_inputs(seed))
    spreads = {'L0_tok_b_qkv': (0.0, 0.1),
     'L0_tok_b_out': (0.0, 0.1),
     'L0_attn_D': (0.0, 0.8),
     'L0_ffn_rb': (0.0, 0.8)}
    factors = {'L0_ffn_Wg_s': 8.0,
     'L0_ffn_Wu_s': 8.0,
     'L0_ffn_Wd_s': 8.0,
     'L0_ffn_Wg': 8.0,
     'L0_ffn_Wu': 8.0,
     'L0_ffn_Wd': 8.0,
     'L0_ffn_Wr': 8.0}
    for name, (base, spread) in spreads.items():
        noise = np.random.default_rng([zlib.crc32(name.encode()), seed]).standard_normal(out[name].shape)
        drawn = base * np.exp(spread * noise) if base else spread * noise
        out[name] = jnp.asarray(drawn.astype(out[name].dtype))
    for name, factor in factors.items():
        out[name] = (out[name] * factor).astype(out[name].dtype)
    return out
```

```python
from contextlib import ExitStack

import numpy as np

import concourse.bass as bass
from concourse import mybir

FP32 = mybir.dt.float32
BF16 = mybir.dt.bfloat16
I32 = mybir.dt.int32
U32 = mybir.dt.uint32
ALU = mybir.AluOpType
ACT = mybir.ActivationFunctionType
AX = mybir.AxisListType

P = 128
B, S, D = 8, 512, 256
DC = D // P
TT = S // P
H, HD = 16, 16
G = 4
NG = H // G
PARTS = 3
Q_PART = (0, 0, 0, 1, 1, 2)
K_PART = (0, 1, 2, 0, 1, 0)
KROWS = HD * len(Q_PART)
SROWS = KROWS + PARTS
VW = 2 * HD

E = 8
F = 512
FC = F // P
T1 = S + 1
ROWS = B * T1
CAP = (B * S + 1 + P - 1) // P
TILES = (2 * (B * S + 1) + E * (P - 1)) // P + 1 & -2
SPARE = TILES - 2 * (B * S + 1) // P
SLOTS = (E * CAP + SPARE) * P
EPS = 1e-5


def places(nc, ctx):
    def sb(name, shape, dtype):
        return ctx.enter_context(nc.sbuf_tensor(name, shape, dtype))

    def pb(name, shape, dtype):
        return ctx.enter_context(nc.psum_tensor(name, shape, dtype))

    def sem(name):
        return ctx.enter_context(nc.semaphore(name))

    return sb, pb, sem


def stage_qkv(nc, mem, dram):
    wqkv, bqk, bv = mem["wqkv"], mem["bqk"], mem["bv"]
    with ExitStack() as ctx:
        sb, pb, sem = places(nc, ctx)
        xt = sb("x_T", [P, 2, DC, S], FP32)
        qk_full = sb("qk_full", [P, 4, S], FP32)
        qk_rest = sb("qk_rest", [P, 4, S], FP32)
        qk_parts = sb("qk_parts", [P, 4, PARTS, S], BF16)
        v_ones = sb("v_ones", [P, TT, H, VW], FP32)
        qk_ps = pb("qk_ps", [P, 4, S], FP32)
        v_ps = pb("v_ps", [P, 2, 2, D], FP32)
        weights_in = sem("weights_in")
        x_in = [sem(f"x_in{n}") for n in range(2)]
        x_used = [sem(f"x_used{n}") for n in range(2)]
        qk_out = [sem(f"qk_out{n}") for n in range(4)]
        cut = [sem(f"cut{n}") for n in range(4)]
        parts_stored = [sem(f"parts_stored{n}") for n in range(4)]
        qk_made = sem("qk_made")
        v_half_made = sem("v_half_made")
        cut_step = sem("cut_step")
        v_step = sem("v_step")
        v_stored = sem("v_stored")
        ones_set = sem("ones_set")
        block = ctx.enter_context(nc.Block())

        @block.gpsimd
        def _(pool):
            pool.memset(v_ones[:, :, :, :], 1.0).then_inc(ones_set, 1)
            with pool.Fori(0, B // 2) as i:
                for par in range(2):
                    pool.wait_ge(x_used[par], i)
                    pool.wait_ge(ones_set, 1)
                    pool.dma_start(xt[:, par, :, :], dram["xT"][bass.ds(2 * i + par, 1), :, :, :]
                                   .rearrange("b c p t -> p (b c) t")).then_inc(x_in[par], 16)

        @block.sync
        def _(sp):
            for dst, src in mem["first_loads"]:
                sp.dma_start(dst, src).then_inc(weights_in, 16)
            with sp.Fori(0, B) as b:
                for j in range(4):
                    sp.wait_ge(cut[j], b + 1)
                    sp.dma_start(
                        dram["qk"][bass.ds(b, 1), j // 2, :, (j % 2) * P:(j % 2 + 1) * P, :]
                        .rearrange("b s p n -> p (b s) n"), qk_parts[:, j, :, :]).then_inc(parts_stored[j], 16)
                sp.wait_ge(v_step, TT * b + TT)
                sp.dma_start(dram["v"][bass.ds(b, 1), :, :].rearrange("b p n -> p (b n)"),
                             v_ones[:, :, :, :].rearrange("p t h w -> p (t h w)")).then_inc(v_stored, 16)
            for j in range(4):
                sp.wait_ge(parts_stored[j], 16 * B)
            sp.wait_ge(v_stored, 16 * B)
            for dst, src in mem["later_loads"]:
                sp.dma_start(dst, src).then_inc(mem["later_in"], 16)

        @block.tensor
        def _(pe):
            pe.wait_ge(weights_in, 16 * len(mem["first_loads"]))
            with pe.Fori(0, B // 2) as i:
                for par in range(2):
                    b = 2 * i + par
                    pe.wait_ge(x_in[par], 16 * i + 16)
                    for j in range(4):
                        pe.wait_ge(qk_out[j], b)
                        for c in range(DC):
                            mm = pe.matmul(qk_ps[:, j, :], wqkv[:, c, j * P:(j + 1) * P], xt[:, par, c, :],
                                           start=(c == 0), stop=(c == DC - 1))
                        mm.then_inc(qk_made, 1)
                    pe.wait_ge(v_step, TT * b)
                    for t in range(TT):
                        for c in range(DC):
                            mm = pe.matmul(v_ps[:, t // 2, t % 2, :], xt[:, par, c, t * P:(t + 1) * P],
                                           wqkv[:, c, 2 * D:3 * D], start=(c == 0), stop=(c == DC - 1))
                        if t == 1:
                            mm.then_inc(v_half_made, 1)
                    mm.then_inc(x_used[par], 1)

        @block.scalar
        def _(act):
            act.wait_ge(weights_in, 16 * len(mem["first_loads"]))
            with act.Fori(0, B) as b:
                for j in range(4):
                    act.wait_ge(cut[j], b)
                    act.wait_ge(qk_made, 4 * b + j + 1)
                    act.activation(qk_full[:, j, :], qk_ps[:, j, :], ACT.Identity,
                                   bias=bqk[:, j:j + 1]).then_inc(qk_out[j], 1)

        @block.vector
        def _(dve):
            dve.wait_ge(weights_in, 16 * len(mem["first_loads"]))
            dve.wait_ge(ones_set, 1)
            with dve.Fori(0, B // 2) as i:
                for par in range(2):
                    b = 2 * i + par
                    for j in range(4):
                        full, rest, parts = qk_full[:, j, :], qk_rest[:, j, :], qk_parts[:, j, :, :]
                        n = 12 * b + 3 * j
                        dve.wait_ge(parts_stored[j], 16 * b)
                        dve.wait_ge(qk_out[j], b + 1)
                        dve.tensor_copy(parts[:, 0, :], full).then_inc(cut_step, 1)
                        dve.wait_ge(cut_step, n + 1)
                        dve.tensor_tensor(rest, full, parts[:, 0, :], ALU.subtract).then_inc(cut_step, 1)
                        dve.wait_ge(cut_step, n + 2)
                        dve.tensor_copy(parts[:, 1, :], rest).then_inc(cut_step, 1)
                        dve.wait_ge(cut_step, n + 3)
                        dve.tensor_tensor(parts[:, 2, :], rest, parts[:, 1, :], ALU.subtract).then_inc(cut[j], 1)
                    dve.wait_ge(v_stored, 16 * b)
                    for t in range(TT):
                        if t < 2:
                            dve.wait_ge(v_half_made, b + 1)
                        else:
                            dve.wait_ge(x_used[par], i + 1)
                        dve.tensor_tensor(v_ones[:, t, :, 0:HD],
                                          v_ps[:, t // 2, t % 2, :].rearrange("p (h d) -> p h d", h=H),
                                          bv[:, :].rearrange("p (h d) -> p h d", h=H), ALU.add).then_inc(v_step, 1)


def stage_attention(nc, mem, dram):
    ident, identb = mem["ident"], mem["identb"]
    with ExitStack() as ctx:
        sb, pb, sem = places(nc, ctx)
        q_rows = sb("q_rows", [P, NG, G, S], BF16)
        k_rows = sb("k_rows", [P, NG, G, S], BF16)
        v_unit = sb("v_unit", [P, NG, TT, G, VW], FP32)
        probs = sb("probs", [P, 8, 2, S], FP32)
        neg_max = sb("neg_max", [P, G * TT], FP32)
        neg_rest = sb("neg_rest", [P, G * TT], FP32)
        max_parts = sb("max_parts", [P, P // (G * TT), G * TT], BF16)
        max_rows = sb("max_rows", [PARTS * G * TT, P], BF16)
        heads_T = sb("heads_T", [P, S], FP32)
        row_sum = sb("row_sum", [P, TT, G], FP32)
        heads = sb("heads_sb", [P, TT, D], FP32)
        by_query = pb("by_query", [P, 2, S], FP32)
        by_key = pb("by_key", [P, 2, 2, S], FP32)
        pv = pb("pv", [P, S], FP32)
        turned = pb("turned", [P, S], FP32)
        unit_in = [sem(f"unit_in{n}") for n in range(NG)]
        unit_used = [sem(f"unit_used{n}") for n in range(NG)]
        max_in = [sem(f"max_in{n}") for n in range(NG)]
        exp_done = [sem(f"exp_done{n}") for n in range(2)]
        ones_row = sem("ones_row")
        query_scored = sem("query_scored")
        max_taken = sem("max_taken")
        max_split = sem("max_split")
        max_turned = sem("max_turned")
        max_copied = sem("max_copied")
        key_scored = sem("key_scored")
        pv_copied = sem("pv_copied")
        heads_turned = sem("heads_turned")
        sum_inv = sem("sum_inv")
        heads_done = sem("heads_done")
        heads_stored = sem("heads_stored")
        block = ctx.enter_context(nc.Block())
        LOADS = 2 * len(Q_PART) + 1
        turned_max = turned[:, 0:P // 2].bitcast(BF16)
        LAST = B - 1

        @block.gpsimd
        def _(pool):
            pool.memset(max_parts[:, :, :], 0.0).then_inc(ones_row, 1)
            pool.wait_ge(ones_row, 1)
            pool.memset(k_rows[KROWS:P, :, :, :], 1.0).then_inc(ones_row, 1)
            pool.memset(q_rows[KROWS:P, :, :, :], 0.0).then_inc(ones_row, 1)
            with pool.Fori(0, B) as b:
                pool.wait_ge(heads_done, NG * b + NG)
                pool.wait_ge(ones_row, 3)
                pool.dma_start(dram["heads"][bass.ds(b, 1), :, :].rearrange("b p n -> p (b n)"),
                               heads[:, :, :].rearrange("p t n -> p (t n)")).then_inc(heads_stored, 16)
            pool.wait_ge(heads_stored, 16 * B)

        @block.sync
        def _(sp):
            with sp.Fori(0, B) as b:
                for g in range(NG):
                    sp.wait_ge(unit_used[g], b)
                    for which, rows, order in ((0, q_rows, Q_PART), (1, k_rows, K_PART)):
                        for n, s in enumerate(order):
                            sp.dma_start(rows[HD * n:HD * (n + 1), g, :, :],
                                         dram["qk"][bass.ds(b, 1), which, s, G * HD * g:G * HD * (g + 1), :]
                                         .rearrange("b (h d) n -> d (b h) n", h=G)).then_inc(unit_in[g], 16)
                    sp.dma_start(v_unit[:, g, :, :, :].rearrange("p t h w -> p t (h w)"),
                                 dram["v"][bass.ds(b, 1), :, :].rearrange("b p (t n) -> p (b t) n", t=TT)
                                 [:, :, G * VW * g:G * VW * (g + 1)]).then_inc(unit_in[g], 16)

        @block.tensor
        def _(pe):
            def score_by_query(b, g, k):
                n = (NG * b + g) * G * TT + k
                h, t = k // TT, k % TT
                if not (isinstance(n, int) and n < 2):
                    pe.wait_ge(max_taken, n - 1)
                pe.matmul(by_query[:, k % 2, :],
                          q_rows[0:KROWS, g, h, t * P:(t + 1) * P], k_rows[0:KROWS, g, h, :],
                          start=True, stop=True).then_inc(query_scored, 1)

            def score_by_key(b, g, i):
                pair, h = i // G, i % G
                pe.wait_ge(exp_done[i % 2], 16 * b + 4 * g + i // 2)
                for t in range(2):
                    kt = 2 * pair + t
                    mm = pe.matmul(by_key[:, i % 2, t, :], k_rows[0:SROWS, g, h, kt * P:(kt + 1) * P],
                                   q_rows[0:SROWS, g, h, :], start=True, stop=True)
                mm.then_inc(key_scored, 1)

            def add_pv(b, g, pair, t):
                kt = 2 * pair + t
                if kt == 0:
                    pe.wait_ge(pv_copied, NG * b + g)
                if t == 0:
                    for buf in range(2):
                        pe.wait_ge(exp_done[buf], 16 * b + 4 * g + 2 * pair + 2)
                for h in range(G):
                    mm = pe.matmul(pv[VW * h:VW * (h + 1), :], v_unit[:, g, kt, h, :],
                                   probs[:, G * pair + h, t, :], start=(kt == 0), stop=(kt == TT - 1))
                if kt == TT - 1:
                    mm.then_inc(unit_used[g], 1)

            def turn_max(b, g):
                pe.wait_ge(max_split, 4 * (NG * b + g) + 4)
                pe.transpose(turned_max, max_parts[:, :, :].rearrange("p s n -> p (s n)"),
                             identb[:, :]).then_inc(max_turned, 1)

            def turn_heads(b, g):
                pe.wait_ge(pv_copied, NG * b + g + 1)
                pe.wait_ge(heads_done, NG * b + g)
                for t in range(TT):
                    mm = pe.transpose(turned[:, t * P:(t + 1) * P], heads_T[:, t * P:(t + 1) * P], ident[:, :])
                mm.then_inc(heads_turned, 1)

            def unit(b, g):
                b1, g1 = b + (g + 2) // NG, (g + 2) % NG
                ahead = not (isinstance(b1, int) and b1 > LAST)
                bm, gm = b + (g + 1) // NG, (g + 1) % NG
                next_max = not (isinstance(bm, int) and bm > LAST)
                by_q = [k for k in range(G * TT)] if ahead else []
                if ahead:
                    pe.wait_ge(unit_in[g1], 16 * LOADS * (b1 + 1))
                pe.wait_ge(max_in[g], 16 * (b + 1))
                for i in range(8):
                    score_by_key(b, g, i)
                    if i == 1 and next_max:
                        if g > 0:
                            pe.wait_ge(heads_done, NG * b + g - 1)
                        else:
                            pe.wait_ge(heads_done, NG * b)
                        turn_max(bm, gm)
                    if i == 4 and g > 0:
                        if next_max:
                            pe.wait_ge(max_copied, NG * bm + gm + 1)
                        turn_heads(b, g - 1)
                    if i == 5:
                        add_pv(b, g, 0, 0)
                    if i == 6:
                        add_pv(b, g, 0, 1)
                    if i >= 1:
                        for k in by_q[2 * (i - 1):2 * i]:
                            score_by_query(b1, g1, k)
                for k in by_q[14:]:
                    score_by_query(b1, g1, k)
                add_pv(b, g, 1, 0)
                add_pv(b, g, 1, 1)
                if g == NG - 1:
                    turn_heads(b, g)

            pe.wait_ge(ones_row, 3)
            for g in range(2):
                pe.wait_ge(unit_in[g], 16 * LOADS)
                for k in range(G * TT):
                    score_by_query(0, g, k)
                if g == 0:
                    turn_max(0, 0)
            with pe.Fori(0, LAST) as b:
                for g in range(NG):
                    unit(b, g)
            for g in range(NG):
                unit(LAST, g)

        @block.vector
        def _(dve):
            def take_max(b, g, k):
                n = (NG * b + g) * G * TT + k
                dve.wait_ge(query_scored, n + 1)
                dve.tensor_reduce(neg_max[:, k:k + 1], by_query[:, k % 2, :], AX.X, ALU.max,
                                  negate=True).then_inc(max_taken, 1)

            def split_max(b, g):
                u = NG * b + g
                dve.wait_ge(max_taken, G * TT * (u + 1))
                dve.wait_ge(max_turned, u)
                dve.tensor_copy(max_parts[:, 0, :], neg_max[:, :]).then_inc(max_split, 1)
                dve.wait_ge(max_split, 4 * u + 1)
                dve.tensor_tensor(neg_rest[:, :], neg_max[:, :], max_parts[:, 0, :],
                                  ALU.subtract).then_inc(max_split, 1)
                dve.wait_ge(max_split, 4 * u + 2)
                dve.tensor_copy(max_parts[:, 1, :], neg_rest[:, :]).then_inc(max_split, 1)
                dve.wait_ge(max_split, 4 * u + 3)
                dve.tensor_tensor(max_parts[:, 2, :], neg_rest[:, :], max_parts[:, 1, :],
                                  ALU.subtract).then_inc(max_split, 1)
                dve.wait_ge(max_split, 4 * u + 4)

            def normalise(b, g):
                u = NG * b + g
                cols = turned[:, :].rearrange("p (t h w) -> p t h w", t=TT, h=G)
                dve.wait_ge(heads_turned, u + 1)
                dve.reciprocal(row_sum[:, :, :], cols[:, :, :, HD]).then_inc(sum_inv, 1)
                dve.wait_ge(sum_inv, u + 1)
                if g == 0:
                    dve.wait_ge(heads_stored, 16 * b)
                dve.tensor_tensor(heads[:, :, G * HD * g:G * HD * (g + 1)].rearrange("p t (h w) -> p t h w", h=G),
                                  cols[:, :, :, 0:HD],
                                  row_sum[:, :, :].unsqueeze(3).to_broadcast([P, TT, G, HD]),
                                  ALU.mult).then_inc(heads_done, 1)

            def unit(b, g):
                b1, g1 = b + (g + 2) // NG, (g + 2) % NG
                ahead = not (isinstance(b1, int) and b1 > LAST)
                for k in range(G * TT if ahead else 0):
                    take_max(b1, g1, k)
                    if k == 9 and g > 0:
                        normalise(b, g - 1)
                if ahead:
                    split_max(b1, g1)
                elif g > 0:
                    normalise(b, g - 1)
                if g == NG - 1:
                    normalise(b, g)

            dve.wait_ge(ones_row, 3)
            for g in range(2):
                for k in range(G * TT):
                    take_max(0, g, k)
                split_max(0, g)
            with dve.Fori(0, LAST) as b:
                for g in range(NG):
                    unit(b, g)
            for g in range(NG):
                unit(LAST, g)

        @block.scalar
        def _(act):
            def place_max(b, g):
                u = NG * b + g
                act.wait_ge(max_turned, u + 1)
                if not (isinstance(u, int) and u < 1):
                    ub, ug = (b, g - 1) if g else (b - 1, NG - 1)
                    act.wait_ge(max_in[ug], 16 * ub + 16)
                act.activation(max_rows[:, :], turned_max[0:PARTS * G * TT, :], ACT.Copy).then_inc(max_copied, 1)
                act.wait_ge(max_copied, u + 1)
                act.wait_ge(unit_used[g], b)
                act.dma_start(q_rows[KROWS:SROWS, g, :, :].rearrange("s h (t p) -> s (h t) p", t=TT),
                              max_rows[:, :]).then_inc(max_in[g], 16)

            def exponentials(b, g, i):
                act.wait_ge(key_scored, 8 * (NG * b + g) + i + 1)
                if i % G == 0:
                    act.wait_ge(unit_used[g - 1] if g else unit_used[NG - 1], b + 1 if g else b)
                act.activation(probs[:, i, :, :], by_key[:, i % 2, :, :], ACT.Exp,
                               scale=float(HD) ** -0.5).then_inc(exp_done[i % 2], 1)

            def unit(b, g):
                bm, gm = b + (g + 1) // NG, (g + 1) % NG
                for i in range(8):
                    exponentials(b, g, i)
                    if i == 1 and not (isinstance(bm, int) and bm > LAST):
                        place_max(bm, gm)
                act.wait_ge(unit_used[g], b + 1)
                act.wait_ge(heads_turned, NG * b + g)
                act.activation(heads_T[:, :], pv[:, :], ACT.Copy).then_inc(pv_copied, 1)

            act.wait_ge(ones_row, 3)
            place_max(0, 0)
            with act.Fori(0, LAST) as b:
                for g in range(NG):
                    unit(b, g)
            for g in range(NG):
                unit(LAST, g)


def chain(eng, sem, start):
    count = [0]

    def link(instruction, wait=True):
        count[0] += 1
        instruction.then_inc(sem, 1)
        if wait:
            eng.wait_ge(sem, start + count[0])

    return link


def top_two(dve, link, mem, probs, t):
    iota = mem["iota_e"][:, :].unsqueeze(1).to_broadcast([P, t, E])
    eq, key, least = mem["eq"][:, 0:t, :], mem["key"][:, 0:t, :], mem["least"][:, 0:t]
    for n in range(2):
        best, hot = mem["best"][:, 0:t, n], mem["hot"][:, 0:t, n, :]
        link(dve.tensor_reduce(best, probs, AX.X, ALU.max))
        link(dve.tensor_tensor(eq, probs, best.unsqueeze(2).to_broadcast([P, t, E]), ALU.is_equal))
        link(dve.tensor_scalar(eq, eq, -float(E), None, ALU.mult))
        link(dve.tensor_tensor(key, eq, iota, ALU.add))
        link(dve.tensor_reduce(least, key, AX.X, ALU.min))
        link(dve.tensor_tensor(hot, key, least.unsqueeze(2).to_broadcast([P, t, E]), ALU.is_equal))
        if n == 0:
            link(dve.tensor_scalar(key, hot, -4.0, None, ALU.mult))
            link(dve.tensor_tensor(probs, probs, key, ALU.add))


TOP_STEPS = 14


def slot_rows(dve, link, mem, t, row_id):
    pos, picked, slot_f = mem["pos"][:, 0:t, :], mem["eq"][:, 0:t, :], mem["slot_f"]
    for n in range(2):
        link(dve.tensor_tensor(picked, mem["hot"][:, 0:t, n, :], pos, ALU.mult))
        link(dve.tensor_reduce(slot_f[:, 0:t, n], picked, AX.X, ALU.add))
        link(dve.tensor_copy(mem["pay"][:, 0:t, n, 0], row_id))
        link(dve.tensor_copy(mem["pay"][:, 0:t, n, 1].bitcast(FP32), mem["best"][:, 0:t, n]))


SLOT_STEPS = 8


def stage_setup(nc, mem, dram):
    with ExitStack() as ctx:
        sb, pb, sem = places(nc, ctx)
        a_col = sb("a_col", [P, 1], FP32)
        sine = sb("sine", [P, P], FP32)
        b_w = sb("b_w", [P, 2, D], FP32)
        c_T = sb("c_T", [P, 2, D], FP32)
        to_planes = sb("to_planes", [P, 2, D], FP32)
        from_planes = sb("from_planes", [P, 2, D], FP32)
        h = sb("cls_h", [P, D], FP32)
        u = sb("cls_u", [P, D], FP32)
        ud = sb("cls_ud", [P, D], FP32)
        u2 = sb("cls_u2", [P, D], FP32)
        stats = sb("cls_stats", [P, 2, 6], FP32)
        mv = sb("cls_mv", [P, 2, 2], FP32)
        rstd = sb("cls_rstd", [P, 2], FP32)
        u_T = sb("cls_u_T", [P, 2, P], FP32)
        bu = sb("cls_bu", [P, 2, P], FP32)
        u2_T = sb("cls_u2_T", [P, 2, P], FP32)
        gate = sb("cls_gate", [P, FC, P], FP32)
        act_T = sb("cls_act_T", [P, FC, P], FP32)
        probs = sb("cls_probs", [P, 1, E], FP32)
        lam = sb("lam", [P, 8], FP32)
        power = sb("power", [P, 11, 2], FP32)
        turned_c = sb("turned_c", [P, S // 2], FP32)
        turned_s = sb("turned_s", [P, S // 2], FP32)
        ps = [pb(f"setup_ps{n}", [P, S], FP32) for n in range(8)]
        names = ("loads first_row stats1 stats2 pow1 pow2 u_done u_turned uT_copied omega m1_made m1_copied "
                 "m2_made m2_copied bu_made bu_copied ud_done y_made h2_done u2_done u2_turned u2T_copied "
                 "logits logits_biased sigmoid gu_made silu act_done down_made acc_done slots stored "
                 "zeros table_set slots_out dve_steps")
        ev = {n: sem("setup_" + n) for n in names.split()}
        block = ctx.enter_context(nc.Block())
        loads = [(h[:, :], dram["cls"].to_broadcast([P, D])), (a_col[:, :], dram["a_params"]),
                 (sine[:, :], dram["sine"]), (b_w[:, :, :], dram["b_w"]), (c_T[:, :, :], dram["c_T"]),
                 (to_planes[:, :, :], dram["to_planes"]), (from_planes[:, :, :], dram["from_planes"])]

        @block.sync
        def _(sp):
            for dst, src in loads:
                sp.dma_start(dst, src).then_inc(ev["loads"], 16)
            sp.dma_start(dram["table"][0:SLOTS, :].rearrange("(p n) c -> p (n c)", p=P),
                         dram["table_init"].rearrange("(p n) c -> p (n c)", p=P)).then_inc(ev["table_set"], 16)
            sp.wait_ge(ev["zeros"], 1)
            sp.dma_start(dram["x_rows"][ROWS:ROWS + P, :], mem["zeros"][:, :]).then_inc(ev["stored"], 16)
            sp.dma_start(dram["out"][ROWS:ROWS + P, :], mem["zeros"][:, :]).then_inc(ev["stored"], 16)
            sp.wait_ge(ev["u2_done"], 1)
            sp.dma_start(dram["x_rows"][0:ROWS, :].rearrange("(b t) n -> b t n", t=T1)[:, 0, :],
                         u2[0:B, :]).then_inc(ev["stored"], 16)
            sp.wait_ge(ev["acc_done"], 1)
            sp.dma_start(dram["out"][0:ROWS, :].rearrange("(b t) n -> b t n", t=T1)[:, 0, :],
                         h[0:B, :]).then_inc(ev["stored"], 16)
            sp.wait_ge(ev["table_set"], 16)
            sp.wait_ge(ev["stored"], 16 * 4)

        @block.gpsimd
        def _(pool):
            pool.wait_ge(ev["stats1"], 1)
            pool.tensor_tensor(rstd[:, 0:1], mv[:, 0, 1:2], mem["minus_half"][:, 0:1], ALU.pow).then_inc(ev["pow1"], 1)
            pool.wait_ge(ev["stats2"], 1)
            pool.tensor_tensor(rstd[:, 1:2], mv[:, 1, 1:2], mem["minus_half"][:, 0:1], ALU.pow).then_inc(ev["pow2"], 1)
            pool.wait_ge(ev["table_set"], 16)
            pool.wait_ge(ev["slots"], 1)
            for n in range(2):
                pool.indirect_dma_start(
                    out=dram["table"], out_offset=bass.IndirectOffsetOnAxis(ap=mem["slot_i"][:, 0, n:n + 1].bitcast(U32), axis=0),
                    in_=mem["pay"][:, 0, n, :], in_offset=None).then_inc(ev["slots_out"], 16)
            pool.wait_ge(ev["slots_out"], 16 * 2)

        @block.scalar
        def _(act):
            act.wait_ge(ev["m1_made"], 1)
            act.activation(mem["m1_T"][:, :, :], ps[1][:, :].rearrange("p (m n) -> p m n", m=2), ACT.Copy).then_inc(ev["m1_copied"], 1)
            act.wait_ge(ev["m2_made"], 1)
            act.activation(mem["m2_T"][:, :, :], ps[2][:, :].rearrange("p (m n) -> p m n", m=2), ACT.Copy).then_inc(ev["m2_copied"], 1)
            act.wait_ge(ev["u_turned"], 1)
            act.activation(u_T[:, :, :], ps[3][:, 0:D].rearrange("p (c n) -> p c n", c=2), ACT.Copy).then_inc(ev["uT_copied"], 1)
            act.wait_ge(ev["bu_made"], 1)
            act.activation(bu[:, :, :], ps[4][:, 0:D].rearrange("p (c n) -> p c n", c=2), ACT.Copy).then_inc(ev["bu_copied"], 1)
            act.wait_ge(ev["u2_turned"], 1)
            act.activation(u2_T[:, :, :], ps[3][:, 0:D].rearrange("p (c n) -> p c n", c=2), ACT.Copy).then_inc(ev["u2T_copied"], 1)
            act.wait_ge(ev["logits_biased"], 1)
            act.activation(probs[:, :, :], probs[:, :, :], ACT.Sigmoid).then_inc(ev["sigmoid"], 1)
            act.wait_ge(ev["gu_made"], 1)
            act.activation(gate[:, :, :], ps[6][:, :].rearrange("p (m n) -> p m n", m=FC), ACT.Silu).then_inc(ev["silu"], 1)

        @block.tensor
        def _(pe):
            pe.wait_ge(ev["loads"], 16 * len(loads))
            pe.wait_ge(mem["later_in"], 16 * len(mem["later_loads"]))
            pe.matmul(ps[0][:, 0:1], sine[:, :], a_col[:, :], start=True, stop=True).then_inc(ev["omega"], 1)
            for m in range(2):
                for c in range(2):
                    mm = pe.matmul(ps[1][:, m * D:(m + 1) * D], b_w[:, c, m * P:(m + 1) * P], to_planes[:, c, :],
                                   start=(c == 0), stop=(c == 1))
            mm.then_inc(ev["m1_made"], 1)
            for m in range(2):
                for c in range(2):
                    mm = pe.matmul(ps[2][:, m * D:(m + 1) * D], from_planes[:, c, m * P:(m + 1) * P], c_T[:, c, :],
                                   start=(c == 0), stop=(c == 1))
            mm.then_inc(ev["m2_made"], 1)
            pe.wait_ge(ev["u_done"], 1)
            for c in range(2):
                mm = pe.transpose(ps[3][:, c * P:(c + 1) * P], u[:, c * P:(c + 1) * P], mem["ident"][:, :])
            mm.then_inc(ev["u_turned"], 1)
            pe.wait_ge(ev["uT_copied"], 1)
            pe.wait_ge(ev["m1_copied"], 1)
            for m in range(2):
                for c in range(2):
                    mm = pe.matmul(ps[4][:, m * P:(m + 1) * P], mem["m1_T"][:, c, m * P:(m + 1) * P], u_T[:, c, :],
                                   start=(c == 0), stop=(c == 1))
            mm.then_inc(ev["bu_made"], 1)
            pe.wait_ge(ev["bu_copied"], 1)
            pe.wait_ge(ev["m2_copied"], 1)
            for m in range(2):
                mm = pe.matmul(ps[5][:, 0:D], bu[:, m, :], mem["m2_T"][:, m, :], start=(m == 0), stop=(m == 1))
            mm.then_inc(ev["y_made"], 1)
            pe.wait_ge(ev["u2_done"], 1)
            for c in range(2):
                mm = pe.transpose(ps[3][:, c * P:(c + 1) * P], u2[:, c * P:(c + 1) * P], mem["ident"][:, :])
            mm.then_inc(ev["u2_turned"], 1)
            pe.wait_ge(ev["u2T_copied"], 1)
            for c in range(2):
                mm = pe.matmul(ps[4][:, 0:E], u2_T[:, c, :], mem["wr_T"][:, c, :], start=(c == 0), stop=(c == 1))
            mm.then_inc(ev["logits"], 1)
            for bank, w in ((6, mem["wg_s"]), (7, mem["wu_s"])):
                for m in range(FC):
                    for c in range(2):
                        mm = pe.matmul(ps[bank][:, m * P:(m + 1) * P], w[:, c, m * P:(m + 1) * P], u2_T[:, c, :],
                                       start=(c == 0), stop=(c == 1))
            mm.then_inc(ev["gu_made"], 1)
            pe.wait_ge(ev["act_done"], 1)
            for m in range(FC):
                mm = pe.matmul(ps[5][:, 0:D], act_T[:, m, :], mem["wd_s"][:, m, :], start=(m == 0), stop=(m == FC - 1))
            mm.then_inc(ev["down_made"], 1)

        @block.vector
        def _(dve):
            link = chain(dve, ev["dve_steps"], 0)
            dve.memset(mem["zeros"][:, :], 0.0).then_inc(ev["zeros"], 1)
            link(dve.memset(mem["minus_half"][:, :], -0.5))
            link(dve.memset(mem["all_ones"][:, :], 1.0))
            link(dve.memset(mem["ones_e"][:, :], 1.0))
            dve.wait_ge(ev["loads"], 16 * len(loads))
            dve.wait_ge(mem["later_in"], 16 * len(mem["later_loads"]))
            link(dve.tensor_copy(mem["identb"][:, :], mem["ident"][:, :]))
            link(dve.tensor_copy(mem["before"][:, :], mem["before_f"][:, :]))
            link(dve.bn_stats(stats[:, 0, :], h[:, :]))
            link(dve.bn_aggr(mv[:, 0, :], stats[:, 0, :]))
            dve.tensor_scalar(mv[:, 0, 1:2], mv[:, 0, 1:2], EPS, None, ALU.add).then_inc(ev["stats1"], 1)
            dve.wait_ge(ev["pow1"], 1)
            dve.tensor_scalar(u[:, :], h[:, :], mv[:, 0, 0:1], rstd[:, 0:1], ALU.subtract, ALU.mult).then_inc(ev["u_done"], 1)
            dve.wait_ge(ev["u_done"], 1)
            link(dve.tensor_tensor(ud[:, :], u[:, :], mem["d_row"][:, :], ALU.mult))
            link(dve.tensor_tensor(h[:, :], h[:, :], ud[:, :], ALU.add))
            dve.wait_ge(ev["y_made"], 1)
            dve.tensor_tensor(h[:, :], h[:, :], ps[5][:, 0:D], ALU.add).then_inc(ev["h2_done"], 1)
            dve.wait_ge(ev["h2_done"], 1)
            link(dve.bn_stats(stats[:, 1, :], h[:, :]))
            link(dve.bn_aggr(mv[:, 1, :], stats[:, 1, :]))
            dve.tensor_scalar(mv[:, 1, 1:2], mv[:, 1, 1:2], EPS, None, ALU.add).then_inc(ev["stats2"], 1)
            dve.wait_ge(ev["pow2"], 1)
            dve.tensor_scalar(u2[:, :], h[:, :], mv[:, 1, 0:1], rstd[:, 1:2], ALU.subtract, ALU.mult).then_inc(ev["u2_done"], 1)
            dve.wait_ge(ev["bu_copied"], 1)
            link(dve.tensor_copy(mem["state0"][:, :], bu[:, :, 0]))
            dve.wait_ge(ev["logits"], 1)
            dve.tensor_tensor(probs[:, 0, :], ps[4][:, 0:E], mem["rb_row"][:, :], ALU.add).then_inc(ev["logits_biased"], 1)
            dve.wait_ge(ev["sigmoid"], 1)
            top_two(dve, link, mem, probs[:, :, :], 1)
            link(dve.tensor_copy(mem["pos"][:, 0, :], mem["slot0"][:, :]))
            slot_rows(dve, link, mem, 1, mem["zeros"][:, 0:1])
            link(dve.tensor_tensor(mem["next_slot"][:, :], mem["hot"][:, 0, 0, :], mem["hot"][:, 0, 1, :], ALU.add))
            link(dve.tensor_tensor(mem["next_slot"][:, :], mem["next_slot"][:, :], mem["slot0"][:, :], ALU.add))
            link(dve.tensor_scalar(mem["slot_f"][:, 0, :], mem["slot_f"][:, 0, :], mem["first"][:, 0:1], None, ALU.mult))
            link(dve.tensor_tensor(mem["slot_f"][:, 0, :], mem["slot_f"][:, 0, :], mem["spare"][:, :], ALU.add))
            dve.tensor_copy(mem["slot_i"][:, 0, :], mem["slot_f"][:, 0, :]).then_inc(ev["slots"], 1)
            dve.wait_ge(ev["silu"], 1)
            dve.tensor_tensor(act_T[:, :, :], gate[:, :, :], ps[7][:, :].rearrange("p (m n) -> p m n", m=FC),
                              ALU.mult).then_inc(ev["act_done"], 1)
            dve.wait_ge(ev["down_made"], 1)
            dve.tensor_tensor(h[:, :], h[:, :], ps[5][:, 0:D], ALU.add).then_inc(ev["acc_done"], 1)

            w, w2, den, num = (lam[:, n:n + 1] for n in range(4))
            cos, sin = mem["cos"], mem["sin"]
            dve.wait_ge(ev["omega"], 1)
            link(dve.tensor_copy(w, ps[0][:, 0:1]))
            link(dve.tensor_tensor(w2, w, w, ALU.mult))
            link(dve.tensor_scalar(den, w2, 1.0, None, ALU.add))
            link(dve.reciprocal(den, den))
            link(dve.tensor_scalar(num, w2, -1.0, 1.0, ALU.mult, ALU.add))
            link(dve.tensor_tensor(power[:, 0, 0:1], num, den, ALU.mult))
            link(dve.tensor_scalar(w, w, -2.0, None, ALU.mult))
            link(dve.tensor_tensor(power[:, 0, 1:2], w, den, ALU.mult))
            link(dve.memset(cos[:, 0:1], 1.0))
            link(dve.memset(sin[:, 0:1], 0.0))
            n, k = 1, 0
            while n <= S:
                m = min(n, S + 1 - n)
                pc, ps_ = power[:, k, 0:1], power[:, k, 1:2]
                link(dve.tensor_scalar(turned_c[:, 0:m], sin[:, 0:m], ps_, None, ALU.mult))
                link(dve.tensor_scalar(turned_s[:, 0:m], cos[:, 0:m], ps_, None, ALU.mult))
                link(dve.scalar_tensor_tensor(out=cos[:, n:n + m], in0=cos[:, 0:m], scalar=pc, in1=turned_c[:, 0:m],
                                              op0=ALU.mult, op1=ALU.subtract))
                link(dve.scalar_tensor_tensor(out=sin[:, n:n + m], in0=sin[:, 0:m], scalar=pc, in1=turned_s[:, 0:m],
                                              op0=ALU.mult, op1=ALU.add))
                link(dve.tensor_tensor(lam[:, 4:6], power[:, k, :], power[:, k, :], ALU.mult))
                link(dve.tensor_tensor(power[:, k + 1, 0:1], lam[:, 4:5], lam[:, 5:6], ALU.subtract))
                link(dve.tensor_tensor(lam[:, 6:7], pc, ps_, ALU.mult))
                link(dve.tensor_scalar(power[:, k + 1, 1:2], lam[:, 6:7], 2.0, None, ALU.mult))
                n, k = 2 * n, k + 1


def stage_mix(nc, mem, dram):
    ident = mem["ident"]
    with ExitStack() as ctx:
        sb, pb, sem = places(nc, ctx)
        heads = sb("mix_heads", [P, TT, D], FP32)
        heads_T = sb("mix_heads_T", [P, DC, S], FP32)
        h = sb("mix_h", [P, TT, D], FP32)
        u = sb("mix_u", [P, TT, D], FP32)
        ud = sb("mix_ud", [P, TT, D], FP32)
        u_T = sb("mix_u_T", [P, DC, S], FP32)
        h2 = sb("mix_h2", [P, 2, TT, D], FP32)
        u2_T = sb("mix_u2_T", [P, DC, S], FP32)
        back = sb("mix_back", [P, 4, S], FP32)
        state = sb("mix_state", [P, 2, S], FP32)
        hidden = sb("mix_hidden", [P, 2, S], FP32)
        gate = sb("mix_gate", [P, FC, S], FP32)
        act_T = sb("mix_act_T", [P, FC, S], FP32)
        stats = sb("mix_stats", [P, TT, 6], FP32)
        mv = sb("mix_mv", [P, TT, 2], FP32)
        rstd = sb("mix_rstd", [P, TT], FP32)
        probs = sb("mix_probs", [P, TT, E], FP32)
        chosen = sb("mix_chosen", [P, TT, E], BF16)
        turn = pb("mix_turn", [P, DC, S], FP32)
        made = pb("mix_made", [P, 2, S], FP32)
        pairs = pb("mix_pairs", [P, 2, 2, S], FP32)
        names = ("heads_in heads_turned hT_copied out_made h_done stats1 pow1 u_done ud_done u_turned uT_copied "
                 "bu_made state_done y_made h2_done stats2 pow2 u2_done u2_turned u2T_copied logits_made "
                 "logits_biased sigmoid chosen_done counts_made counts_read slots_ready slots_out "
                 "gate_made gate_done act_done down_made acc_done u2_stored acc_stored "
                 "scatter_begun stats_ready ln_steps scan_steps top_steps slot_steps")
        ev = {n: sem("mix_" + n) for n in names.split()}
        block = ctx.enter_context(nc.Block())
        cos, sin = mem["cos"][:, 1:T1], mem["sin"][:, 1:T1]
        out_rows = dram["out"]

        def batches(eng, step):
            step(0, 0, False, True)
            with eng.Fori(0, (B - 2) // 2) as i:
                for par in range(2):
                    step(2 * i + par + 1, 1 - par, True, True)
            step(B - 1, 1, True, True)
            step(B, 0, True, False)

        @block.sync
        def _(sp):
            def step(b, par, prev, this):
                if this:
                    sp.wait_ge(ev["heads_turned"], b)
                    if prev:
                        sp.dma_start(heads[:, :, :].rearrange("p t n -> p (t n)"),
                                     dram["heads"][bass.ds(b, 1), :, :].rearrange("b p n -> p (b n)")
                                     ).then_inc(ev["heads_in"], 16)
                    else:
                        sp.dma_start(heads[:, :, :].rearrange("p t n -> p (t n)"),
                                     dram["heads"][0, :, :]).then_inc(ev["heads_in"], 16)
                        for dst, src in mem["expert_loads"]:
                            sp.dma_start(dst, src).then_inc(mem["experts_in"], 16)
                    sp.wait_ge(ev["u2_done"], b + 1)
                    sp.dma_start(dram["x_rows"][bass.ds(T1 * b + 1, S), :].rearrange("(t p) n -> p t n", p=P),
                                 u[:, :, :]).then_inc(ev["u2_stored"], 16)
                if prev:
                    sp.wait_ge(ev["acc_done"], 2 * b)
                    sp.dma_start(out_rows[bass.ds(T1 * b - T1 + 1, S), :].rearrange("(t p) n -> p t n", p=P),
                                 h2[:, 1 - par, :, :]).then_inc(ev["acc_stored"], 16)

            batches(sp, step)
            sp.wait_ge(ev["u2_stored"], 16 * B)
            sp.wait_ge(ev["acc_stored"], 16 * B)

        @block.gpsimd
        def _(pool):
            def step(b, par, prev, this):
                if prev:
                    pool.wait_ge(ev["slots_ready"], b)
                    pool.sem_inc(ev["scatter_begun"])
                    for t in range(TT):
                        for n in range(2):
                            pool.indirect_dma_start(
                                out=dram["table"], in_offset=None, in_=mem["pay"][:, t, n, :],
                                out_offset=bass.IndirectOffsetOnAxis(
                                    ap=mem["slot_i"][:, t, n:n + 1].bitcast(U32), axis=0)).then_inc(ev["slots_out"], 16)
                if this:
                    pool.wait_ge(ev["stats1"], b + 1)
                    pool.tensor_tensor(rstd[:, :], mv[:, :, 1], mem["minus_half"][:, 0:TT], ALU.pow).then_inc(ev["pow1"], 1)
                    pool.wait_ge(ev["u_done"], b + 1)
                    pool.tensor_tensor(ud[:, :, :], u[:, :, :], mem["d_row"][:, :].unsqueeze(1).to_broadcast([P, TT, D]),
                                       ALU.mult).then_inc(ev["ud_done"], 1)
                    pool.wait_ge(ev["ud_done"], 2 * b + 1)
                    if prev:
                        pool.wait_ge(ev["acc_stored"], 16 * (b - 1))
                    pool.tensor_tensor(h2[:, par, :, :], ud[:, :, :], h[:, :, :], ALU.add).then_inc(ev["ud_done"], 1)
                    pool.wait_ge(ev["stats2"], b + 1)
                    pool.tensor_tensor(rstd[:, :], mv[:, :, 1], mem["minus_half"][:, 0:TT], ALU.pow).then_inc(ev["pow2"], 1)

            batches(pool, step)
            pool.wait_ge(ev["slots_out"], 16 * 2 * TT * B)

        @block.scalar
        def _(act):
            def silu(b, m):
                act.wait_ge(ev["gate_made"], FC * (b - 1) + m + 1)
                act.wait_ge(ev["act_done"], FC * (b - 1))
                act.activation(gate[:, m, :], pairs[:, m % 2, 0, :], ACT.Silu).then_inc(ev["gate_done"], 1)

            def step(b, par, prev, this):
                if this:
                    act.wait_ge(ev["heads_turned"], b + 1)
                    act.activation(heads_T[:, :, :], turn[:, :, :], ACT.Copy).then_inc(ev["hT_copied"], 1)
                if prev:
                    silu(b, 0)
                    silu(b, 1)
                if this:
                    act.wait_ge(ev["u_turned"], b + 1)
                    act.activation(u_T[:, :, :], turn[:, :, :], ACT.Copy).then_inc(ev["uT_copied"], 1)
                if prev:
                    silu(b, 2)
                    silu(b, 3)
                if this:
                    act.wait_ge(ev["u2_turned"], b + 1)
                    act.activation(u2_T[:, :, :], turn[:, :, :], ACT.Copy).then_inc(ev["u2T_copied"], 1)
                    act.wait_ge(ev["logits_biased"], b + 1)
                    act.activation(probs[:, :, :], probs[:, :, :], ACT.Sigmoid).then_inc(ev["sigmoid"], 1)

            batches(act, step)

        @block.tensor
        def _(pe):
            def shared_up(b, m):
                if m >= 2:
                    pe.wait_ge(ev["act_done"], FC * (b - 1) + m - 1)
                else:
                    pe.wait_ge(ev["acc_done"], 2 * (b - 1))
                for n, w in enumerate((mem["wg_s"], mem["wu_s"])):
                    for c in range(DC):
                        mm = pe.matmul(pairs[:, m % 2, n, :], w[:, c, m * P:(m + 1) * P], u2_T[:, c, :],
                                       start=(c == 0), stop=(c == DC - 1))
                mm.then_inc(ev["gate_made"], 1)

            def shared_down(b, half):
                pe.wait_ge(ev["act_done"], FC * b)
                for t in (2 * half, 2 * half + 1):
                    for m in range(FC):
                        mm = pe.matmul(pairs[:, 0, half, (t % 2) * D:(t % 2 + 1) * D], act_T[:, m, t * P:(t + 1) * P],
                                       mem["wd_s"][:, m, :], start=(m == 0), stop=(m == FC - 1))
                mm.then_inc(ev["down_made"], 1)

            def count(b):
                pe.wait_ge(ev["chosen_done"], b)
                pe.wait_ge(ev["logits_biased"], b)
                pos = made[:, 1, 0:(TT + 1) * E].rearrange("p (t e) -> p t e", e=E)
                for t in range(TT + 1):
                    for k in range(min(t, TT - 1) + 1):
                        w = mem["before"] if k == t else mem["all_ones"]
                        mm = pe.matmul(pos[:, t, :], w[:, :], chosen[:, k, :], start=(k == 0), stop=(k == min(t, TT - 1)))
                mm.then_inc(ev["counts_made"], 1)

            def step(b, par, prev, this):
                if this:
                    pe.wait_ge(ev["heads_in"], 16 * b + 16)
                    pe.wait_ge(ev["u2T_copied"], b)
                    for c in range(DC):
                        for t in range(TT):
                            mm = pe.transpose(turn[:, c, t * P:(t + 1) * P], heads[:, t, c * P:(c + 1) * P], ident[:, :])
                    mm.then_inc(ev["heads_turned"], 1)
                if prev:
                    count(b)
                    shared_up(b, 0)
                if this:
                    pe.wait_ge(ev["hT_copied"], b + 1)
                    pe.wait_ge(ev["counts_read"], b)
                    for t in range(TT):
                        for c in range(DC):
                            mm = pe.matmul(made[:, t // 2, (t % 2) * D:(t % 2 + 1) * D], heads_T[:, c, t * P:(t + 1) * P],
                                           mem["wo_T"][:, c, :], start=(c == 0), stop=(c == DC - 1))
                    mm.then_inc(ev["out_made"], 1)
                if prev:
                    shared_up(b, 1)
                if this:
                    pe.wait_ge(ev["u_done"], b + 1)
                    for c in range(DC):
                        for t in range(TT):
                            mm = pe.transpose(turn[:, c, t * P:(t + 1) * P], u[:, t, c * P:(c + 1) * P], ident[:, :])
                    mm.then_inc(ev["u_turned"], 1)
                if prev:
                    shared_up(b, 2)
                if this:
                    pe.wait_ge(ev["uT_copied"], b + 1)
                    for m in range(2):
                        for c in range(DC):
                            mm = pe.matmul(made[:, m, :], mem["m1_T"][:, c, m * P:(m + 1) * P], u_T[:, c, :],
                                           start=(c == 0), stop=(c == DC - 1))
                    mm.then_inc(ev["bu_made"], 1)
                if prev:
                    shared_up(b, 3)
                    shared_down(b, 0)
                if this:
                    pe.wait_ge(ev["state_done"], b + 1)
                    for t in range(TT):
                        for m in range(2):
                            mm = pe.matmul(made[:, t // 2, (t % 2) * D:(t % 2 + 1) * D], hidden[:, m, t * P:(t + 1) * P],
                                           mem["m2_T"][:, m, :], start=(m == 0), stop=(m == 1))
                    mm.then_inc(ev["y_made"], 1)
                if prev:
                    shared_down(b, 1)
                if this:
                    pe.wait_ge(ev["u2_done"], b + 1)
                    for c in range(DC):
                        for t in range(TT):
                            mm = pe.transpose(turn[:, c, t * P:(t + 1) * P], u[:, t, c * P:(c + 1) * P], ident[:, :])
                    mm.then_inc(ev["u2_turned"], 1)
                    pe.wait_ge(ev["u2T_copied"], b + 1)
                    for t in range(TT):
                        for c in range(DC):
                            mm = pe.matmul(made[:, 0, t * E:(t + 1) * E], u2_T[:, c, t * P:(t + 1) * P],
                                           mem["wr_T"][:, c, :], start=(c == 0), stop=(c == DC - 1))
                    mm.then_inc(ev["logits_made"], 1)

            batches(pe, step)

        @block.vector
        def _(dve):
            def shared_act(b, m):
                dve.wait_ge(ev["gate_done"], FC * (b - 1) + m + 1)
                dve.wait_ge(ev["down_made"], 2 * (b - 1))
                dve.tensor_tensor(act_T[:, m, :], gate[:, m, :], pairs[:, m % 2, 1, :], ALU.mult).then_inc(ev["act_done"], 1)

            def shared_add(b, par, half):
                dve.wait_ge(ev["down_made"], 2 * (b - 1) + half + 1)
                rows = h2[:, 1 - par, 2 * half:2 * half + 2, :]
                dve.tensor_tensor(rows, pairs[:, 0, half, :].rearrange("p (t n) -> p t n", t=2), rows,
                                  ALU.add).then_inc(ev["acc_done"], 1)

            def normalise(b, rows, out, which, link):
                for t in range(TT):
                    link(dve.bn_stats(stats[:, t, :], rows[:, t, :]))
                dve.sem_inc(ev["stats_ready"])
                for t in range(TT):
                    link(dve.bn_aggr(mv[:, t, :], stats[:, t, :]), wait=(t == TT - 1))
                dve.tensor_scalar(mv[:, :, 1], mv[:, :, 1], EPS, None, ALU.add).then_inc(ev[f"stats{which}"], 1)
                dve.wait_ge(ev[f"pow{which}"], b + 1)
                for t in range(TT):
                    last = dve.tensor_scalar(out[:, t, :], rows[:, t, :], mv[:, t, 0:1], rstd[:, t:t + 1],
                                             ALU.subtract, ALU.mult)
                    if t < TT - 1:
                        link(last)
                last.then_inc(ev["u_done" if which == 1 else "u2_done"], 1)

            def place(b):
                link = chain(dve, ev["slot_steps"], (SLOT_STEPS + 2) * (b - 1))
                pos = made[:, 1, 0:TT * E].rearrange("p (t e) -> p t e", e=E)
                dve.wait_ge(ev["counts_made"], b)
                dve.wait_ge(ev["counts_read"], b - 1)
                dve.wait_ge(ev["slots_out"], 16 * 2 * TT * (b - 1))
                link(dve.tensor_tensor(mem["pos"][:, :, :], pos, mem["next_slot"][:, :].unsqueeze(1).to_broadcast([P, TT, E]),
                                       ALU.add))
                dve.tensor_tensor(mem["next_slot"][:, :], made[:, 1, TT * E:(TT + 1) * E], mem["next_slot"][:, :],
                                  ALU.add).then_inc(ev["counts_read"], 1)
                slot_rows(dve, link, mem, TT, mem["row_id"][:, :])
                link(dve.tensor_scalar(mem["row_id"][:, :], mem["row_id"][:, :], float(T1), None, ALU.add))
                dve.tensor_copy(mem["slot_i"][:, :, :], mem["slot_f"][:, :, :]).then_inc(ev["slots_ready"], 1)

            def step(b, par, prev, this):
                ln = chain(dve, ev["ln_steps"], 2 * (3 * TT - 1) * b)
                scan = chain(dve, ev["scan_steps"], 7 * b)
                top = chain(dve, ev["top_steps"], TOP_STEPS * b)
                if prev:
                    place(b)
                    shared_act(b, 0)
                if this:
                    dve.wait_ge(ev["out_made"], b + 1)
                    dve.wait_ge(ev["ud_done"], 2 * b)
                    for t in range(2):
                        last = dve.tensor_tensor(h[:, 2 * t:2 * t + 2, :], made[:, t, :].rearrange("p (t n) -> p t n", t=2),
                                                 mem["bo_row"][:, :].unsqueeze(1).to_broadcast([P, 2, D]), ALU.add)
                        last.then_inc(ev["h_done"], 1)
                    dve.wait_ge(ev["h_done"], 2 * b + 2)
                    dve.wait_ge(ev["u2_stored"], 16 * b)
                    normalise(b, h, u, 1, ln)
                if prev:
                    shared_act(b, 1)
                    shared_act(b, 2)
                if this:
                    dve.wait_ge(ev["bu_made"], b + 1)
                    dve.tensor_tensor(back[:, 0, :], made[:, 0, :], cos, ALU.mult)
                    scan(dve.tensor_tensor(back[:, 1, :], made[:, 1, :], sin, ALU.mult))
                    dve.tensor_tensor(back[:, 2, :], made[:, 1, :], cos, ALU.mult)
                    scan(dve.tensor_tensor(back[:, 3, :], made[:, 0, :], sin, ALU.mult))
                    scan(dve.tensor_tensor_scan(state[:, 0, :], back[:, 0, :], back[:, 1, :], mem["state0"][:, 0:1],
                                                ALU.add, ALU.add))
                    scan(dve.tensor_tensor_scan(state[:, 1, :], back[:, 2, :], back[:, 3, :], mem["state0"][:, 1:2],
                                                ALU.add, ALU.subtract))
                if prev:
                    shared_act(b, 3)
                if this:
                    dve.wait_ge(ev["y_made"], b)
                    dve.tensor_tensor(back[:, 0, :], state[:, 0, :], cos, ALU.mult)
                    scan(dve.tensor_tensor(back[:, 1, :], state[:, 1, :], sin, ALU.mult))
                    dve.tensor_tensor(back[:, 2, :], state[:, 0, :], sin, ALU.mult)
                    scan(dve.tensor_tensor(back[:, 3, :], state[:, 1, :], cos, ALU.mult))
                    scan(dve.tensor_tensor(hidden[:, 0, :], back[:, 0, :], back[:, 1, :], ALU.subtract))
                    dve.tensor_tensor(hidden[:, 1, :], back[:, 2, :], back[:, 3, :], ALU.add).then_inc(ev["state_done"], 1)
                    dve.wait_ge(ev["y_made"], b + 1)
                    dve.wait_ge(ev["ud_done"], 2 * b + 2)
                    for t in range(2):
                        rows = h2[:, par, 2 * t:2 * t + 2, :]
                        dve.tensor_tensor(rows, made[:, t, :].rearrange("p (t n) -> p t n", t=2), rows,
                                          ALU.add).then_inc(ev["h2_done"], 1)
                    dve.wait_ge(ev["h2_done"], 2 * b + 2)
                    ln2 = h2[:, par, :, :]
                    normalise(b, ln2, u, 2, ln)
                if prev:
                    shared_add(b, par, 0)
                    shared_add(b, par, 1)
                if this:
                    dve.wait_ge(ev["logits_made"], b + 1)
                    dve.wait_ge(ev["chosen_done"], b)
                    dve.tensor_tensor(probs[:, :, :], made[:, 0, 0:TT * E].rearrange("p (t e) -> p t e", e=E),
                                      mem["rb_row"][:, :].unsqueeze(1).to_broadcast([P, TT, E]),
                                      ALU.add).then_inc(ev["logits_biased"], 1)
                    dve.wait_ge(ev["sigmoid"], b + 1)
                    top_two(dve, top, mem, probs[:, :, :], TT)
                    dve.tensor_tensor(chosen[:, :, :], mem["hot"][:, :, 0, :], mem["hot"][:, :, 1, :],
                                      ALU.add).then_inc(ev["chosen_done"], 1)

            batches(dve, step)


def stage_experts(nc, mem, dram):
    ident = mem["ident"]
    R = 4
    with ExitStack() as ctx:
        sb, pb, sem = places(nc, ctx)
        counts = sb("counts", [P, E], FP32)
        over = sb("over", [P, E, CAP], FP32)
        need = sb("need", [P, E], FP32)
        ends = sb("ends", [P, E], FP32)
        passed = sb("passed", [P, TILES, E], FP32)
        skipped = sb("skipped", [P, TILES, E], FP32)
        tile_f = sb("tile_f", [P, 2, TILES], FP32)
        tile_i = sb("tile_i", [P, 2, TILES], I32)
        slot = sb("slot", [P, R, 2], I32)
        x_in = sb("x_in", [P, 2, D], FP32)
        x_T = sb("x_T2", [P, 2, DC, P], FP32)
        gate = sb("gate", [P, 2, F], FP32)
        acts = sb("acts", [P, 2, F], FP32)
        acts_T = sb("acts_T", [P, FC, P], FP32)
        y = sb("y", [P, 2, D], FP32)
        ps_up = pb("ps_up", [P, 2, 2, F], FP32)
        ps_x = pb("ps_x", [P, S], FP32)
        ps_a = pb("ps_a", [P, S], FP32)
        ps_y = pb("ps_y", [P, 2, S], FP32)
        slot_in = [sem(f"slot_in{r}") for r in range(R)]
        y_added = [sem(f"y_added{r}") for r in range(R)]
        x_gathered = [sem(f"x_gathered{r}") for r in range(2)]
        names = ("tiles x_turned xT_copied gate_made up_made silu acts_done acts_turned aT_copied down_made y_done "
                 "copied steps dma_begun")
        ev = {n: sem("x_" + n) for n in names.split()}
        block = ctx.enter_context(nc.Block())
        N4 = TILES // R

        @block.sync
        def _(sp):
            sp.wait_ge(ev["tiles"], 1)
            with sp.Fori(0, N4) as i:
                for r in range(R):
                    sp.wait_ge(y_added[r], 16 * i)
                    q = sp.value_load(tile_i[0:1, 0, bass.ds(R * i + r, 1)], min_val=0, max_val=SLOTS // P - 1)
                    sp.dma_start(slot[:, r, :], dram["table"][bass.ds(q * P, P), :]).then_inc(slot_in[r], 16)
            for r in range(R):
                sp.wait_ge(y_added[r], 16 * N4)
            for b in range(1, B):
                sp.dma_start(dram["out"][T1 * b:T1 * b + 1, :], dram["out"][0:1, :]).then_inc(ev["copied"], 16)
            sp.wait_ge(ev["copied"], 16 * (B - 1))

        @block.gpsimd
        def _(pool):
            def gather(i, r, par):
                pool.wait_ge(slot_in[r % R], 16 * (i + r // R) + 16)
                if not (isinstance(i, int) and i == 0 and r < 2):
                    pool.wait_ge(ev["x_turned"], R * i + r - 1)
                pool.sem_inc(ev["dma_begun"])
                pool.indirect_dma_start(
                    out=x_in[:, par, :], out_offset=None, in_=dram["x_rows"],
                    in_offset=bass.IndirectOffsetOnAxis(ap=slot[:, r % R, 0:1].bitcast(U32), axis=0)
                ).then_inc(x_gathered[par], 16)

            def add(i, r):
                pool.wait_ge(ev["y_done"], R * i + r + 1)
                pool.wait_ge(y_added[(r - 1) % R], 16 * i + (16 if r else 0))
                pool.sem_inc(ev["dma_begun"])
                pool.indirect_dma_start(
                    out=dram["out"], in_=y[:, r % 2, :], in_offset=None, compute_op=ALU.add,
                    out_offset=bass.IndirectOffsetOnAxis(ap=slot[:, r, 0:1].bitcast(U32), axis=0)
                ).then_inc(y_added[r], 16)

            gather(0, 0, 0)
            gather(0, 1, 1)
            with pool.Fori(0, N4 - 1) as i:
                for r in range(R):
                    gather(i, r + 2, r % 2)
                    add(i, r)
            for r in range(R):
                if r < 2:
                    gather(N4 - 1, r + 2, r % 2)
                add(N4 - 1, r)

        @block.tensor
        def _(pe):
            def turn_x(t, use, par):
                pe.wait_ge(x_gathered[par], 16 * use + 16)
                pe.wait_ge(ev["xT_copied"], t)
                for c in range(DC):
                    mm = pe.transpose(ps_x[:, c * P:(c + 1) * P], x_in[:, par, c * P:(c + 1) * P], ident[:, :])
                mm.then_inc(ev["x_turned"], 1)

            def up(t, par, which, e):
                w = mem["wg_e"] if which == 0 else mem["wu_e"]
                if which == 0:
                    pe.wait_ge(ev["xT_copied"], t + 1)
                    if not (isinstance(t, int) and t == 0):
                        pe.wait_ge(ev["acts_done"], t - 1)
                for c in range(DC):
                    mm = pe.matmul(ps_up[:, par, which, :], x_T[:, par, c, :], w[:, bass.ds(e, 1), c, :],
                                   start=(c == 0), stop=(c == DC - 1))
                mm.then_inc(ev["gate_made" if which == 0 else "up_made"], 1)

            def turn_acts(t, par):
                pe.wait_ge(ev["acts_done"], t + 1)
                pe.wait_ge(ev["aT_copied"], t)
                for m in range(FC):
                    mm = pe.transpose(ps_a[:, m * P:(m + 1) * P], acts[:, par, m * P:(m + 1) * P], ident[:, :])
                mm.then_inc(ev["acts_turned"], 1)

            def down(i, r, e):
                pe.wait_ge(ev["aT_copied"], R * i + r + 1)
                pe.wait_ge(ev["y_done"], R * i + max(r - 1, 0))
                for m in range(FC):
                    mm = pe.matmul(ps_y[:, r % 2, 0:D], acts_T[:, m, :], mem["wd_e"][:, bass.ds(e, 1), m, :],
                                   start=(m == 0), stop=(m == FC - 1))
                mm.then_inc(ev["down_made"], 1)

            def expert(t):
                return pe.value_load(tile_i[0:1, 1, bass.ds(t, 1)], min_val=0, max_val=E - 1)

            pe.wait_ge(ev["tiles"], 1)
            pe.wait_ge(mem["experts_in"], 16 * len(mem["expert_loads"]))
            for t in range(2):
                turn_x(t, 0, t)
            first = expert(0)
            for which in range(2):
                up(0, 0, which, first)

            def body(i, last):
                for r in range(R):
                    t, par = R * i + r, r % 2
                    more = not (last and r == R - 1)
                    if more:
                        following = expert(t + 1)
                        up(t + 1, 1 - par, 0, following)
                    turn_acts(t, par)
                    if not (last and r >= R - 2):
                        turn_x(t + 2, 2 * i + (r + 2) // 2, par)
                    if more:
                        up(t + 1, 1 - par, 1, following)
                    down(i, r, expert(t))

            with pe.Fori(0, N4 - 1) as i:
                body(i, False)
            body(N4 - 1, True)

        @block.scalar
        def _(act):
            def silu(t, par):
                act.wait_ge(ev["gate_made"], t + 1)
                if not (isinstance(t, int) and t == 0):
                    act.wait_ge(ev["acts_done"], t - 1)
                act.activation(gate[:, par, :], ps_up[:, par, 0, :], ACT.Silu).then_inc(ev["silu"], 1)

            def body(i, last):
                for r in range(R):
                    t, par = R * i + r, r % 2
                    if not (last and r == R - 1):
                        silu(t + 1, 1 - par)
                    act.wait_ge(ev["acts_turned"], t + 1)
                    act.wait_ge(ev["down_made"], t)
                    act.activation(acts_T[:, :, :], ps_a[:, :].rearrange("p (m n) -> p m n", m=FC),
                                   ACT.Copy).then_inc(ev["aT_copied"], 1)

            silu(0, 0)
            with act.Fori(0, N4 - 1) as i:
                body(i, False)
            body(N4 - 1, True)

        @block.vector
        def _(dve):
            link = chain(dve, ev["steps"], 0)
            link(dve.tensor_tensor(counts[:, :], mem["next_slot"][:, :], mem["slot0"][:, :], ALU.subtract))
            link(dve.tensor_tensor(over[:, :, :], counts[:, :].unsqueeze(2).to_broadcast([P, E, CAP]),
                                   mem["tile_rows"][:, 0:CAP].unsqueeze(1).to_broadcast([P, E, CAP]), ALU.is_gt))
            link(dve.tensor_reduce(need[:, :], over[:, :, :], AX.X, ALU.add))
            link(dve.tensor_tensor_scan(ends[:, :], mem["ones_e"][:, :], need[:, :], 0.0, ALU.mult, ALU.add))
            link(dve.tensor_scalar(need[:, :], need[:, :], -1.0, float(CAP), ALU.mult, ALU.add))
            index = mem["tile_index"][:, 0:TILES]
            link(dve.tensor_tensor(passed[:, :, :], index.unsqueeze(2).to_broadcast([P, TILES, E]),
                                   ends[:, :].unsqueeze(1).to_broadcast([P, TILES, E]), ALU.is_ge))
            link(dve.tensor_reduce(tile_f[:, 1, :], passed[:, :, :], AX.X, ALU.add))
            link(dve.tensor_scalar(tile_f[:, 1, :], tile_f[:, 1, :], float(E - 1), None, ALU.min))
            link(dve.tensor_tensor(skipped[:, :, :], passed[:, :, :], need[:, :].unsqueeze(1).to_broadcast([P, TILES, E]),
                                   ALU.mult))
            link(dve.tensor_reduce(tile_f[:, 0, :], skipped[:, :, :], AX.X, ALU.add))
            link(dve.tensor_tensor(tile_f[:, 0, :], tile_f[:, 0, :], index, ALU.add))
            dve.tensor_copy(tile_i[:, :, :], tile_f[:, :, :]).then_inc(ev["tiles"], 1)

            def copy_x(t, par):
                dve.wait_ge(ev["x_turned"], t + 1)
                if not (isinstance(t, int) and t < 2):
                    dve.wait_ge(ev["up_made"], t - 1)
                dve.tensor_copy(x_T[:, par, :, :], ps_x[:, 0:D].rearrange("p (c n) -> p c n", c=DC)).then_inc(ev["xT_copied"], 1)

            def act(t, par):
                dve.wait_ge(ev["silu"], t + 1)
                dve.wait_ge(ev["up_made"], t + 1)
                if not (isinstance(t, int) and t == 0):
                    dve.wait_ge(ev["acts_turned"], t - 1)
                dve.tensor_tensor(acts[:, par, :], gate[:, par, :], ps_up[:, par, 1, :], ALU.mult).then_inc(ev["acts_done"], 1)

            def weigh(i, r):
                dve.wait_ge(ev["down_made"], R * i + r + 1)
                dve.wait_ge(y_added[(r - 2) % R], 16 * i + (16 if r >= 2 else 0))
                dve.tensor_scalar(y[:, r % 2, :], ps_y[:, r % 2, 0:D], slot[:, r, 1:2].bitcast(FP32), None,
                                  ALU.mult).then_inc(ev["y_done"], 1)

            def body(i, last):
                for r in range(R):
                    t, par = R * i + r, r % 2
                    if not (last and r >= R - 2):
                        copy_x(t + 2, par)
                    if not (last and r == R - 1):
                        act(t + 1, 1 - par)
                    weigh(i, r)

            copy_x(0, 0)
            copy_x(1, 1)
            act(0, 0)
            with dve.Fori(0, N4 - 1) as i:
                body(i, False)
            body(N4 - 1, True)


INPUTS = ("x", "cls_tok", "L0_tok_w_qkv", "L0_tok_b_qkv", "L0_tok_w_out", "L0_tok_b_out", "L0_attn_a_params",
          "L0_attn_B_w", "L0_attn_C_w", "L0_attn_D", "L0_ffn_Wg_s", "L0_ffn_Wu_s", "L0_ffn_Wd_s", "L0_ffn_Wg",
          "L0_ffn_Wu", "L0_ffn_Wd", "L0_ffn_Wr", "L0_ffn_rb")


def laid_out(x, cls_tok, w_qkv, b_qkv, w_out, b_out, a_params, b_w, c_w, d, wg_s, wu_s, wd_s, wg, wu, wd, wr, rb):
    def chunks(w):
        return w.reshape(-1, P, w.shape[-1]).transpose(1, 0, 2)

    def experts(w):
        return w.transpose(0, 2, 1).reshape(E, -1, P, w.shape[1]).transpose(2, 0, 1, 3)

    w = w_qkv.reshape(H, 3, HD, D).transpose(3, 1, 0, 2).reshape(D, 3 * D)
    bias = b_qkv.reshape(H, 3, HD).transpose(1, 0, 2).reshape(3, D)
    return {
        "xT": x.reshape(B, S, D).transpose(0, 2, 1).reshape(B, DC, P, S), "cls": cls_tok.reshape(1, D),
        "wqkv": chunks(w), "bqk": bias[:2].reshape(4, P).T, "bv": bias[2:3], "wo_T": chunks(w_out.T),
        "bo": b_out.reshape(1, D), "a_params": a_params.reshape(P, 1), "b_w": chunks(b_w), "c_T": chunks(c_w.T),
        "d": d.reshape(1, D), "wg_s": chunks(wg_s.T), "wu_s": chunks(wu_s.T), "wd_s": chunks(wd_s.T),
        "wg_e": experts(wg), "wu_e": experts(wu), "wd_e": experts(wd), "wr_T": chunks(wr.T), "rb": rb.reshape(1, E),
    }


def constants():
    f32, n = np.float32, np.arange(D)
    k = np.arange(P)
    angle = 2 * np.pi / D * (np.outer(n, k) % D)
    nyquist = np.where(n % 2, -1.0, 1.0)
    to_planes = np.concatenate([np.cos(angle), -np.sin(angle)], 1)
    to_planes[:, P] = nyquist
    from_planes = 2.0 / D * to_planes
    from_planes[:, 0] /= 2
    from_planes[:, P] /= 2
    sine = -2 * np.sin(2 * np.pi / D * (np.outer(k + 1, k) % D))
    sine[P - 1] = 0
    rows = np.arange(SLOTS)
    p = np.arange(P)
    return {
        "ident": np.eye(P, dtype=f32),
        "before": (p[:, None] < p[None, :]).astype(f32),
        "sine": sine.astype(f32),
        "to_planes": to_planes.reshape(2, P, D).transpose(1, 0, 2).astype(f32),
        "from_planes": from_planes.reshape(2, P, D).transpose(1, 0, 2).astype(f32),
        "table_init": np.stack([ROWS + rows % P, 0 * rows], 1).astype(np.int32),
        "iota_e": np.tile(np.arange(E, dtype=f32), (P, 1)),
        "slot0": np.tile(np.arange(E, dtype=f32) * CAP * P, (P, 1)),
        "first": (p == 0).astype(f32)[:, None],
        "spare": np.where(p[:, None] == 0, 0, SLOTS + p[:, None] + [[0, P]]).astype(f32),
        "row_first": (1 + p[:, None] + P * np.arange(TT)[None, :]).astype(f32),
        "tile_index": np.tile(np.arange(TILES, dtype=f32), (P, 1)),
        "tile_rows": np.tile(np.arange(TILES, dtype=f32) * P, (P, 1)),
    }


def program(nc, dram):
    with ExitStack() as ctx:
        sb, _, sem = places(nc, ctx)
        mem = {"later_in": sem("later_in"), "experts_in": sem("experts_in")}

        def rows(name):
            return dram[name].to_broadcast([P, dram[name].shape[1]])

        kept = {
            "ident": ([P, P], dram["ident"]), "bo_row": ([P, D], rows("bo")), "d_row": ([P, D], rows("d")),
            "wo_T": ([P, DC, D], dram["wo_T"]), "wr_T": ([P, DC, E], dram["wr_T"]), "rb_row": ([P, E], rows("rb")),
            "wg_s": ([P, DC, F], dram["wg_s"]), "wu_s": ([P, DC, F], dram["wu_s"]), "wd_s": ([P, FC, D], dram["wd_s"]),
            "iota_e": ([P, E], dram["iota_e"]), "slot0": ([P, E], dram["slot0"]), "first": ([P, 1], dram["first"]),
            "spare": ([P, 2], dram["spare"]), "row_id": ([P, TT], dram["row_first"]),
            "tile_index": ([P, TILES], dram["tile_index"]), "tile_rows": ([P, TILES], dram["tile_rows"]),
            "before_f": ([P, P], dram["before"]),
        }
        for name, (shape, _) in kept.items():
            mem[name] = sb("k_" + name, shape, FP32)
        for name, shape, dtype in (
                ("identb", [P, P], BF16), ("before", [P, P], BF16), ("all_ones", [P, P], BF16), ("ones_e", [P, E], FP32),
                ("m1_T", [P, DC, D], FP32), ("m2_T", [P, 2, D], FP32), ("cos", [P, T1], FP32), ("sin", [P, T1], FP32),
                ("state0", [P, 2], FP32), ("zeros", [P, D], FP32), ("minus_half", [P, TT], FP32),
                ("best", [P, TT, 2], FP32), ("hot", [P, TT, 2, E], FP32), ("eq", [P, TT, E], FP32), ("key", [P, TT, E], FP32),
                ("least", [P, TT], FP32), ("pos", [P, TT, E], FP32), ("slot_f", [P, TT, 2], FP32),
                ("slot_i", [P, TT, 2], I32), ("pay", [P, TT, 2, 2], I32), ("next_slot", [P, E], FP32)):
            mem[name] = sb("k_" + name, shape, dtype)
        loads = [(mem[name][tuple(slice(None) for _ in shape)], src) for name, (shape, src) in kept.items()]
        mem["later_loads"] = loads
        with ExitStack() as first:
            sb1, _, _ = places(nc, first)
            for name, shape in (("wqkv", [P, DC, 3 * D]), ("bqk", [P, 4]), ("bv", [P, D])):
                mem[name] = sb1("k_" + name, shape, FP32)
            mem["first_loads"] = [(mem["wqkv"][:, :, :], dram["wqkv"]), (mem["bqk"][:, :], dram["bqk"]),
                                  (mem["bv"][:, :], rows("bv"))]
            stage_qkv(nc, mem, dram)
        stage_setup(nc, mem, dram)
        stage_attention(nc, mem, dram)
        with ExitStack() as last:
            sb5, _, _ = places(nc, last)
            mem["wg_e"] = sb5("k_wg_e", [P, E, DC, F], FP32)
            mem["wu_e"] = sb5("k_wu_e", [P, E, DC, F], FP32)
            mem["wd_e"] = sb5("k_wd_e", [P, E, FC, D], FP32)
            mem["expert_loads"] = [(mem[n][:, e, :, :], dram[n][:, e, :, :]) for e in range(E)
                                   for n in ("wg_e", "wu_e", "wd_e")]
            stage_mix(nc, mem, dram)
            stage_experts(nc, mem, dram)


def kernel(**inputs):
    import concourse.bacc as _bacc
    from concourse.bass_utils import run_bass_kernel_spmd as _run

    arrays = dict(constants(), **laid_out(*(np.asarray(inputs[name]) for name in INPUTS)))
    arrays = {name: np.ascontiguousarray(a) for name, a in arrays.items()}
    nc = _bacc.Bacc("TRN2", target_bir_lowering=False, num_devices=1)
    dram = {name: nc.dram_tensor("in_" + name, a.shape, mybir.dt.from_np(a.dtype), kind="ExternalInput").ap()
            for name, a in arrays.items()}
    for name, shape, dtype in (
            ("qk", (B, 2, PARTS, D, S), BF16), ("v", (B, P, TT * H * VW), FP32), ("heads", (B, P, TT * D), FP32),
            ("x_rows", (ROWS + P, D), FP32), ("table", (SLOTS + 2 * P, 2), I32)):
        dram[name] = nc.dram_tensor("kept_" + name, shape, dtype, kind="Internal").ap()
    dram["out"] = nc.dram_tensor("out_rows", (ROWS + P, D), FP32, kind="ExternalOutput").ap()
    program(nc, dram)
    result = _run(nc, [{"in_" + name: a for name, a in arrays.items()}], core_ids=[0])
    return result.results[0]["out_rows"][:ROWS].reshape(B, T1, D)
```

```python
from contextlib import ExitStack

import numpy as np

import concourse.bass as bass
from concourse import mybir

FP32 = mybir.dt.float32
BF16 = mybir.dt.bfloat16
I32 = mybir.dt.int32
U32 = mybir.dt.uint32
ALU = mybir.AluOpType
ACT = mybir.ActivationFunctionType
AX = mybir.AxisListType

P = 128
B, S, D = 8, 512, 256
DC = D // P
TT = S // P
H, HD = 16, 16
G = 4
NG = H // G
PARTS = 3
Q_PART = (0, 0, 0, 1, 1, 2)
K_PART = (0, 1, 2, 0, 1, 0)
KROWS = HD * len(Q_PART)
SROWS = KROWS + PARTS
VW = 2 * HD

E = 8
F = 512
FC = F // P
T1 = S + 1
ROWS = B * T1
CAP = (B * S + 1 + P - 1) // P
RING = 8
TILES = -(-((2 * (B * S + 1) + E * (P - 1)) // P) // RING) * RING
SPARE = TILES - 2 * (B * S + 1) // P
SLOTS = (E * CAP + SPARE) * P
EPS = 1e-5


def places(nc, ctx):
    def sb(name, shape, dtype):
        return ctx.enter_context(nc.sbuf_tensor(name, shape, dtype))

    def pb(name, shape, dtype):
        return ctx.enter_context(nc.psum_tensor(name, shape, dtype))

    def sem(name):
        return ctx.enter_context(nc.semaphore(name))

    return sb, pb, sem


def stage_qkv(nc, mem, dram):
    wqkv, bqk, bv = mem["wqkv"], mem["bqk"], mem["bv"]
    with ExitStack() as ctx:
        sb, pb, sem = places(nc, ctx)
        xt = sb("x_T", [P, 2, DC, S], FP32)
        qk_full = sb("qk_full", [P, 4, S], FP32)
        qk_rest = sb("qk_rest", [P, 4, S], FP32)
        qk_parts = sb("qk_parts", [P, 4, PARTS, S], BF16)
        v_ones = sb("v_ones", [P, TT, H, VW], FP32)
        qk_ps = pb("qk_ps", [P, 4, S], FP32)
        v_ps = pb("v_ps", [P, 2, 2, D], FP32)
        weights_in = sem("weights_in")
        x_in = [sem(f"x_in{n}") for n in range(2)]
        x_used = [sem(f"x_used{n}") for n in range(2)]
        qk_out = [sem(f"qk_out{n}") for n in range(4)]
        cut = [sem(f"cut{n}") for n in range(4)]
        parts_stored = [sem(f"parts_stored{n}") for n in range(4)]
        qk_made = sem("qk_made")
        v_half_made = sem("v_half_made")
        cut_step = sem("cut_step")
        v_step = sem("v_step")
        v_stored = sem("v_stored")
        ones_set = sem("ones_set")
        block = ctx.enter_context(nc.Block())

        @block.gpsimd
        def _(pool):
            pool.memset(v_ones[:, :, :, :], 1.0).then_inc(ones_set, 1)
            with pool.Fori(0, B // 2) as i:
                for par in range(2):
                    pool.wait_ge(x_used[par], i)
                    pool.wait_ge(ones_set, 1)
                    pool.dma_start(xt[:, par, :, :], dram["xT"][bass.ds(2 * i + par, 1), :, :, :]
                                   .rearrange("b c p t -> p (b c) t")).then_inc(x_in[par], 16)

        @block.sync
        def _(sp):
            for dst, src in mem["first_loads"]:
                sp.dma_start(dst, src).then_inc(weights_in, 16)
            with sp.Fori(0, B) as b:
                for j in range(4):
                    sp.wait_ge(cut[j], b + 1)
                    sp.dma_start(
                        dram["qk"][bass.ds(b, 1), j // 2, :, (j % 2) * P:(j % 2 + 1) * P, :]
                        .rearrange("b s p n -> p (b s) n"), qk_parts[:, j, :, :]).then_inc(parts_stored[j], 16)
                sp.wait_ge(v_step, TT * b + TT)
                sp.dma_start(dram["v"][bass.ds(b, 1), :, :].rearrange("b p n -> p (b n)"),
                             v_ones[:, :, :, :].rearrange("p t h w -> p (t h w)")).then_inc(v_stored, 16)
            for j in range(4):
                sp.wait_ge(parts_stored[j], 16 * B)
            sp.wait_ge(v_stored, 16 * B)
            for dst, src in mem["later_loads"]:
                sp.dma_start(dst, src).then_inc(mem["later_in"], 16)

        @block.tensor
        def _(pe):
            pe.wait_ge(weights_in, 16 * len(mem["first_loads"]))
            with pe.Fori(0, B // 2) as i:
                for par in range(2):
                    b = 2 * i + par
                    pe.wait_ge(x_in[par], 16 * i + 16)
                    for j in range(4):
                        pe.wait_ge(qk_out[j], b)
                        for c in range(DC):
                            mm = pe.matmul(qk_ps[:, j, :], wqkv[:, c, j * P:(j + 1) * P], xt[:, par, c, :],
                                           start=(c == 0), stop=(c == DC - 1))
                        mm.then_inc(qk_made, 1)
                    pe.wait_ge(v_step, TT * b)
                    for t in range(TT):
                        for c in range(DC):
                            mm = pe.matmul(v_ps[:, t // 2, t % 2, :], xt[:, par, c, t * P:(t + 1) * P],
                                           wqkv[:, c, 2 * D:3 * D], start=(c == 0), stop=(c == DC - 1))
                        if t == 1:
                            mm.then_inc(v_half_made, 1)
                    mm.then_inc(x_used[par], 1)

        @block.scalar
        def _(act):
            act.wait_ge(weights_in, 16 * len(mem["first_loads"]))
            with act.Fori(0, B) as b:
                for j in range(4):
                    act.wait_ge(cut[j], b)
                    act.wait_ge(qk_made, 4 * b + j + 1)
                    act.activation(qk_full[:, j, :], qk_ps[:, j, :], ACT.Identity,
                                   bias=bqk[:, j:j + 1]).then_inc(qk_out[j], 1)

        @block.vector
        def _(dve):
            dve.wait_ge(weights_in, 16 * len(mem["first_loads"]))
            dve.wait_ge(ones_set, 1)
            with dve.Fori(0, B // 2) as i:
                for par in range(2):
                    b = 2 * i + par
                    for j in range(4):
                        full, rest, parts = qk_full[:, j, :], qk_rest[:, j, :], qk_parts[:, j, :, :]
                        n = 12 * b + 3 * j
                        dve.wait_ge(parts_stored[j], 16 * b)
                        dve.wait_ge(qk_out[j], b + 1)
                        dve.tensor_copy(parts[:, 0, :], full).then_inc(cut_step, 1)
                        dve.wait_ge(cut_step, n + 1)
                        dve.tensor_tensor(rest, full, parts[:, 0, :], ALU.subtract).then_inc(cut_step, 1)
                        dve.wait_ge(cut_step, n + 2)
                        dve.tensor_copy(parts[:, 1, :], rest).then_inc(cut_step, 1)
                        dve.wait_ge(cut_step, n + 3)
                        dve.tensor_tensor(parts[:, 2, :], rest, parts[:, 1, :], ALU.subtract).then_inc(cut[j], 1)
                    dve.wait_ge(v_stored, 16 * b)
                    for t in range(TT):
                        if t < 2:
                            dve.wait_ge(v_half_made, b + 1)
                        else:
                            dve.wait_ge(x_used[par], i + 1)
                        dve.tensor_tensor(v_ones[:, t, :, 0:HD],
                                          v_ps[:, t // 2, t % 2, :].rearrange("p (h d) -> p h d", h=H),
                                          bv[:, :].rearrange("p (h d) -> p h d", h=H), ALU.add).then_inc(v_step, 1)


def stage_attention(nc, mem, dram):
    ident, identb = mem["ident"], mem["identb"]
    with ExitStack() as ctx:
        sb, pb, sem = places(nc, ctx)
        q_rows = sb("q_rows", [P, NG, G, S], BF16)
        k_rows = sb("k_rows", [P, NG, G, S], BF16)
        v_unit = sb("v_unit", [P, NG, TT, G, VW], FP32)
        probs = sb("probs", [P, 8, 2, S], FP32)
        neg_max = sb("neg_max", [P, G * TT], FP32)
        neg_rest = sb("neg_rest", [P, G * TT], FP32)
        max_parts = sb("max_parts", [P, P // (G * TT), G * TT], BF16)
        max_rows = sb("max_rows", [PARTS * G * TT, P], BF16)
        heads_T = sb("heads_T", [P, S], FP32)
        row_sum = sb("row_sum", [P, TT, G], FP32)
        heads = sb("heads_sb", [P, TT, D], FP32)
        by_query = pb("by_query", [P, 2, S], FP32)
        by_key = pb("by_key", [P, 2, 2, S], FP32)
        pv = pb("pv", [P, S], FP32)
        turned = pb("turned", [P, S], FP32)
        unit_in = [sem(f"unit_in{n}") for n in range(NG)]
        unit_used = [sem(f"unit_used{n}") for n in range(NG)]
        max_in = [sem(f"max_in{n}") for n in range(NG)]
        exp_done = [sem(f"exp_done{n}") for n in range(2)]
        ones_row = sem("ones_row")
        query_scored = sem("query_scored")
        max_taken = sem("max_taken")
        max_split = sem("max_split")
        max_turned = sem("max_turned")
        max_copied = sem("max_copied")
        key_scored = sem("key_scored")
        pv_copied = sem("pv_copied")
        heads_turned = sem("heads_turned")
        sum_inv = sem("sum_inv")
        heads_done = sem("heads_done")
        heads_stored = sem("heads_stored")
        block = ctx.enter_context(nc.Block())
        LOADS = 2 * len(Q_PART) + 1
        turned_max = turned[:, 0:P // 2].bitcast(BF16)
        LAST = B - 1

        @block.gpsimd
        def _(pool):
            pool.memset(max_parts[:, :, :], 0.0).then_inc(ones_row, 1)
            pool.wait_ge(ones_row, 1)
            pool.memset(k_rows[KROWS:P, :, :, :], 1.0).then_inc(ones_row, 1)
            pool.memset(q_rows[KROWS:P, :, :, :], 0.0).then_inc(ones_row, 1)
            with pool.Fori(0, B) as b:
                pool.wait_ge(heads_done, NG * b + NG)
                pool.wait_ge(ones_row, 3)
                pool.dma_start(dram["heads"][bass.ds(b, 1), :, :].rearrange("b p n -> p (b n)"),
                               heads[:, :, :].rearrange("p t n -> p (t n)")).then_inc(heads_stored, 16)
            pool.wait_ge(heads_stored, 16 * B)

        @block.sync
        def _(sp):
            with sp.Fori(0, B) as b:
                for g in range(NG):
                    sp.wait_ge(unit_used[g], b)
                    for which, rows, order in ((0, q_rows, Q_PART), (1, k_rows, K_PART)):
                        for n, s in enumerate(order):
                            sp.dma_start(rows[HD * n:HD * (n + 1), g, :, :],
                                         dram["qk"][bass.ds(b, 1), which, s, G * HD * g:G * HD * (g + 1), :]
                                         .rearrange("b (h d) n -> d (b h) n", h=G)).then_inc(unit_in[g], 16)
                    sp.dma_start(v_unit[:, g, :, :, :].rearrange("p t h w -> p t (h w)"),
                                 dram["v"][bass.ds(b, 1), :, :].rearrange("b p (t n) -> p (b t) n", t=TT)
                                 [:, :, G * VW * g:G * VW * (g + 1)]).then_inc(unit_in[g], 16)

        @block.tensor
        def _(pe):
            def score_by_query(b, g, k):
                n = (NG * b + g) * G * TT + k
                h, t = k // TT, k % TT
                if not (isinstance(n, int) and n < 2):
                    pe.wait_ge(max_taken, n - 1)
                pe.matmul(by_query[:, k % 2, :],
                          q_rows[0:KROWS, g, h, t * P:(t + 1) * P], k_rows[0:KROWS, g, h, :],
                          start=True, stop=True).then_inc(query_scored, 1)

            def score_by_key(b, g, i):
                pair, h = i // G, i % G
                pe.wait_ge(exp_done[i % 2], 16 * b + 4 * g + i // 2)
                for t in range(2):
                    kt = 2 * pair + t
                    mm = pe.matmul(by_key[:, i % 2, t, :], k_rows[0:SROWS, g, h, kt * P:(kt + 1) * P],
                                   q_rows[0:SROWS, g, h, :], start=True, stop=True)
                mm.then_inc(key_scored, 1)

            def add_pv(b, g, pair, t):
                kt = 2 * pair + t
                if kt == 0:
                    pe.wait_ge(pv_copied, NG * b + g)
                if t == 0:
                    for buf in range(2):
                        pe.wait_ge(exp_done[buf], 16 * b + 4 * g + 2 * pair + 2)
                for h in range(G):
                    mm = pe.matmul(pv[VW * h:VW * (h + 1), :], v_unit[:, g, kt, h, :],
                                   probs[:, G * pair + h, t, :], start=(kt == 0), stop=(kt == TT - 1))
                if kt == TT - 1:
                    mm.then_inc(unit_used[g], 1)

            def turn_max(b, g):
                pe.wait_ge(max_split, 4 * (NG * b + g) + 4)
                pe.transpose(turned_max, max_parts[:, :, :].rearrange("p s n -> p (s n)"),
                             identb[:, :]).then_inc(max_turned, 1)

            def turn_heads(b, g):
                pe.wait_ge(pv_copied, NG * b + g + 1)
                pe.wait_ge(heads_done, NG * b + g)
                for t in range(TT):
                    mm = pe.transpose(turned[:, t * P:(t + 1) * P], heads_T[:, t * P:(t + 1) * P], ident[:, :])
                mm.then_inc(heads_turned, 1)

            def unit(b, g):
                b1, g1 = b + (g + 2) // NG, (g + 2) % NG
                ahead = not (isinstance(b1, int) and b1 > LAST)
                bm, gm = b + (g + 1) // NG, (g + 1) % NG
                next_max = not (isinstance(bm, int) and bm > LAST)
                by_q = [k for k in range(G * TT)] if ahead else []
                if ahead:
                    pe.wait_ge(unit_in[g1], 16 * LOADS * (b1 + 1))
                pe.wait_ge(max_in[g], 16 * (b + 1))
                for i in range(8):
                    score_by_key(b, g, i)
                    if i == 1 and next_max:
                        if g > 0:
                            pe.wait_ge(heads_done, NG * b + g - 1)
                        else:
                            pe.wait_ge(heads_done, NG * b)
                        turn_max(bm, gm)
                    if i == 4 and g > 0:
                        if next_max:
                            pe.wait_ge(max_copied, NG * bm + gm + 1)
                        turn_heads(b, g - 1)
                    if i == 5:
                        add_pv(b, g, 0, 0)
                    if i == 6:
                        add_pv(b, g, 0, 1)
                    if i >= 1:
                        for k in by_q[2 * (i - 1):2 * i]:
                            score_by_query(b1, g1, k)
                for k in by_q[14:]:
                    score_by_query(b1, g1, k)
                add_pv(b, g, 1, 0)
                add_pv(b, g, 1, 1)
                if g == NG - 1:
                    turn_heads(b, g)

            pe.wait_ge(ones_row, 3)
            for g in range(2):
                pe.wait_ge(unit_in[g], 16 * LOADS)
                for k in range(G * TT):
                    score_by_query(0, g, k)
                if g == 0:
                    turn_max(0, 0)
            with pe.Fori(0, LAST) as b:
                for g in range(NG):
                    unit(b, g)
            for g in range(NG):
                unit(LAST, g)

        @block.vector
        def _(dve):
            def take_max(b, g, k):
                n = (NG * b + g) * G * TT + k
                dve.wait_ge(query_scored, n + 1)
                dve.tensor_reduce(neg_max[:, k:k + 1], by_query[:, k % 2, :], AX.X, ALU.max,
                                  negate=True).then_inc(max_taken, 1)

            def split_max(b, g):
                u = NG * b + g
                dve.wait_ge(max_taken, G * TT * (u + 1))
                dve.wait_ge(max_turned, u)
                dve.tensor_copy(max_parts[:, 0, :], neg_max[:, :]).then_inc(max_split, 1)
                dve.wait_ge(max_split, 4 * u + 1)
                dve.tensor_tensor(neg_rest[:, :], neg_max[:, :], max_parts[:, 0, :],
                                  ALU.subtract).then_inc(max_split, 1)
                dve.wait_ge(max_split, 4 * u + 2)
                dve.tensor_copy(max_parts[:, 1, :], neg_rest[:, :]).then_inc(max_split, 1)
                dve.wait_ge(max_split, 4 * u + 3)
                dve.tensor_tensor(max_parts[:, 2, :], neg_rest[:, :], max_parts[:, 1, :],
                                  ALU.subtract).then_inc(max_split, 1)
                dve.wait_ge(max_split, 4 * u + 4)

            def normalise(b, g):
                u = NG * b + g
                cols = turned[:, :].rearrange("p (t h w) -> p t h w", t=TT, h=G)
                dve.wait_ge(heads_turned, u + 1)
                dve.reciprocal(row_sum[:, :, :], cols[:, :, :, HD]).then_inc(sum_inv, 1)
                dve.wait_ge(sum_inv, u + 1)
                if g == 0:
                    dve.wait_ge(heads_stored, 16 * b)
                dve.tensor_tensor(heads[:, :, G * HD * g:G * HD * (g + 1)].rearrange("p t (h w) -> p t h w", h=G),
                                  cols[:, :, :, 0:HD],
                                  row_sum[:, :, :].unsqueeze(3).to_broadcast([P, TT, G, HD]),
                                  ALU.mult).then_inc(heads_done, 1)

            def unit(b, g):
                b1, g1 = b + (g + 2) // NG, (g + 2) % NG
                ahead = not (isinstance(b1, int) and b1 > LAST)
                for k in range(G * TT if ahead else 0):
                    take_max(b1, g1, k)
                    if k == 9 and g > 0:
                        normalise(b, g - 1)
                if ahead:
                    split_max(b1, g1)
                elif g > 0:
                    normalise(b, g - 1)
                if g == NG - 1:
                    normalise(b, g)

            dve.wait_ge(ones_row, 3)
            for g in range(2):
                for k in range(G * TT):
                    take_max(0, g, k)
                split_max(0, g)
            with dve.Fori(0, LAST) as b:
                for g in range(NG):
                    unit(b, g)
            for g in range(NG):
                unit(LAST, g)

        @block.scalar
        def _(act):
            def place_max(b, g):
                u = NG * b + g
                act.wait_ge(max_turned, u + 1)
                if not (isinstance(u, int) and u < 1):
                    ub, ug = (b, g - 1) if g else (b - 1, NG - 1)
                    act.wait_ge(max_in[ug], 16 * ub + 16)
                act.activation(max_rows[:, :], turned_max[0:PARTS * G * TT, :], ACT.Copy).then_inc(max_copied, 1)
                act.wait_ge(max_copied, u + 1)
                act.wait_ge(unit_used[g], b)
                act.dma_start(q_rows[KROWS:SROWS, g, :, :].rearrange("s h (t p) -> s (h t) p", t=TT),
                              max_rows[:, :]).then_inc(max_in[g], 16)

            def exponentials(b, g, i):
                act.wait_ge(key_scored, 8 * (NG * b + g) + i + 1)
                if i % G == 0:
                    act.wait_ge(unit_used[g - 1] if g else unit_used[NG - 1], b + 1 if g else b)
                act.activation(probs[:, i, :, :], by_key[:, i % 2, :, :], ACT.Exp,
                               scale=float(HD) ** -0.5).then_inc(exp_done[i % 2], 1)

            def unit(b, g):
                bm, gm = b + (g + 1) // NG, (g + 1) % NG
                for i in range(8):
                    exponentials(b, g, i)
                    if i == 1 and not (isinstance(bm, int) and bm > LAST):
                        place_max(bm, gm)
                act.wait_ge(unit_used[g], b + 1)
                act.wait_ge(heads_turned, NG * b + g)
                act.activation(heads_T[:, :], pv[:, :], ACT.Copy).then_inc(pv_copied, 1)

            act.wait_ge(ones_row, 3)
            place_max(0, 0)
            with act.Fori(0, LAST) as b:
                for g in range(NG):
                    unit(b, g)
            for g in range(NG):
                unit(LAST, g)


def chain(eng, sem, start):
    count = [0]

    def link(instruction, wait=True):
        count[0] += 1
        instruction.then_inc(sem, 1)
        if wait:
            eng.wait_ge(sem, start + count[0])

    return link


def top_two(dve, link, mem, probs, t):
    iota = mem["iota_e"][:, :].unsqueeze(1).to_broadcast([P, t, E])
    eq, key, least = mem["eq"][:, 0:t, :], mem["key"][:, 0:t, :], mem["least"][:, 0:t]
    for n in range(2):
        best, hot = mem["best"][:, 0:t, n], mem["hot"][:, 0:t, n, :]
        link(dve.tensor_reduce(best, probs, AX.X, ALU.max))
        link(dve.tensor_tensor(eq, probs, best.unsqueeze(2).to_broadcast([P, t, E]), ALU.is_equal))
        link(dve.tensor_scalar(eq, eq, -float(E), None, ALU.mult))
        link(dve.tensor_tensor(key, eq, iota, ALU.add))
        link(dve.tensor_reduce(least, key, AX.X, ALU.min))
        link(dve.tensor_tensor(hot, key, least.unsqueeze(2).to_broadcast([P, t, E]), ALU.is_equal))
        if n == 0:
            link(dve.tensor_scalar(key, hot, -4.0, None, ALU.mult))
            link(dve.tensor_tensor(probs, probs, key, ALU.add))


TOP_STEPS = 14


def slot_rows(dve, link, mem, t, row_id):
    pos, picked, slot_f = mem["pos"][:, 0:t, :], mem["eq"][:, 0:t, :], mem["slot_f"]
    for n in range(2):
        link(dve.tensor_tensor(picked, mem["hot"][:, 0:t, n, :], pos, ALU.mult))
        link(dve.tensor_reduce(slot_f[:, 0:t, n], picked, AX.X, ALU.add))
        link(dve.tensor_copy(mem["pay"][:, 0:t, n, 0], row_id))
        link(dve.tensor_copy(mem["pay"][:, 0:t, n, 1].bitcast(FP32), mem["best"][:, 0:t, n]))


SLOT_STEPS = 8


def stage_setup(nc, mem, dram):
    with ExitStack() as ctx:
        sb, pb, sem = places(nc, ctx)
        a_col = sb("a_col", [P, 1], FP32)
        sine = sb("sine", [P, P], FP32)
        b_w = sb("b_w", [P, 2, D], FP32)
        c_T = sb("c_T", [P, 2, D], FP32)
        to_planes = sb("to_planes", [P, 2, D], FP32)
        from_planes = sb("from_planes", [P, 2, D], FP32)
        h = sb("cls_h", [P, D], FP32)
        u = sb("cls_u", [P, D], FP32)
        ud = sb("cls_ud", [P, D], FP32)
        u2 = sb("cls_u2", [P, D], FP32)
        stats = sb("cls_stats", [P, 2, 6], FP32)
        mv = sb("cls_mv", [P, 2, 2], FP32)
        rstd = sb("cls_rstd", [P, 2], FP32)
        u_T = sb("cls_u_T", [P, 2, P], FP32)
        bu = sb("cls_bu", [P, 2, P], FP32)
        u2_T = sb("cls_u2_T", [P, 2, P], FP32)
        gate = sb("cls_gate", [P, FC, P], FP32)
        act_T = sb("cls_act_T", [P, FC, P], FP32)
        probs = sb("cls_probs", [P, 1, E], FP32)
        lam = sb("lam", [P, 8], FP32)
        power = sb("power", [P, 11, 2], FP32)
        turned_c = sb("turned_c", [P, S // 2], FP32)
        turned_s = sb("turned_s", [P, S // 2], FP32)
        ps = [pb(f"setup_ps{n}", [P, S], FP32) for n in range(8)]
        names = ("loads first_row stats1 stats2 pow1 pow2 u_done u_turned uT_copied omega m1_made m1_copied "
                 "m2_made m2_copied bu_made bu_copied ud_done y_made h2_done u2_done u2_turned u2T_copied "
                 "logits logits_biased sigmoid gu_made silu act_done down_made acc_done slots stored "
                 "zeros table_set slots_out dve_steps")
        ev = {n: sem("setup_" + n) for n in names.split()}
        block = ctx.enter_context(nc.Block())
        loads = [(h[:, :], dram["cls"].to_broadcast([P, D])), (a_col[:, :], dram["a_params"]),
                 (sine[:, :], dram["sine"]), (b_w[:, :, :], dram["b_w"]), (c_T[:, :, :], dram["c_T"]),
                 (to_planes[:, :, :], dram["to_planes"]), (from_planes[:, :, :], dram["from_planes"])]

        @block.sync
        def _(sp):
            for dst, src in loads:
                sp.dma_start(dst, src).then_inc(ev["loads"], 16)
            sp.dma_start(dram["table"][0:SLOTS, :].rearrange("(p n) c -> p (n c)", p=P),
                         dram["table_init"].rearrange("(p n) c -> p (n c)", p=P)).then_inc(ev["table_set"], 16)
            sp.wait_ge(ev["zeros"], 1)
            sp.dma_start(dram["x_rows"][ROWS:ROWS + P, :], mem["zeros"][:, :]).then_inc(ev["stored"], 16)
            sp.dma_start(dram["out"][ROWS:ROWS + P, :], mem["zeros"][:, :]).then_inc(ev["stored"], 16)
            sp.wait_ge(ev["u2_done"], 1)
            sp.dma_start(dram["x_rows"][0:ROWS, :].rearrange("(b t) n -> b t n", t=T1)[:, 0, :],
                         u2[0:B, :]).then_inc(ev["stored"], 16)
            sp.wait_ge(ev["acc_done"], 1)
            sp.dma_start(dram["out"][0:ROWS, :].rearrange("(b t) n -> b t n", t=T1)[:, 0, :],
                         h[0:B, :]).then_inc(ev["stored"], 16)
            sp.wait_ge(ev["table_set"], 16)
            sp.wait_ge(ev["stored"], 16 * 4)

        @block.gpsimd
        def _(pool):
            pool.wait_ge(ev["stats1"], 1)
            pool.tensor_tensor(rstd[:, 0:1], mv[:, 0, 1:2], mem["minus_half"][:, 0:1], ALU.pow).then_inc(ev["pow1"], 1)
            pool.wait_ge(ev["stats2"], 1)
            pool.tensor_tensor(rstd[:, 1:2], mv[:, 1, 1:2], mem["minus_half"][:, 0:1], ALU.pow).then_inc(ev["pow2"], 1)
            pool.wait_ge(ev["table_set"], 16)
            pool.wait_ge(ev["slots"], 1)
            for n in range(2):
                pool.indirect_dma_start(
                    out=dram["table"], out_offset=bass.IndirectOffsetOnAxis(ap=mem["slot_i"][:, 0, n:n + 1].bitcast(U32), axis=0),
                    in_=mem["pay"][:, 0, n, :], in_offset=None).then_inc(ev["slots_out"], 16)
            pool.wait_ge(ev["slots_out"], 16 * 2)

        @block.scalar
        def _(act):
            act.wait_ge(ev["m1_made"], 1)
            act.activation(mem["m1_T"][:, :, :], ps[1][:, :].rearrange("p (m n) -> p m n", m=2), ACT.Copy).then_inc(ev["m1_copied"], 1)
            act.wait_ge(ev["m2_made"], 1)
            act.activation(mem["m2_T"][:, :, :], ps[2][:, :].rearrange("p (m n) -> p m n", m=2), ACT.Copy).then_inc(ev["m2_copied"], 1)
            act.wait_ge(ev["u_turned"], 1)
            act.activation(u_T[:, :, :], ps[3][:, 0:D].rearrange("p (c n) -> p c n", c=2), ACT.Copy).then_inc(ev["uT_copied"], 1)
            act.wait_ge(ev["bu_made"], 1)
            act.activation(bu[:, :, :], ps[4][:, 0:D].rearrange("p (c n) -> p c n", c=2), ACT.Copy).then_inc(ev["bu_copied"], 1)
            act.wait_ge(ev["u2_turned"], 1)
            act.activation(u2_T[:, :, :], ps[3][:, 0:D].rearrange("p (c n) -> p c n", c=2), ACT.Copy).then_inc(ev["u2T_copied"], 1)
            act.wait_ge(ev["logits_biased"], 1)
            act.activation(probs[:, :, :], probs[:, :, :], ACT.Sigmoid).then_inc(ev["sigmoid"], 1)
            act.wait_ge(ev["gu_made"], 1)
            act.activation(gate[:, :, :], ps[6][:, :].rearrange("p (m n) -> p m n", m=FC), ACT.Silu).then_inc(ev["silu"], 1)

        @block.tensor
        def _(pe):
            pe.wait_ge(ev["loads"], 16 * len(loads))
            pe.wait_ge(mem["later_in"], 16 * len(mem["later_loads"]))
            pe.matmul(ps[0][:, 0:1], sine[:, :], a_col[:, :], start=True, stop=True).then_inc(ev["omega"], 1)
            for m in range(2):
                for c in range(2):
                    mm = pe.matmul(ps[1][:, m * D:(m + 1) * D], b_w[:, c, m * P:(m + 1) * P], to_planes[:, c, :],
                                   start=(c == 0), stop=(c == 1))
            mm.then_inc(ev["m1_made"], 1)
            for m in range(2):
                for c in range(2):
                    mm = pe.matmul(ps[2][:, m * D:(m + 1) * D], from_planes[:, c, m * P:(m + 1) * P], c_T[:, c, :],
                                   start=(c == 0), stop=(c == 1))
            mm.then_inc(ev["m2_made"], 1)
            pe.wait_ge(ev["u_done"], 1)
            for c in range(2):
                mm = pe.transpose(ps[3][:, c * P:(c + 1) * P], u[:, c * P:(c + 1) * P], mem["ident"][:, :])
            mm.then_inc(ev["u_turned"], 1)
            pe.wait_ge(ev["uT_copied"], 1)
            pe.wait_ge(ev["m1_copied"], 1)
            for m in range(2):
                for c in range(2):
                    mm = pe.matmul(ps[4][:, m * P:(m + 1) * P], mem["m1_T"][:, c, m * P:(m + 1) * P], u_T[:, c, :],
                                   start=(c == 0), stop=(c == 1))
            mm.then_inc(ev["bu_made"], 1)
            pe.wait_ge(ev["bu_copied"], 1)
            pe.wait_ge(ev["m2_copied"], 1)
            for m in range(2):
                mm = pe.matmul(ps[5][:, 0:D], bu[:, m, :], mem["m2_T"][:, m, :], start=(m == 0), stop=(m == 1))
            mm.then_inc(ev["y_made"], 1)
            pe.wait_ge(ev["u2_done"], 1)
            for c in range(2):
                mm = pe.transpose(ps[3][:, c * P:(c + 1) * P], u2[:, c * P:(c + 1) * P], mem["ident"][:, :])
            mm.then_inc(ev["u2_turned"], 1)
            pe.wait_ge(ev["u2T_copied"], 1)
            for c in range(2):
                mm = pe.matmul(ps[4][:, 0:E], u2_T[:, c, :], mem["wr_T"][:, c, :], start=(c == 0), stop=(c == 1))
            mm.then_inc(ev["logits"], 1)
            for bank, w in ((6, mem["wg_s"]), (7, mem["wu_s"])):
                for m in range(FC):
                    for c in range(2):
                        mm = pe.matmul(ps[bank][:, m * P:(m + 1) * P], w[:, c, m * P:(m + 1) * P], u2_T[:, c, :],
                                       start=(c == 0), stop=(c == 1))
            mm.then_inc(ev["gu_made"], 1)
            pe.wait_ge(ev["act_done"], 1)
            for m in range(FC):
                mm = pe.matmul(ps[5][:, 0:D], act_T[:, m, :], mem["wd_s"][:, m, :], start=(m == 0), stop=(m == FC - 1))
            mm.then_inc(ev["down_made"], 1)

        @block.vector
        def _(dve):
            link = chain(dve, ev["dve_steps"], 0)
            dve.memset(mem["zeros"][:, :], 0.0).then_inc(ev["zeros"], 1)
            link(dve.memset(mem["minus_half"][:, :], -0.5))
            link(dve.memset(mem["all_ones"][:, :], 1.0))
            link(dve.memset(mem["ones_e"][:, :], 1.0))
            dve.wait_ge(ev["loads"], 16 * len(loads))
            dve.wait_ge(mem["later_in"], 16 * len(mem["later_loads"]))
            link(dve.tensor_copy(mem["identb"][:, :], mem["ident"][:, :]))
            link(dve.tensor_copy(mem["before"][:, :], mem["before_f"][:, :]))
            link(dve.bn_stats(stats[:, 0, :], h[:, :]))
            link(dve.bn_aggr(mv[:, 0, :], stats[:, 0, :]))
            dve.tensor_scalar(mv[:, 0, 1:2], mv[:, 0, 1:2], EPS, None, ALU.add).then_inc(ev["stats1"], 1)
            dve.wait_ge(ev["pow1"], 1)
            dve.tensor_scalar(u[:, :], h[:, :], mv[:, 0, 0:1], rstd[:, 0:1], ALU.subtract, ALU.mult).then_inc(ev["u_done"], 1)
            dve.wait_ge(ev["u_done"], 1)
            link(dve.tensor_tensor(ud[:, :], u[:, :], mem["d_row"][:, :], ALU.mult))
            link(dve.tensor_tensor(h[:, :], h[:, :], ud[:, :], ALU.add))
            dve.wait_ge(ev["y_made"], 1)
            dve.tensor_tensor(h[:, :], h[:, :], ps[5][:, 0:D], ALU.add).then_inc(ev["h2_done"], 1)
            dve.wait_ge(ev["h2_done"], 1)
            link(dve.bn_stats(stats[:, 1, :], h[:, :]))
            link(dve.bn_aggr(mv[:, 1, :], stats[:, 1, :]))
            dve.tensor_scalar(mv[:, 1, 1:2], mv[:, 1, 1:2], EPS, None, ALU.add).then_inc(ev["stats2"], 1)
            dve.wait_ge(ev["pow2"], 1)
            dve.tensor_scalar(u2[:, :], h[:, :], mv[:, 1, 0:1], rstd[:, 1:2], ALU.subtract, ALU.mult).then_inc(ev["u2_done"], 1)
            dve.wait_ge(ev["bu_copied"], 1)
            link(dve.tensor_copy(mem["state0"][:, :], bu[:, :, 0]))
            dve.wait_ge(ev["logits"], 1)
            dve.tensor_tensor(probs[:, 0, :], ps[4][:, 0:E], mem["rb_row"][:, :], ALU.add).then_inc(ev["logits_biased"], 1)
            dve.wait_ge(ev["sigmoid"], 1)
            top_two(dve, link, mem, probs[:, :, :], 1)
            link(dve.tensor_copy(mem["pos"][:, 0, :], mem["slot0"][:, :]))
            slot_rows(dve, link, mem, 1, mem["zeros"][:, 0:1])
            link(dve.tensor_tensor(mem["next_slot"][:, :], mem["hot"][:, 0, 0, :], mem["hot"][:, 0, 1, :], ALU.add))
            link(dve.tensor_tensor(mem["next_slot"][:, :], mem["next_slot"][:, :], mem["slot0"][:, :], ALU.add))
            link(dve.tensor_scalar(mem["slot_f"][:, 0, :], mem["slot_f"][:, 0, :], mem["first"][:, 0:1], None, ALU.mult))
            link(dve.tensor_tensor(mem["slot_f"][:, 0, :], mem["slot_f"][:, 0, :], mem["spare"][:, :], ALU.add))
            dve.tensor_copy(mem["slot_i"][:, 0, :], mem["slot_f"][:, 0, :]).then_inc(ev["slots"], 1)
            dve.wait_ge(ev["silu"], 1)
            dve.tensor_tensor(act_T[:, :, :], gate[:, :, :], ps[7][:, :].rearrange("p (m n) -> p m n", m=FC),
                              ALU.mult).then_inc(ev["act_done"], 1)
            dve.wait_ge(ev["down_made"], 1)
            dve.tensor_tensor(h[:, :], h[:, :], ps[5][:, 0:D], ALU.add).then_inc(ev["acc_done"], 1)

            w, w2, den, num = (lam[:, n:n + 1] for n in range(4))
            cos, sin = mem["cos"], mem["sin"]
            dve.wait_ge(ev["omega"], 1)
            link(dve.tensor_copy(w, ps[0][:, 0:1]))
            link(dve.tensor_tensor(w2, w, w, ALU.mult))
            link(dve.tensor_scalar(den, w2, 1.0, None, ALU.add))
            link(dve.reciprocal(den, den))
            link(dve.tensor_scalar(num, w2, -1.0, 1.0, ALU.mult, ALU.add))
            link(dve.tensor_tensor(power[:, 0, 0:1], num, den, ALU.mult))
            link(dve.tensor_scalar(w, w, -2.0, None, ALU.mult))
            link(dve.tensor_tensor(power[:, 0, 1:2], w, den, ALU.mult))
            link(dve.memset(cos[:, 0:1], 1.0))
            link(dve.memset(sin[:, 0:1], 0.0))
            n, k = 1, 0
            while n <= S:
                m = min(n, S + 1 - n)
                pc, ps_ = power[:, k, 0:1], power[:, k, 1:2]
                link(dve.tensor_scalar(turned_c[:, 0:m], sin[:, 0:m], ps_, None, ALU.mult))
                link(dve.tensor_scalar(turned_s[:, 0:m], cos[:, 0:m], ps_, None, ALU.mult))
                link(dve.scalar_tensor_tensor(out=cos[:, n:n + m], in0=cos[:, 0:m], scalar=pc, in1=turned_c[:, 0:m],
                                              op0=ALU.mult, op1=ALU.subtract))
                link(dve.scalar_tensor_tensor(out=sin[:, n:n + m], in0=sin[:, 0:m], scalar=pc, in1=turned_s[:, 0:m],
                                              op0=ALU.mult, op1=ALU.add))
                link(dve.tensor_tensor(lam[:, 4:6], power[:, k, :], power[:, k, :], ALU.mult))
                link(dve.tensor_tensor(power[:, k + 1, 0:1], lam[:, 4:5], lam[:, 5:6], ALU.subtract))
                link(dve.tensor_tensor(lam[:, 6:7], pc, ps_, ALU.mult))
                link(dve.tensor_scalar(power[:, k + 1, 1:2], lam[:, 6:7], 2.0, None, ALU.mult))
                n, k = 2 * n, k + 1


def stage_mix(nc, mem, dram):
    ident = mem["ident"]
    with ExitStack() as ctx:
        sb, pb, sem = places(nc, ctx)
        heads = sb("mix_heads", [P, TT, D], FP32)
        heads_T = sb("mix_heads_T", [P, DC, S], FP32)
        h = sb("mix_h", [P, TT, D], FP32)
        u = sb("mix_u", [P, TT, D], FP32)
        ud = sb("mix_ud", [P, TT, D], FP32)
        u_T = sb("mix_u_T", [P, DC, S], FP32)
        h2 = sb("mix_h2", [P, 2, TT, D], FP32)
        u2_T = sb("mix_u2_T", [P, DC, S], FP32)
        back = sb("mix_back", [P, 4, S], FP32)
        state = sb("mix_state", [P, 2, S], FP32)
        hidden = sb("mix_hidden", [P, 2, S], FP32)
        gate = sb("mix_gate", [P, FC, S], FP32)
        act_T = sb("mix_act_T", [P, FC, S], FP32)
        stats = sb("mix_stats", [P, TT, 6], FP32)
        mv = sb("mix_mv", [P, TT, 2], FP32)
        rstd = sb("mix_rstd", [P, TT], FP32)
        probs = sb("mix_probs", [P, TT, E], FP32)
        chosen = sb("mix_chosen", [P, TT, E], BF16)
        turn = pb("mix_turn", [P, DC, S], FP32)
        made = pb("mix_made", [P, 2, S], FP32)
        pairs = pb("mix_pairs", [P, 2, 2, S], FP32)
        names = ("heads_in heads_turned hT_copied out_made h_done stats1 pow1 u_done ud_done u_turned uT_copied "
                 "bu_made state_done y_made h2_done stats2 pow2 u2_done u2_turned u2T_copied logits_made "
                 "logits_biased sigmoid chosen_done counts_made counts_read slots_ready slots_out "
                 "gate_made gate_done act_done down_made acc_done u2_stored acc_stored "
                 "scatter_begun stats_ready ln_steps scan_steps top_steps slot_steps")
        ev = {n: sem("mix_" + n) for n in names.split()}
        block = ctx.enter_context(nc.Block())
        cos, sin = mem["cos"][:, 1:T1], mem["sin"][:, 1:T1]
        out_rows = dram["out"]

        def batches(eng, step):
            step(0, 0, False, True, True)
            with eng.Fori(0, (B - 2) // 2) as i:
                for par in range(2):
                    step(2 * i + par + 1, 1 - par, True, True, True)
            step(B - 1, 1, True, True, False)
            step(B, 0, True, False, False)

        @block.sync
        def _(sp):
            sp.dma_start(heads[:, :, :].rearrange("p t n -> p (t n)"), dram["heads"][0, :, :]).then_inc(ev["heads_in"], 16)

            def step(b, par, prev, this, nxt):
                if nxt:
                    sp.wait_ge(ev["heads_turned"], b + 1)
                    sp.dma_start(heads[:, :, :].rearrange("p t n -> p (t n)"),
                                 dram["heads"][bass.ds(b + 1, 1), :, :].rearrange("b p n -> p (b n)")
                                 ).then_inc(ev["heads_in"], 16)
                if this:
                    for name in ("wg_e", "wu_e", "wd_e"):
                        sp.dma_start(mem[name][:, bass.ds(b, 1), :, :], dram[name][:, bass.ds(b, 1), :, :]
                                     ).then_inc(mem["experts_in"], 16)
                    sp.wait_ge(ev["u2_done"], b + 1)
                    sp.dma_start(dram["x_rows"][bass.ds(T1 * b + 1, S), :].rearrange("(t p) n -> p t n", p=P),
                                 u[:, :, :]).then_inc(ev["u2_stored"], 16)
                if prev:
                    sp.wait_ge(ev["acc_done"], 2 * b)
                    sp.dma_start(out_rows[bass.ds(T1 * b - T1 + 1, S), :].rearrange("(t p) n -> p t n", p=P),
                                 h2[:, 1 - par, :, :]).then_inc(ev["acc_stored"], 16)

            batches(sp, step)
            sp.wait_ge(ev["u2_stored"], 16 * B)
            sp.wait_ge(ev["acc_stored"], 16 * B)

        @block.gpsimd
        def _(pool):
            def inverse_deviation(b, which):
                pool.wait_ge(ev[f"stats{which}"], b + 1)
                pool.tensor_tensor(rstd[:, :], mv[:, :, 1], mem["minus_half"][:, 0:TT], ALU.pow).then_inc(ev[f"pow{which}"], 1)

            def step(b, par, prev, this, nxt):
                if this:
                    pool.wait_ge(ev["u_done"], b + 1)
                    pool.tensor_tensor(ud[:, :, :], u[:, :, :], mem["d_row"][:, :].unsqueeze(1).to_broadcast([P, TT, D]),
                                       ALU.mult).then_inc(ev["ud_done"], 1)
                    pool.wait_ge(ev["ud_done"], 2 * b + 1)
                    if prev:
                        pool.wait_ge(ev["acc_stored"], 16 * (b - 1))
                    pool.tensor_tensor(h2[:, par, :, :], ud[:, :, :], h[:, :, :], ALU.add).then_inc(ev["ud_done"], 1)
                    inverse_deviation(b, 2)
                if prev:
                    pool.wait_ge(ev["slots_ready"], b)
                    pool.sem_inc(ev["scatter_begun"])
                    for t in range(TT):
                        for n in range(2):
                            pool.indirect_dma_start(
                                out=dram["table"], in_offset=None, in_=mem["pay"][:, t, n, :],
                                out_offset=bass.IndirectOffsetOnAxis(
                                    ap=mem["slot_i"][:, t, n:n + 1].bitcast(U32), axis=0)).then_inc(ev["slots_out"], 16)
                if nxt:
                    inverse_deviation(b + 1, 1)

            inverse_deviation(0, 1)
            batches(pool, step)
            pool.wait_ge(ev["slots_out"], 16 * 2 * TT * B)

        @block.scalar
        def _(act):
            def silu(j, m):
                act.wait_ge(ev["gate_made"], FC * j + m + 1)
                act.wait_ge(ev["act_done"], FC * j)
                act.activation(gate[:, m, :], pairs[:, m % 2, 0, :], ACT.Silu).then_inc(ev["gate_done"], 1)

            def copy_turned(to, b, turned, copied):
                act.wait_ge(ev[turned], b + 1)
                act.activation(to[:, :, :], turn[:, :, :], ACT.Copy).then_inc(ev[copied], 1)

            def step(b, par, prev, this, nxt):
                if this:
                    copy_turned(u_T, b, "u_turned", "uT_copied")
                if prev:
                    silu(b - 1, 1)
                    silu(b - 1, 2)
                if nxt:
                    copy_turned(heads_T, b + 1, "heads_turned", "hT_copied")
                if prev:
                    silu(b - 1, 3)
                if this:
                    copy_turned(u2_T, b, "u2_turned", "u2T_copied")
                    act.wait_ge(ev["logits_biased"], b + 1)
                    act.activation(probs[:, :, :], probs[:, :, :], ACT.Sigmoid).then_inc(ev["sigmoid"], 1)
                    silu(b, 0)

            copy_turned(heads_T, 0, "heads_turned", "hT_copied")
            batches(act, step)

        @block.tensor
        def _(pe):
            def turn_rows(rows, done):
                for c in range(DC):
                    for t in range(TT):
                        mm = pe.transpose(turn[:, c, t * P:(t + 1) * P], rows[:, t, c * P:(c + 1) * P], ident[:, :])
                mm.then_inc(ev[done], 1)

            def turn_heads(b):
                pe.wait_ge(ev["heads_in"], 16 * b + 16)
                turn_rows(heads, "heads_turned")

            def by_token(lhs, w, done):
                for t in range(TT):
                    for c in range(DC):
                        mm = pe.matmul(made[:, t // 2, (t % 2) * D:(t % 2 + 1) * D], lhs[:, c, t * P:(t + 1) * P],
                                       w[:, c, :], start=(c == 0), stop=(c == DC - 1))
                mm.then_inc(ev[done], 1)

            def project_out(b):
                pe.wait_ge(ev["hT_copied"], b + 1)
                pe.wait_ge(ev["h2_done"], 2 * b)
                by_token(heads_T, mem["wo_T"], "out_made")

            def shared_up(j, m):
                if m == 0:
                    pe.wait_ge(ev["acc_done"], 2 * j)
                elif m >= 2:
                    pe.wait_ge(ev["act_done"], FC * j + m - 1)
                for n, w in enumerate((mem["wg_s"], mem["wu_s"])):
                    for c in range(DC):
                        mm = pe.matmul(pairs[:, m % 2, n, :], w[:, c, m * P:(m + 1) * P], u2_T[:, c, :],
                                       start=(c == 0), stop=(c == DC - 1))
                mm.then_inc(ev["gate_made"], 1)

            def shared_down(j, half):
                pe.wait_ge(ev["act_done"], FC * j + FC)
                for t in (2 * half, 2 * half + 1):
                    for m in range(FC):
                        mm = pe.matmul(pairs[:, 0, half, (t % 2) * D:(t % 2 + 1) * D], act_T[:, m, t * P:(t + 1) * P],
                                       mem["wd_s"][:, m, :], start=(m == 0), stop=(m == FC - 1))
                mm.then_inc(ev["down_made"], 1)

            def count(j, nxt):
                pe.wait_ge(ev["chosen_done"], j + 1)
                if nxt:
                    pe.wait_ge(ev["hT_copied"], j + 3)
                pos = turn[:, 1, 0:(TT + 1) * E].rearrange("p (t e) -> p t e", e=E)
                for t in range(TT + 1):
                    for k in range(min(t, TT - 1) + 1):
                        w = mem["before"] if k == t else mem["all_ones"]
                        mm = pe.matmul(pos[:, t, :], w[:, :], chosen[:, k, :], start=(k == 0), stop=(k == min(t, TT - 1)))
                mm.then_inc(ev["counts_made"], 1)

            def step(b, par, prev, this, nxt):
                if this:
                    pe.wait_ge(ev["u_done"], b + 1)
                    pe.wait_ge(ev["logits_biased"], b)
                    turn_rows(u, "u_turned")
                if prev:
                    shared_up(b - 1, 1)
                if this:
                    pe.wait_ge(ev["uT_copied"], b + 1)
                    for m in range(2):
                        for c in range(DC):
                            mm = pe.matmul(made[:, m, :], mem["m1_T"][:, c, m * P:(m + 1) * P], u_T[:, c, :],
                                           start=(c == 0), stop=(c == DC - 1))
                    mm.then_inc(ev["bu_made"], 1)
                if prev:
                    shared_up(b - 1, 2)
                if nxt:
                    turn_heads(b + 1)
                if prev:
                    shared_up(b - 1, 3)
                    count(b - 1, nxt)
                if this:
                    pe.wait_ge(ev["state_done"], b + 1)
                    by_token(hidden, mem["m2_T"], "y_made")
                if prev:
                    shared_down(b - 1, 0)
                    shared_down(b - 1, 1)
                if this:
                    pe.wait_ge(ev["u2_done"], b + 1)
                    pe.wait_ge(ev["counts_read"], b)
                    if nxt:
                        pe.wait_ge(ev["hT_copied"], b + 2)
                    turn_rows(u, "u2_turned")
                if nxt:
                    project_out(b + 1)
                if this:
                    pe.wait_ge(ev["u2T_copied"], b + 1)
                    for t in range(TT):
                        for c in range(DC):
                            mm = pe.matmul(turn[:, 0, t * E:(t + 1) * E], u2_T[:, c, t * P:(t + 1) * P],
                                           mem["wr_T"][:, c, :], start=(c == 0), stop=(c == DC - 1))
                    mm.then_inc(ev["logits_made"], 1)
                    shared_up(b, 0)

            turn_heads(0)
            project_out(0)
            batches(pe, step)

        @block.vector
        def _(dve):
            def shared_act(j, m):
                dve.wait_ge(ev["gate_done"], FC * j + m + 1)
                dve.wait_ge(ev["down_made"], 2 * j)
                dve.tensor_tensor(act_T[:, m, :], gate[:, m, :], pairs[:, m % 2, 1, :], ALU.mult).then_inc(ev["act_done"], 1)

            def shared_add(j, par, half):
                dve.wait_ge(ev["down_made"], 2 * j + half + 1)
                rows = h2[:, par, 2 * half:2 * half + 2, :]
                dve.tensor_tensor(rows, pairs[:, 0, half, :].rearrange("p (t n) -> p t n", t=2), rows,
                                  ALU.add).then_inc(ev["acc_done"], 1)

            def statistics(rows, which, link):
                for t in range(TT):
                    link(dve.bn_stats(stats[:, t, :], rows[:, t, :]), wait=(t == TT - 1))
                dve.sem_inc(ev["stats_ready"])
                for t in range(TT):
                    link(dve.bn_aggr(mv[:, t, :], stats[:, t, :]), wait=(t == TT - 1))
                dve.tensor_scalar(mv[:, :, 1], mv[:, :, 1], EPS, None, ALU.add).then_inc(ev[f"stats{which}"], 1)

            def normalise(b, rows, which):
                dve.wait_ge(ev[f"pow{which}"], b + 1)
                for t in range(TT):
                    last = dve.tensor_scalar(u[:, t, :], rows[:, t, :], mv[:, t, 0:1], rstd[:, t:t + 1],
                                             ALU.subtract, ALU.mult)
                last.then_inc(ev["u_done" if which == 1 else "u2_done"], 1)

            def place(j):
                link = chain(dve, ev["slot_steps"], (SLOT_STEPS + 2) * j)
                pos = turn[:, 1, 0:TT * E].rearrange("p (t e) -> p t e", e=E)
                dve.wait_ge(ev["counts_made"], j + 1)
                dve.wait_ge(ev["counts_read"], j)
                dve.wait_ge(ev["slots_out"], 16 * 2 * TT * j)
                link(dve.tensor_tensor(mem["pos"][:, :, :], pos, mem["next_slot"][:, :].unsqueeze(1).to_broadcast([P, TT, E]),
                                       ALU.add))
                dve.tensor_tensor(mem["next_slot"][:, :], turn[:, 1, TT * E:(TT + 1) * E], mem["next_slot"][:, :],
                                  ALU.add).then_inc(ev["counts_read"], 1)
                slot_rows(dve, link, mem, TT, mem["row_id"][:, :])
                link(dve.tensor_scalar(mem["row_id"][:, :], mem["row_id"][:, :], float(T1), None, ALU.add))
                dve.tensor_copy(mem["slot_i"][:, :, :], mem["slot_f"][:, :, :]).then_inc(ev["slots_ready"], 1)

            def first_sum(b):
                dve.wait_ge(ev["out_made"], b + 1)
                dve.wait_ge(ev["ud_done"], 2 * b)
                for t in range(2):
                    dve.tensor_tensor(h[:, 2 * t:2 * t + 2, :], made[:, t, :].rearrange("p (t n) -> p t n", t=2),
                                      mem["bo_row"][:, :].unsqueeze(1).to_broadcast([P, 2, D]),
                                      ALU.add).then_inc(ev["h_done"], 1)
                dve.wait_ge(ev["h_done"], 2 * b + 2)
                statistics(h, 1, chain(dve, ev["ln_steps"], 4 * TT * b))

            def step(b, par, prev, this, nxt):
                scan = chain(dve, ev["scan_steps"], 7 * b)
                if prev:
                    dve.wait_ge(ev["sigmoid"], b)
                    top_two(dve, chain(dve, ev["top_steps"], TOP_STEPS * (b - 1)), mem, probs[:, :, :], TT)
                    dve.tensor_tensor(chosen[:, :, :], mem["hot"][:, :, 0, :], mem["hot"][:, :, 1, :],
                                      ALU.add).then_inc(ev["chosen_done"], 1)
                    shared_act(b - 1, 0)
                    shared_act(b - 1, 1)
                if this:
                    dve.wait_ge(ev["bu_made"], b + 1)
                    dve.tensor_tensor(back[:, 0, :], made[:, 0, :], cos, ALU.mult)
                    scan(dve.tensor_tensor(back[:, 1, :], made[:, 1, :], sin, ALU.mult), wait=False)
                    dve.tensor_tensor(back[:, 2, :], made[:, 1, :], cos, ALU.mult)
                    scan(dve.tensor_tensor(back[:, 3, :], made[:, 0, :], sin, ALU.mult))
                    scan(dve.tensor_tensor_scan(state[:, 0, :], back[:, 0, :], back[:, 1, :], mem["state0"][:, 0:1],
                                                ALU.add, ALU.add), wait=False)
                    scan(dve.tensor_tensor_scan(state[:, 1, :], back[:, 2, :], back[:, 3, :], mem["state0"][:, 1:2],
                                                ALU.add, ALU.subtract))
                if prev:
                    shared_act(b - 1, 2)
                if this:
                    dve.tensor_tensor(back[:, 0, :], state[:, 0, :], cos, ALU.mult)
                    scan(dve.tensor_tensor(back[:, 1, :], state[:, 1, :], sin, ALU.mult), wait=False)
                    dve.tensor_tensor(back[:, 2, :], state[:, 0, :], sin, ALU.mult)
                    scan(dve.tensor_tensor(back[:, 3, :], state[:, 1, :], cos, ALU.mult))
                    dve.wait_ge(ev["y_made"], b)
                    scan(dve.tensor_tensor(hidden[:, 0, :], back[:, 0, :], back[:, 1, :], ALU.subtract), wait=False)
                    dve.tensor_tensor(hidden[:, 1, :], back[:, 2, :], back[:, 3, :], ALU.add).then_inc(ev["state_done"], 1)
                if prev:
                    shared_act(b - 1, 3)
                    place(b - 1)
                if this:
                    dve.wait_ge(ev["y_made"], b + 1)
                    dve.wait_ge(ev["ud_done"], 2 * b + 2)
                    for t in range(2):
                        rows = h2[:, par, 2 * t:2 * t + 2, :]
                        dve.tensor_tensor(rows, made[:, t, :].rearrange("p (t n) -> p t n", t=2), rows,
                                          ALU.add).then_inc(ev["h2_done"], 1)
                    dve.wait_ge(ev["h2_done"], 2 * b + 2)
                    statistics(h2[:, par, :, :], 2, chain(dve, ev["ln_steps"], 4 * TT * b + 2 * TT))
                if prev:
                    shared_add(b - 1, 1 - par, 0)
                if this:
                    normalise(b, h2[:, par, :, :], 2)
                if prev:
                    shared_add(b - 1, 1 - par, 1)
                if nxt:
                    first_sum(b + 1)
                if this:
                    dve.wait_ge(ev["logits_made"], b + 1)
                    dve.tensor_tensor(probs[:, :, :], turn[:, 0, 0:TT * E].rearrange("p (t e) -> p t e", e=E),
                                      mem["rb_row"][:, :].unsqueeze(1).to_broadcast([P, TT, E]),
                                      ALU.add).then_inc(ev["logits_biased"], 1)
                if nxt:
                    dve.wait_ge(ev["u2_stored"], 16 * b + 16)
                    normalise(b + 1, h, 1)

            first_sum(0)
            normalise(0, h, 1)
            batches(dve, step)


def stage_experts(nc, mem, dram):
    ident = mem["ident"]
    R = RING
    X = 4
    with ExitStack() as ctx:
        sb, pb, sem = places(nc, ctx)
        counts = sb("counts", [P, E], FP32)
        over = sb("over", [P, E, CAP], FP32)
        need = sb("need", [P, E], FP32)
        ends = sb("ends", [P, E], FP32)
        passed = sb("passed", [P, TILES, E], FP32)
        skipped = sb("skipped", [P, TILES, E], FP32)
        tile_f = sb("tile_f", [P, 2, TILES], FP32)
        tile_i = sb("tile_i", [P, 2, TILES], I32)
        slot = sb("slot", [P, R, 2], I32)
        x_in = sb("x_in", [P, X, D], FP32)
        x_T = sb("x_T2", [P, 2, DC, P], FP32)
        gate = sb("gate", [P, 2, F], FP32)
        acts = sb("acts", [P, 2, F], FP32)
        acts_T = sb("acts_T", [P, FC, P], FP32)
        y = sb("y", [P, 2, D], FP32)
        ps_up = pb("ps_up", [P, 2, 2, F], FP32)
        ps_x = pb("ps_x", [P, S], FP32)
        ps_a = pb("ps_a", [P, S], FP32)
        ps_y = pb("ps_y", [P, 2, S], FP32)
        slot_in = [sem(f"slot_in{r}") for r in range(R)]
        y_added = sem("y_added")
        x_gathered = [sem(f"x_gathered{r}") for r in range(X)]
        names = ("tiles x_turned xT_copied gate_made up_made silu acts_done acts_turned aT_copied down_made y_done "
                 "copied steps dma_begun")
        ev = {n: sem("x_" + n) for n in names.split()}
        block = ctx.enter_context(nc.Block())
        LOOPS = TILES // R

        @block.sync
        def _(sp):
            sp.wait_ge(ev["tiles"], 1)
            def load_slot(i, r):
                q = sp.value_load(tile_i[0:1, 0, bass.ds(R * i + r, 1)], min_val=0, max_val=SLOTS // P - 1)
                sp.dma_start(slot[:, r, :], dram["table"][bass.ds(q * P, P), :]).then_inc(slot_in[r], 16)

            for r in range(R):
                load_slot(0, r)
            with sp.Fori(0, LOOPS - 1) as i:
                for r in range(R):
                    sp.wait_ge(y_added, 16 * (R * i + r + 1))
                    load_slot(i + 1, r)
            sp.wait_ge(y_added, 16 * TILES)
            for b in range(1, B):
                sp.dma_start(dram["out"][T1 * b:T1 * b + 1, :], dram["out"][0:1, :]).then_inc(ev["copied"], 16)
            sp.wait_ge(ev["copied"], 16 * (B - 1))

        @block.gpsimd
        def _(pool):
            def gather(i, r):
                pool.wait_ge(slot_in[r % R], 16 * (i + r // R) + 16)
                if not (isinstance(i, int) and i == 0 and r < X):
                    pool.wait_ge(ev["x_turned"], R * i + r - X + 1)
                pool.sem_inc(ev["dma_begun"])
                pool.indirect_dma_start(
                    out=x_in[:, r % X, :], out_offset=None, in_=dram["x_rows"],
                    in_offset=bass.IndirectOffsetOnAxis(ap=slot[:, r % R, 0:1].bitcast(U32), axis=0)
                ).then_inc(x_gathered[r % X], 16)

            def add(i, r):
                pool.wait_ge(ev["y_done"], R * i + r + 1)
                pool.wait_ge(y_added, 16 * (R * i + r))
                pool.sem_inc(ev["dma_begun"])
                pool.indirect_dma_start(
                    out=dram["out"], in_=y[:, r % 2, :], in_offset=None, compute_op=ALU.add,
                    out_offset=bass.IndirectOffsetOnAxis(ap=slot[:, r, 0:1].bitcast(U32), axis=0)
                ).then_inc(y_added, 16)

            for r in range(X):
                gather(0, r)
            with pool.Fori(0, LOOPS - 1) as i:
                for r in range(R):
                    add(i, r)
                    gather(i, r + X)
            for r in range(R):
                add(LOOPS - 1, r)
                if r < R - X:
                    gather(LOOPS - 1, r + X)

        @block.tensor
        def _(pe):
            def turn_x(i, r):
                t = R * i + r
                pe.wait_ge(x_gathered[r % X], 16 * (R // X * i + r // X) + 16)
                pe.wait_ge(ev["xT_copied"], t)
                for c in range(DC):
                    mm = pe.transpose(ps_x[:, c * P:(c + 1) * P], x_in[:, r % X, c * P:(c + 1) * P], ident[:, :])
                mm.then_inc(ev["x_turned"], 1)

            def up(t, par, which, e):
                w = mem["wg_e"] if which == 0 else mem["wu_e"]
                if which == 0:
                    pe.wait_ge(ev["xT_copied"], t + 1)
                    if not (isinstance(t, int) and t == 0):
                        pe.wait_ge(ev["acts_done"], t - 1)
                for c in range(DC):
                    mm = pe.matmul(ps_up[:, par, which, :], x_T[:, par, c, :], w[:, bass.ds(e, 1), c, :],
                                   start=(c == 0), stop=(c == DC - 1))
                mm.then_inc(ev["gate_made" if which == 0 else "up_made"], 1)

            def turn_acts(t, par):
                pe.wait_ge(ev["acts_done"], t + 1)
                pe.wait_ge(ev["aT_copied"], t)
                for m in range(FC):
                    mm = pe.transpose(ps_a[:, m * P:(m + 1) * P], acts[:, par, m * P:(m + 1) * P], ident[:, :])
                mm.then_inc(ev["acts_turned"], 1)

            def down(i, r, e):
                pe.wait_ge(ev["aT_copied"], R * i + r + 1)
                pe.wait_ge(ev["y_done"], R * i + max(r - 1, 0))
                for m in range(FC):
                    mm = pe.matmul(ps_y[:, r % 2, 0:D], acts_T[:, m, :], mem["wd_e"][:, bass.ds(e, 1), m, :],
                                   start=(m == 0), stop=(m == FC - 1))
                mm.then_inc(ev["down_made"], 1)

            def expert(t):
                return pe.value_load(tile_i[0:1, 1, bass.ds(t, 1)], min_val=0, max_val=E - 1)

            pe.wait_ge(ev["tiles"], 1)
            pe.wait_ge(mem["experts_in"], 16 * 3 * E)
            for t in range(2):
                turn_x(0, t)
            first = expert(0)
            for which in range(2):
                up(0, 0, which, first)

            def body(i, last):
                for r in range(R):
                    t, par = R * i + r, r % 2
                    more = not (last and r == R - 1)
                    if more:
                        following = expert(t + 1)
                        up(t + 1, 1 - par, 0, following)
                    turn_acts(t, par)
                    if not (last and r >= R - 2):
                        turn_x(i, r + 2)
                    if more:
                        up(t + 1, 1 - par, 1, following)
                    down(i, r, expert(t))

            with pe.Fori(0, LOOPS - 1) as i:
                body(i, False)
            body(LOOPS - 1, True)

        @block.scalar
        def _(act):
            def silu(t, par):
                act.wait_ge(ev["gate_made"], t + 1)
                if not (isinstance(t, int) and t == 0):
                    act.wait_ge(ev["acts_done"], t - 1)
                act.activation(gate[:, par, :], ps_up[:, par, 0, :], ACT.Silu).then_inc(ev["silu"], 1)

            def body(i, last):
                for r in range(R):
                    t, par = R * i + r, r % 2
                    if not (last and r == R - 1):
                        silu(t + 1, 1 - par)
                    act.wait_ge(ev["acts_turned"], t + 1)
                    act.wait_ge(ev["down_made"], t)
                    act.activation(acts_T[:, :, :], ps_a[:, :].rearrange("p (m n) -> p m n", m=FC),
                                   ACT.Copy).then_inc(ev["aT_copied"], 1)

            silu(0, 0)
            with act.Fori(0, LOOPS - 1) as i:
                body(i, False)
            body(LOOPS - 1, True)

        @block.vector
        def _(dve):
            link = chain(dve, ev["steps"], 0)
            link(dve.tensor_tensor(counts[:, :], mem["next_slot"][:, :], mem["slot0"][:, :], ALU.subtract))
            link(dve.tensor_tensor(over[:, :, :], counts[:, :].unsqueeze(2).to_broadcast([P, E, CAP]),
                                   mem["tile_rows"][:, 0:CAP].unsqueeze(1).to_broadcast([P, E, CAP]), ALU.is_gt))
            link(dve.tensor_reduce(need[:, :], over[:, :, :], AX.X, ALU.add))
            link(dve.tensor_tensor_scan(ends[:, :], mem["ones_e"][:, :], need[:, :], 0.0, ALU.mult, ALU.add))
            link(dve.tensor_scalar(need[:, :], need[:, :], -1.0, float(CAP), ALU.mult, ALU.add))
            index = mem["tile_index"][:, 0:TILES]
            link(dve.tensor_tensor(passed[:, :, :], index.unsqueeze(2).to_broadcast([P, TILES, E]),
                                   ends[:, :].unsqueeze(1).to_broadcast([P, TILES, E]), ALU.is_ge))
            link(dve.tensor_reduce(tile_f[:, 1, :], passed[:, :, :], AX.X, ALU.add))
            link(dve.tensor_scalar(tile_f[:, 1, :], tile_f[:, 1, :], float(E - 1), None, ALU.min))
            link(dve.tensor_tensor(skipped[:, :, :], passed[:, :, :], need[:, :].unsqueeze(1).to_broadcast([P, TILES, E]),
                                   ALU.mult))
            link(dve.tensor_reduce(tile_f[:, 0, :], skipped[:, :, :], AX.X, ALU.add))
            link(dve.tensor_tensor(tile_f[:, 0, :], tile_f[:, 0, :], index, ALU.add))
            dve.tensor_copy(tile_i[:, :, :], tile_f[:, :, :]).then_inc(ev["tiles"], 1)

            def copy_x(t, par):
                dve.wait_ge(ev["x_turned"], t + 1)
                if not (isinstance(t, int) and t < 2):
                    dve.wait_ge(ev["up_made"], t - 1)
                dve.tensor_copy(x_T[:, par, :, :], ps_x[:, 0:D].rearrange("p (c n) -> p c n", c=DC)).then_inc(ev["xT_copied"], 1)

            def act(t, par):
                dve.wait_ge(ev["silu"], t + 1)
                dve.wait_ge(ev["up_made"], t + 1)
                if not (isinstance(t, int) and t == 0):
                    dve.wait_ge(ev["acts_turned"], t - 1)
                dve.tensor_tensor(acts[:, par, :], gate[:, par, :], ps_up[:, par, 1, :], ALU.mult).then_inc(ev["acts_done"], 1)

            def weigh(i, r):
                dve.wait_ge(ev["down_made"], R * i + r + 1)
                if not (isinstance(i, int) and i == 0 and r < 2):
                    dve.wait_ge(y_added, 16 * (R * i + r - 1))
                dve.tensor_scalar(y[:, r % 2, :], ps_y[:, r % 2, 0:D], slot[:, r, 1:2].bitcast(FP32), None,
                                  ALU.mult).then_inc(ev["y_done"], 1)

            def body(i, last):
                for r in range(R):
                    t, par = R * i + r, r % 2
                    if not (last and r >= R - 2):
                        copy_x(t + 2, par)
                    if not (last and r == R - 1):
                        act(t + 1, 1 - par)
                    weigh(i, r)

            copy_x(0, 0)
            copy_x(1, 1)
            act(0, 0)
            body(0, False)
            with dve.Fori(1, LOOPS - 1) as i:
                body(i, False)
            body(LOOPS - 1, True)


INPUTS = ("x", "cls_tok", "L0_tok_w_qkv", "L0_tok_b_qkv", "L0_tok_w_out", "L0_tok_b_out", "L0_attn_a_params",
          "L0_attn_B_w", "L0_attn_C_w", "L0_attn_D", "L0_ffn_Wg_s", "L0_ffn_Wu_s", "L0_ffn_Wd_s", "L0_ffn_Wg",
          "L0_ffn_Wu", "L0_ffn_Wd", "L0_ffn_Wr", "L0_ffn_rb")


def laid_out(x, cls_tok, w_qkv, b_qkv, w_out, b_out, a_params, b_w, c_w, d, wg_s, wu_s, wd_s, wg, wu, wd, wr, rb):
    def chunks(w):
        return w.reshape(-1, P, w.shape[-1]).transpose(1, 0, 2)

    def experts(w):
        return w.transpose(0, 2, 1).reshape(E, -1, P, w.shape[1]).transpose(2, 0, 1, 3)

    w = w_qkv.reshape(H, 3, HD, D).transpose(3, 1, 0, 2).reshape(D, 3 * D)
    bias = b_qkv.reshape(H, 3, HD).transpose(1, 0, 2).reshape(3, D)
    return {
        "xT": x.reshape(B, S, D).transpose(0, 2, 1).reshape(B, DC, P, S), "cls": cls_tok.reshape(1, D),
        "wqkv": chunks(w), "bqk": bias[:2].reshape(4, P).T, "bv": bias[2:3], "wo_T": chunks(w_out.T),
        "bo": b_out.reshape(1, D), "a_params": a_params.reshape(P, 1), "b_w": chunks(b_w), "c_T": chunks(c_w.T),
        "d": d.reshape(1, D), "wg_s": chunks(wg_s.T), "wu_s": chunks(wu_s.T), "wd_s": chunks(wd_s.T),
        "wg_e": experts(wg), "wu_e": experts(wu), "wd_e": experts(wd), "wr_T": chunks(wr.T), "rb": rb.reshape(1, E),
    }


def constants():
    f32, n = np.float32, np.arange(D)
    k = np.arange(P)
    angle = 2 * np.pi / D * (np.outer(n, k) % D)
    nyquist = np.where(n % 2, -1.0, 1.0)
    to_planes = np.concatenate([np.cos(angle), -np.sin(angle)], 1)
    to_planes[:, P] = nyquist
    from_planes = 2.0 / D * to_planes
    from_planes[:, 0] /= 2
    from_planes[:, P] /= 2
    sine = -2 * np.sin(2 * np.pi / D * (np.outer(k + 1, k) % D))
    sine[P - 1] = 0
    rows = np.arange(SLOTS)
    p = np.arange(P)
    return {
        "ident": np.eye(P, dtype=f32),
        "before": (p[:, None] < p[None, :]).astype(f32),
        "sine": sine.astype(f32),
        "to_planes": to_planes.reshape(2, P, D).transpose(1, 0, 2).astype(f32),
        "from_planes": from_planes.reshape(2, P, D).transpose(1, 0, 2).astype(f32),
        "table_init": np.stack([ROWS + rows % P, 0 * rows], 1).astype(np.int32),
        "iota_e": np.tile(np.arange(E, dtype=f32), (P, 1)),
        "slot0": np.tile(np.arange(E, dtype=f32) * CAP * P, (P, 1)),
        "first": (p == 0).astype(f32)[:, None],
        "spare": np.where(p[:, None] == 0, 0, SLOTS + p[:, None] + [[0, P]]).astype(f32),
        "row_first": (1 + p[:, None] + P * np.arange(TT)[None, :]).astype(f32),
        "tile_index": np.tile(np.arange(TILES, dtype=f32), (P, 1)),
        "tile_rows": np.tile(np.arange(TILES, dtype=f32) * P, (P, 1)),
    }


def program(nc, dram):
    with ExitStack() as ctx:
        sb, _, sem = places(nc, ctx)
        mem = {"later_in": sem("later_in"), "experts_in": sem("experts_in")}

        def rows(name):
            return dram[name].to_broadcast([P, dram[name].shape[1]])

        kept = {
            "ident": ([P, P], dram["ident"]), "bo_row": ([P, D], rows("bo")), "d_row": ([P, D], rows("d")),
            "wo_T": ([P, DC, D], dram["wo_T"]), "wr_T": ([P, DC, E], dram["wr_T"]), "rb_row": ([P, E], rows("rb")),
            "wg_s": ([P, DC, F], dram["wg_s"]), "wu_s": ([P, DC, F], dram["wu_s"]), "wd_s": ([P, FC, D], dram["wd_s"]),
            "iota_e": ([P, E], dram["iota_e"]), "slot0": ([P, E], dram["slot0"]), "first": ([P, 1], dram["first"]),
            "spare": ([P, 2], dram["spare"]), "row_id": ([P, TT], dram["row_first"]),
            "tile_index": ([P, TILES], dram["tile_index"]), "tile_rows": ([P, TILES], dram["tile_rows"]),
            "before_f": ([P, P], dram["before"]),
        }
        for name, (shape, _) in kept.items():
            mem[name] = sb("k_" + name, shape, FP32)
        for name, shape, dtype in (
                ("identb", [P, P], BF16), ("before", [P, P], BF16), ("all_ones", [P, P], BF16), ("ones_e", [P, E], FP32),
                ("m1_T", [P, DC, D], FP32), ("m2_T", [P, 2, D], FP32), ("cos", [P, T1], FP32), ("sin", [P, T1], FP32),
                ("state0", [P, 2], FP32), ("zeros", [P, D], FP32), ("minus_half", [P, TT], FP32),
                ("best", [P, TT, 2], FP32), ("hot", [P, TT, 2, E], FP32), ("eq", [P, TT, E], FP32), ("key", [P, TT, E], FP32),
                ("least", [P, TT], FP32), ("pos", [P, TT, E], FP32), ("slot_f", [P, TT, 2], FP32),
                ("slot_i", [P, TT, 2], I32), ("pay", [P, TT, 2, 2], I32), ("next_slot", [P, E], FP32)):
            mem[name] = sb("k_" + name, shape, dtype)
        loads = [(mem[name][tuple(slice(None) for _ in shape)], src) for name, (shape, src) in kept.items()]
        mem["later_loads"] = loads
        with ExitStack() as first:
            sb1, _, _ = places(nc, first)
            for name, shape in (("wqkv", [P, DC, 3 * D]), ("bqk", [P, 4]), ("bv", [P, D])):
                mem[name] = sb1("k_" + name, shape, FP32)
            mem["first_loads"] = [(mem["wqkv"][:, :, :], dram["wqkv"]), (mem["bqk"][:, :], dram["bqk"]),
                                  (mem["bv"][:, :], rows("bv"))]
            stage_qkv(nc, mem, dram)
        stage_setup(nc, mem, dram)
        stage_attention(nc, mem, dram)
        with ExitStack() as last:
            sb5, _, _ = places(nc, last)
            mem["wg_e"] = sb5("k_wg_e", [P, E, DC, F], FP32)
            mem["wu_e"] = sb5("k_wu_e", [P, E, DC, F], FP32)
            mem["wd_e"] = sb5("k_wd_e", [P, E, FC, D], FP32)
            stage_mix(nc, mem, dram)
            stage_experts(nc, mem, dram)


def kernel(**inputs):
    import concourse.bacc as _bacc
    from concourse.bass_utils import run_bass_kernel_spmd as _run

    arrays = dict(constants(), **laid_out(*(np.asarray(inputs[name]) for name in INPUTS)))
    arrays = {name: np.ascontiguousarray(a) for name, a in arrays.items()}
    nc = _bacc.Bacc("TRN2", target_bir_lowering=False, num_devices=1)
    dram = {name: nc.dram_tensor("in_" + name, a.shape, mybir.dt.from_np(a.dtype), kind="ExternalInput").ap()
            for name, a in arrays.items()}
    for name, shape, dtype in (
            ("qk", (B, 2, PARTS, D, S), BF16), ("v", (B, P, TT * H * VW), FP32), ("heads", (B, P, TT * D), FP32),
            ("x_rows", (ROWS + P, D), FP32), ("table", (SLOTS + 2 * P, 2), I32)):
        dram[name] = nc.dram_tensor("kept_" + name, shape, dtype, kind="Internal").ap()
    dram["out"] = nc.dram_tensor("out_rows", (ROWS + P, D), FP32, kind="ExternalOutput").ap()
    program(nc, dram)
    result = _run(nc, [{"in_" + name: a for name, a in arrays.items()}], core_ids=[0])
    return result.results[0]["out_rows"][:ROWS].reshape(B, T1, D)
```

```python
from contextlib import ExitStack

import numpy as np

import concourse.bass as bass
from concourse import mybir

FP32 = mybir.dt.float32
BF16 = mybir.dt.bfloat16
I32 = mybir.dt.int32
U32 = mybir.dt.uint32
ALU = mybir.AluOpType
ACT = mybir.ActivationFunctionType
AX = mybir.AxisListType

P = 128
B, S, D = 8, 512, 256
DC = D // P
TT = S // P
H, HD = 16, 16
G = 4
NG = H // G
PARTS = 3
Q_PART = (0, 0, 0, 1, 1, 2)
K_PART = (0, 1, 2, 0, 1, 0)
KROWS = HD * len(Q_PART)
SROWS = KROWS + PARTS
VW = 2 * HD

E = 8
F = 512
FC = F // P
T1 = S + 1
ROWS = B * T1
CAP = (ROWS + P - 1) // P
RING = 8
TILES = -(-((2 * ROWS + E * (P - 1)) // P) // RING) * RING
SPARE = TILES - 2 * ROWS // P
SLOTS = (E * CAP + SPARE) * P
EPS = 1e-5


def short(ap):
    return ap.bitcast(mybir.dt.float32r)


def split_products(pe, out, lhs, rhs, start, stop):
    for n, (a, b) in enumerate(((0, 0), (0, 1), (1, 0))):
        mm = pe.matmul(out, short(lhs[a]), short(rhs[b]), start=(start and n == 0), stop=(stop and n == 2))
    return mm


def places(nc, ctx):
    def sb(name, shape, dtype):
        return ctx.enter_context(nc.sbuf_tensor(name, shape, dtype))

    def pb(name, shape, dtype):
        return ctx.enter_context(nc.psum_tensor(name, shape, dtype))

    def sem(name):
        return ctx.enter_context(nc.semaphore(name))

    return sb, pb, sem


def chain(eng, sem, start):
    count = [0]

    def link(instruction, wait=True):
        count[0] += 1
        instruction.then_inc(sem, 1)
        if wait:
            eng.wait_ge(sem, start + count[0])

    return link


def stage_qkv(nc, mem, dram):
    wqkv, bqk, bv = mem["wqkv"], mem["bqk"], mem["bv"]
    with ExitStack() as ctx:
        sb, pb, sem = places(nc, ctx)
        xt = mem["wu_e"][:, 0:2, :, :]
        qk_full, qk_rest = (mem["wu_e"][:, n:n + 2, :, :].rearrange("p e c n -> p (e c) n") for n in (2, 4))
        qk_parts = sb("qk_parts", [P, 4, PARTS, S], BF16)
        v_ones = sb("v_ones", [P, TT, H, VW], FP32)
        qk_ps = pb("qk_ps", [P, 4, S], FP32)
        v_ps = pb("v_ps", [P, 2, 2, D], FP32)
        fold_ps = pb("fold_ps", [P, 2, S], FP32)
        b_w, c_T = mem["mix_ud"][:, 0:2, :], mem["mix_ud"][:, 2:4, :]
        to_planes, from_planes = mem["mix_u"][:, 0:2, :], mem["mix_u"][:, 2:4, :]
        a_col = sb("a_col", [P, 1], FP32)
        sine = sb("sine", [P, P], FP32)
        before_f = sb("before_f", [P, P], FP32)
        lam = sb("lam", [P, 4], FP32)
        weights_in = sem("weights_in")
        x_in = [sem(f"x_in{n}") for n in range(2)]
        x_used = [sem(f"x_used{n}") for n in range(2)]
        qk_out = [sem(f"qk_out{n}") for n in range(4)]
        cut = [sem(f"cut{n}") for n in range(4)]
        parts_stored = [sem(f"parts_stored{n}") for n in range(4)]
        qk_made = sem("qk_made")
        v_half_made = sem("v_half_made")
        cut_step = sem("cut_step")
        v_step = sem("v_step")
        v_stored = sem("v_stored")
        ones_set = sem("ones_set")
        later_in = sem("later_in")
        omega_made = sem("omega_made")
        folded = sem("folded")
        lam_step = sem("lam_step")
        filled = sem("filled")
        block = ctx.enter_context(nc.Block())
        later_loads = mem["later_loads"] + [
            (a_col[:, :], dram["a_params"]), (sine[:, :], dram["sine"]), (b_w[:, :, :], dram["b_w"]),
            (c_T[:, :, :], dram["c_T"]), (to_planes[:, :, :], dram["to_planes"]),
            (from_planes[:, :, :], dram["from_planes"]), (before_f[:, :], dram["before"])]

        @block.gpsimd
        def _(pool):
            pool.memset(v_ones[:, :, :, :], 1.0).then_inc(ones_set, 1)
            with pool.Fori(0, B // 2) as i:
                for par in range(2):
                    pool.wait_ge(x_used[par], i)
                    pool.wait_ge(ones_set, 1)
                    pool.dma_start(xt[:, par, :, :], dram["xT"][bass.ds(2 * i + par, 1), :, :, :]
                                   .rearrange("b c p t -> p (b c) t")).then_inc(x_in[par], 16)
            pool.memset(mem["max_parts"][:, :, :], 0.0).then_inc(ones_set, 1)
            pool.wait_ge(ones_set, 2)
            pool.memset(mem["k_rows"][KROWS:SROWS, :, :, :], 1.0)

        @block.sync
        def _(sp):
            for dst, src in mem["first_loads"]:
                sp.dma_start(dst, src).then_inc(weights_in, 16)
            for dst, src in later_loads:
                sp.dma_start(dst, src).then_inc(later_in, 16)
            sp.dma_start(dram["table"][0:SLOTS, :].rearrange("(p n) c -> p (n c)", p=P),
                         dram["table_init"].rearrange("(p n) c -> p (n c)", p=P)).then_inc(filled, 16)
            sp.wait_ge(lam_step, 1)
            sp.dma_start(dram["x_rows"][ROWS:ROWS + P, :], mem["zeros"][:, :]).then_inc(filled, 16)
            sp.dma_start(dram["out"][ROWS:ROWS + P, :], mem["zeros"][:, :]).then_inc(filled, 16)

            def store(b):
                for j in range(4):
                    sp.wait_ge(cut[j], b + 1)
                    sp.dma_start(
                        dram["qk"][bass.ds(b, 1), j // 2, :, (j % 2) * P:(j % 2 + 1) * P, :]
                        .rearrange("b s p n -> p (b s) n"), qk_parts[:, j, :, :]).then_inc(parts_stored[j], 16)
                sp.wait_ge(v_step, TT * b + TT)
                sp.dma_start(dram["v"][bass.ds(b, 1), :, :].rearrange("b p n -> p (b n)"),
                             v_ones[:, :, :, :].rearrange("p t h w -> p (t h w)")).then_inc(v_stored, 16)

            with sp.Fori(0, B - 2) as b:
                store(b)
            for j in range(4):
                sp.wait_ge(parts_stored[j], 16)
            sp.wait_ge(v_stored, 16)
            load_unit(sp, mem, dram, 0, 0)
            store(B - 2)
            store(B - 1)
            for j in range(4):
                sp.wait_ge(parts_stored[j], 16 * B)
            sp.wait_ge(v_stored, 16 * B)
            sp.wait_ge(filled, 16 * 3)

        @block.tensor
        def _(pe):
            pe.wait_ge(weights_in, 16 * len(mem["first_loads"]))
            with pe.Fori(0, B // 2) as i:
                for par in range(2):
                    b = 2 * i + par
                    pe.wait_ge(x_in[par], 16 * i + 16)
                    for j in range(4):
                        pe.wait_ge(qk_out[j], b)
                        for c in range(DC):
                            mm = pe.matmul(qk_ps[:, j, :], wqkv[:, c, j * P:(j + 1) * P], xt[:, par, c, :],
                                           start=(c == 0), stop=(c == DC - 1))
                        mm.then_inc(qk_made, 1)
                    pe.wait_ge(v_step, TT * b)
                    for t in range(TT):
                        for c in range(DC):
                            mm = pe.matmul(v_ps[:, t // 2, t % 2, :], xt[:, par, c, t * P:(t + 1) * P],
                                           wqkv[:, c, 2 * D:3 * D], start=(c == 0), stop=(c == DC - 1))
                        if t == 1:
                            mm.then_inc(v_half_made, 1)
                    mm.then_inc(x_used[par], 1)
            pe.wait_ge(later_in, 16 * len(later_loads))
            for m in range(2):
                for c in range(2):
                    mm = pe.matmul(fold_ps[:, 0, m * D:(m + 1) * D], b_w[:, c, m * P:(m + 1) * P], to_planes[:, c, :],
                                   start=(c == 0), stop=(c == 1))
            mm.then_inc(folded, 1)
            for m in range(2):
                for c in range(2):
                    mm = pe.matmul(fold_ps[:, 1, m * D:(m + 1) * D], from_planes[:, c, m * P:(m + 1) * P], c_T[:, c, :],
                                   start=(c == 0), stop=(c == 1))
            mm.then_inc(folded, 1)
            pe.wait_ge(qk_out[0], B)
            pe.matmul(qk_ps[:, 0, 0:1], sine[:, :], a_col[:, :], start=True, stop=True).then_inc(omega_made, 1)

        @block.scalar
        def _(act):
            act.wait_ge(weights_in, 16 * len(mem["first_loads"]))
            with act.Fori(0, B) as b:
                for j in range(4):
                    act.wait_ge(cut[j], b)
                    act.wait_ge(qk_made, 4 * b + j + 1)
                    act.activation(qk_full[:, j, :], qk_ps[:, j, :], ACT.Identity,
                                   bias=bqk[:, j:j + 1]).then_inc(qk_out[j], 1)
            act.wait_ge(later_in, 16 * len(later_loads))
            act.activation(mem["identb"][:, :], mem["ident"][:, :], ACT.Copy)
            act.activation(mem["before"][:, :], before_f[:, :], ACT.Copy)
            for n, name in enumerate(("m1_T", "m2_T")):
                act.wait_ge(folded, n + 1)
                act.activation(mem[name][:, :, :], fold_ps[:, n, :].rearrange("p (m n) -> p m n", m=2), ACT.Copy)

        @block.vector
        def _(dve):
            dve.memset(mem["zeros"][:, :], 0.0)
            dve.memset(mem["minus_half"][:, :], -0.5)
            dve.memset(mem["all_ones"][:, :], 1.0)
            dve.memset(mem["ones_e"][:, :], 1.0)
            dve.memset(mem["cos"][:, 0:1], 1.0)
            dve.memset(mem["sin"][:, 0:1], 0.0).then_inc(lam_step, 1)
            dve.wait_ge(weights_in, 16 * len(mem["first_loads"]))
            dve.wait_ge(ones_set, 1)
            with dve.Fori(0, B // 2) as i:
                for par in range(2):
                    b = 2 * i + par
                    for j in range(4):
                        full, rest, parts = qk_full[:, j, :], qk_rest[:, j, :], qk_parts[:, j, :, :]
                        n = 12 * b + 3 * j
                        dve.wait_ge(parts_stored[j], 16 * b)
                        dve.wait_ge(qk_out[j], b + 1)
                        dve.tensor_copy(parts[:, 0, :], full).then_inc(cut_step, 1)
                        dve.wait_ge(cut_step, n + 1)
                        dve.tensor_tensor(rest, full, parts[:, 0, :], ALU.subtract).then_inc(cut_step, 1)
                        dve.wait_ge(cut_step, n + 2)
                        dve.tensor_copy(parts[:, 1, :], rest).then_inc(cut_step, 1)
                        dve.wait_ge(cut_step, n + 3)
                        dve.tensor_tensor(parts[:, 2, :], rest, parts[:, 1, :], ALU.subtract).then_inc(cut[j], 1)
                    dve.wait_ge(v_stored, 16 * b)
                    for t in range(TT):
                        if t < 2:
                            dve.wait_ge(v_half_made, b + 1)
                        else:
                            dve.wait_ge(x_used[par], i + 1)
                        dve.tensor_tensor(v_ones[:, t, :, 0:HD],
                                          v_ps[:, t // 2, t % 2, :].rearrange("p (h d) -> p h d", h=H),
                                          bv[:, :].rearrange("p (h d) -> p h d", h=H), ALU.add).then_inc(v_step, 1)
            w, w2, den, num = (lam[:, n:n + 1] for n in range(4))
            power = mem["power"]
            link = chain(dve, lam_step, 1)
            dve.wait_ge(omega_made, 1)
            link(dve.tensor_copy(w, qk_ps[:, 0, 0:1]))
            link(dve.tensor_tensor(w2, w, w, ALU.mult))
            link(dve.tensor_scalar(den, w2, 1.0, None, ALU.add))
            link(dve.reciprocal(den, den))
            link(dve.tensor_scalar(num, w2, -1.0, 1.0, ALU.mult, ALU.add))
            link(dve.tensor_tensor(power[:, 0, 0:1], num, den, ALU.mult))
            link(dve.tensor_scalar(w, w, -2.0, None, ALU.mult))
            link(dve.tensor_tensor(power[:, 0, 1:2], w, den, ALU.mult))


LOADS = 2 * len(Q_PART) + 1


def load_unit(sp, mem, dram, b, g, v_used=None):
    q_rows, k_rows, v_unit, done = mem["q_rows"], mem["k_rows"], mem["v_unit"], mem["unit_in"][g]
    for which, rows, order in ((0, q_rows, Q_PART), (1, k_rows, K_PART)):
        for n, s in enumerate(order):
            sp.dma_start(rows[HD * n:HD * (n + 1), g, :, :],
                         dram["qk"][bass.ds(b, 1), which, s, G * HD * g:G * HD * (g + 1), :]
                         .rearrange("b (h d) n -> d (b h) n", h=G)).then_inc(done, 16)
    if v_used is not None:
        sp.wait_ge(v_used, b)
    sp.dma_start(v_unit[:, g, :, :, :].rearrange("p t h w -> p t (h w)"),
                 dram["v"][bass.ds(b, 1), :, :].rearrange("b p (t n) -> p (b t) n", t=TT)
                 [:, :, G * VW * g:G * VW * (g + 1)]).then_inc(done, 16)


def raise_powers(pool, link, mem, scratch, k):
    cos, sin, power = mem["cos"], mem["sin"], mem["power"]
    n = 2 ** k
    m = min(n, S + 1 - n)
    pc, ps = power[:, k, 0:1], power[:, k, 1:2]
    for to, part, by in ((0, cos, pc), (1, sin, ps), (2, cos, ps), (3, sin, pc)):
        link(pool.tensor_tensor(scratch[:, to, 0:m], part[:, 0:m], by.to_broadcast([P, m]), ALU.mult))
    link(pool.tensor_tensor(cos[:, n:n + m], scratch[:, 0, 0:m], scratch[:, 1, 0:m], ALU.subtract))
    link(pool.tensor_tensor(sin[:, n:n + m], scratch[:, 2, 0:m], scratch[:, 3, 0:m], ALU.add))
    if n < S:
        link(pool.tensor_tensor(scratch[:, 4, 0:2], power[:, k, :], power[:, k, :], ALU.mult))
        link(pool.tensor_tensor(power[:, k + 1, 0:1], scratch[:, 4, 0:1], scratch[:, 4, 1:2], ALU.subtract))
        link(pool.tensor_tensor(scratch[:, 4, 2:3], pc, ps, ALU.mult))
        link(pool.tensor_tensor(power[:, k + 1, 1:2], scratch[:, 4, 2:3], scratch[:, 4, 2:3], ALU.add))


def stage_attention(nc, mem, dram):
    ident, identb = mem["ident"], mem["identb"]
    with ExitStack() as ctx:
        sb, pb, sem = places(nc, ctx)
        q_rows, k_rows, v_unit, unit_in = (mem[n] for n in ("q_rows", "k_rows", "v_unit", "unit_in"))
        max_parts = mem["max_parts"]
        probs = mem["probs"]
        neg_max = sb("neg_max", [P, 2, G * TT], FP32)
        neg_rest = sb("neg_rest", [P, G * TT], FP32)
        max_rows = sb("max_rows", [PARTS * G * TT, P], BF16)
        heads_T = sb("heads_T", [P, S], FP32)
        row_sum = sb("row_sum", [P, TT, G], FP32)
        heads = mem["heads"]
        turned_by = sb("turned_by", [P, 5, S // 2], FP32)
        by_query = pb("by_query", [P, 4, S], FP32)
        by_key = pb("by_key", [P, 2, S], FP32)
        pv = pb("pv", [P, S], FP32)
        turned = pb("turned", [P, S], FP32)
        unit_used = [sem(f"unit_used{n}") for n in range(NG)]
        max_in = [sem(f"max_in{n}") for n in range(NG)]
        exp_done = [sem(f"exp_done{n}") for n in range(2)]
        split_step = sem("split_step")
        power_step = sem("power_step")
        query_scored = sem("query_scored")
        max_taken = sem("max_taken")
        max_split = sem("max_split")
        max_turned = sem("max_turned")
        max_copied = sem("max_copied")
        key_scored = sem("key_scored")
        pv_copied = sem("pv_copied")
        heads_turned = sem("heads_turned")
        sum_inv = sem("sum_inv")
        heads_done = sem("heads_done")
        heads_stored = mem["heads_stored"]
        first_in = sem("first_in")
        block = ctx.enter_context(nc.Block())
        turned_max = turned[:, 0:P // 2].bitcast(BF16)
        LAST = B - 1

        @block.gpsimd
        def _(pool):
            def split_max(b, g):
                u, rows = NG * b + g, neg_max[:, g % 2, :]
                pool.wait_ge(max_taken, G * TT // 2 * (u + 1))
                pool.wait_ge(max_turned, u)
                pool.sem_inc(split_step)
                pool.tensor_copy(max_parts[:, 0, :], rows).then_inc(max_split, 1)
                pool.wait_ge(max_split, 4 * u + 1)
                pool.tensor_tensor(neg_rest[:, :], rows, max_parts[:, 0, :], ALU.subtract).then_inc(max_split, 1)
                pool.wait_ge(max_split, 4 * u + 2)
                pool.sem_inc(split_step)
                pool.tensor_copy(max_parts[:, 1, :], neg_rest[:, :]).then_inc(max_split, 1)
                pool.wait_ge(max_split, 4 * u + 3)
                pool.tensor_tensor(max_parts[:, 2, :], neg_rest[:, :], max_parts[:, 1, :],
                                   ALU.subtract).then_inc(max_split, 1)

            def place_max(b, g):
                pool.wait_ge(max_copied, NG * b + g + 1)
                pool.sem_inc(split_step)
                pool.dma_start(q_rows[KROWS:SROWS, g, :, :].rearrange("s h (t p) -> s (h t) p", t=TT),
                               max_rows[:, :]).then_inc(max_in[g], 16)

            def batch(b):
                for g in range(NG):
                    b1, g1 = b + (g + 1) // NG, (g + 1) % NG
                    if not (isinstance(b1, int) and b1 > LAST):
                        place_max(b1, g1)
                    b2, g2 = b + (g + 2) // NG, (g + 2) % NG
                    if not (isinstance(b2, int) and b2 > LAST):
                        split_max(b2, g2)

            link = chain(pool, power_step, 0)
            for g in range(2):
                split_max(0, g)
                for k in range(2 * g, 2 * g + 2):
                    raise_powers(pool, link, mem, turned_by, k)
                if g == 0:
                    place_max(0, 0)
            for g in range(NG):
                place_max((g + 1) // NG, (g + 1) % NG)
                b2, g2 = (g + 2) // NG, (g + 2) % NG
                split_max(b2, g2)
                for k in ((4, 5), (6, 7), (8,), (9,))[g]:
                    raise_powers(pool, link, mem, turned_by, k)
            with pool.Fori(1, LAST) as b:
                batch(b)
            batch(LAST)

        @block.sync
        def _(sp):
            def reload_unit(b, g):
                sp.wait_ge(key_scored, G * TT * (NG * b + g - NG + 1))
                load_unit(sp, mem, dram, b, g, unit_used[g])

            def store_heads(b):
                sp.wait_ge(heads_done, NG * b + NG)
                sp.dma_start(dram["heads"][bass.ds(b, 1), :, :].rearrange("b p n -> p (b n)"),
                             heads[:, :, :].rearrange("p t n -> p (t n)")).then_inc(heads_stored, 16)

            for g in range(1, NG):
                load_unit(sp, mem, dram, 0, g)
            with sp.Fori(1, B) as b:
                for g in range(NG):
                    reload_unit(b, g)
                store_heads(b - 1)
            sp.dma_start(mem["heads_in"][:, :, :].rearrange("p t n -> p (t n)"), dram["heads"][0, :, :]).then_inc(first_in, 16)
            sp.wait_ge(first_in, 16)
            store_heads(LAST)

        def before(b, g):
            return (b, g - 1) if g else (b - 1, NG - 1)

        def key_tile(j):
            return j // 8 * 2 + j % 2

        EARLY_PV = ((), (0, 1), (2,), (3, 4), (5,), (6, 7))
        LATE_PV = ((), (8, 9), (10, 11), (12,), (13, 14), (15,))

        @block.tensor
        def _(pe):
            def score_by_query(b, g, k):
                h, t = k // TT, k % TT
                pairs = (NG * b + g) * (G * TT // 2) + k // 2
                if k % 2 == 0 and not (isinstance(pairs, int) and pairs < 2):
                    pe.wait_ge(max_taken, pairs - 1)
                pe.matmul(by_query[:, k % 4, :],
                          q_rows[0:KROWS, g, h, t * P:(t + 1) * P], k_rows[0:KROWS, g, h, :],
                          start=True, stop=True).then_inc(query_scored, 1)

            def score_by_key(b, g, j):
                kt, h = key_tile(j), j // 2 % G
                pe.wait_ge(exp_done[j % 2], G * TT // 2 * (NG * b + g) + j // 2)
                pe.matmul(by_key[:, j % 2, :], k_rows[0:SROWS, g, h, kt * P:(kt + 1) * P],
                          q_rows[0:SROWS, g, h, :], start=True, stop=True).then_inc(key_scored, 1)

            def add_pv(b, g, steps):
                for n in steps:
                    kt, h = n // G, n % G
                    if n == 0:
                        pe.wait_ge(pv_copied, NG * b + g)
                    if n % 8 == 0:
                        for buf in range(2):
                            pe.wait_ge(exp_done[buf], G * TT // 2 * (NG * b + g) + G + n // 2)
                    mm = pe.matmul(pv[VW * h:VW * (h + 1), :], v_unit[:, g, kt, h, :],
                                   probs[:, G * (kt // 2) + h, kt % 2, :], start=(kt == 0), stop=(kt == TT - 1))
                    if n == G * TT - 1:
                        mm.then_inc(unit_used[g], 1)

            def turn_max(b, g):
                u = NG * b + g
                pe.wait_ge(max_split, 4 * u + 4)
                if not (isinstance(u, int) and u < 3):
                    pe.wait_ge(heads_done, u - 2)
                pe.transpose(turned_max, max_parts[:, :, :].rearrange("p s n -> p (s n)"),
                             identb[:, :]).then_inc(max_turned, 1)

            def turn_heads(b, g, maxima):
                pe.wait_ge(pv_copied, NG * b + g + 1)
                if maxima:
                    pe.wait_ge(max_copied, NG * b + g + 3)
                else:
                    pe.wait_ge(heads_done, NG * b + g)
                for t in range(TT):
                    mm = pe.transpose(turned[:, t * P:(t + 1) * P], heads_T[:, t * P:(t + 1) * P], ident[:, :])
                mm.then_inc(heads_turned, 1)

            def unit(b, g):
                b2, g2 = b + (g + 2) // NG, (g + 2) % NG
                ahead = not (isinstance(b2, int) and b2 > LAST)
                b1, g1 = b + (g + 1) // NG, (g + 1) % NG
                next_max = not (isinstance(b1, int) and b1 > LAST)
                prev = not (isinstance(b, int) and b == 0 and g == 0)
                bp, gp = before(b, g)
                if ahead:
                    pe.wait_ge(unit_in[g2], 16 * LOADS * (b2 + 1))
                pe.wait_ge(max_in[g], 16 * (b + 1))
                for j in range(G * TT):
                    score_by_key(b, g, j)
                    if j == 4 and next_max:
                        turn_max(b1, g1)
                    if ahead:
                        score_by_query(b2, g2, j)
                    if j == 10 and prev:
                        turn_heads(bp, gp, next_max)
                    if 2 <= j < 8 and prev:
                        add_pv(bp, gp, LATE_PV[j - 2])
                    if j >= 10:
                        add_pv(b, g, EARLY_PV[j - 10])

            for g in range(2):
                pe.wait_ge(unit_in[g], 16 * LOADS)
                for k in range(G * TT):
                    score_by_query(0, g, k)
                    if g == 1 and k == 3:
                        turn_max(0, 0)
            for g in range(NG):
                unit(0, g)
            with pe.Fori(1, LAST) as b:
                for g in range(NG):
                    unit(b, g)
            for g in range(NG):
                unit(LAST, g)
            add_pv(LAST, NG - 1, range(8, 16))
            turn_heads(LAST, NG - 1, False)

        @block.vector
        def _(dve):
            def take_max(b, g, n):
                u = NG * b + g
                if n == 0 and not (isinstance(u, int) and u < 2):
                    dve.wait_ge(max_split, 4 * (u - 1))
                dve.wait_ge(query_scored, u * G * TT + 2 * n + 2)
                dve.tensor_reduce(neg_max[:, g % 2, 2 * n:2 * n + 2], by_query[:, 2 * (n % 2):2 * (n % 2) + 2, :], AX.X,
                                  ALU.max, negate=True).then_inc(max_taken, 1)

            def normalise(b, g):
                u = NG * b + g
                cols = turned[:, :].rearrange("p (t h w) -> p t h w", t=TT, h=G)
                dve.wait_ge(heads_turned, u + 1)
                dve.reciprocal(row_sum[:, :, :], cols[:, :, :, HD]).then_inc(sum_inv, 1)
                dve.wait_ge(sum_inv, u + 1)
                if g == 0:
                    dve.wait_ge(heads_stored, 16 * b)
                dve.tensor_tensor(heads[:, :, G * HD * g:G * HD * (g + 1)].rearrange("p t (h w) -> p t h w", h=G),
                                  cols[:, :, :, 0:HD],
                                  row_sum[:, :, :].unsqueeze(3).to_broadcast([P, TT, G, HD]),
                                  ALU.mult).then_inc(heads_done, 1)

            def unit(b, g):
                b2, g2 = b + (g + 2) // NG, (g + 2) % NG
                ahead = not (isinstance(b2, int) and b2 > LAST)
                prev = not (isinstance(b, int) and b == 0 and g == 0)
                for n in range(G * TT // 2):
                    if ahead:
                        take_max(b2, g2, n)
                    if n == 5 and prev:
                        normalise(*before(b, g))

            for g in range(2):
                for n in range(G * TT // 2):
                    take_max(0, g, n)
            for g in range(NG):
                unit(0, g)
            with dve.Fori(1, LAST) as b:
                for g in range(NG):
                    unit(b, g)
            for g in range(NG):
                unit(LAST, g)
            normalise(LAST, NG - 1)

        @block.scalar
        def _(act):
            def copy_max(b, g):
                u = NG * b + g
                act.wait_ge(max_turned, u + 1)
                if not (isinstance(u, int) and u < 1):
                    bp, gp = before(b, g)
                    act.wait_ge(max_in[gp], 16 * bp + 16)
                act.activation(max_rows[:, :], turned_max[0:PARTS * G * TT, :], ACT.Copy).then_inc(max_copied, 1)

            def exponentials(b, g, j):
                act.wait_ge(key_scored, G * TT * (NG * b + g) + j + 1)
                act.activation(probs[:, key_tile(j) // 2 * G + j // 2 % G, j % 2, :], by_key[:, j % 2, :], ACT.Exp,
                               scale=float(HD) ** -0.5).then_inc(exp_done[j % 2], 1)

            def copy_pv(b, g):
                act.wait_ge(unit_used[g], b + 1)
                act.wait_ge(heads_turned, NG * b + g)
                act.activation(heads_T[:, :], pv[:, :], ACT.Copy).then_inc(pv_copied, 1)

            def unit(b, g):
                b1, g1 = b + (g + 1) // NG, (g + 1) % NG
                for j in range(G * TT):
                    exponentials(b, g, j)
                    if j == 5 and not (isinstance(b1, int) and b1 > LAST):
                        copy_max(b1, g1)
                    if j == 8 and not (isinstance(b, int) and b == 0 and g == 0):
                        copy_pv(*before(b, g))

            copy_max(0, 0)
            for g in range(NG):
                unit(0, g)
            with act.Fori(1, LAST) as b:
                for g in range(NG):
                    unit(b, g)
            for g in range(NG):
                unit(LAST, g)
            copy_pv(LAST, NG - 1)


def top_two(dve, link, mem, probs, t):
    iota = mem["iota_e"][:, :].unsqueeze(1).to_broadcast([P, t, E])
    eq, key, least = mem["eq"][:, 0:t, :], mem["key"][:, 0:t, :], mem["least"][:, 0:t]
    for n in range(2):
        best, hot = mem["best"][:, 0:t, n], mem["hot"][:, 0:t, n, :]
        link(dve.tensor_reduce(best, probs, AX.X, ALU.max))
        link(dve.tensor_tensor(eq, probs, best.unsqueeze(2).to_broadcast([P, t, E]), ALU.is_equal))
        link(dve.tensor_scalar(eq, eq, -float(E), None, ALU.mult))
        link(dve.tensor_tensor(key, eq, iota, ALU.add))
        link(dve.tensor_reduce(least, key, AX.X, ALU.min))
        link(dve.tensor_tensor(hot, key, least.unsqueeze(2).to_broadcast([P, t, E]), ALU.is_equal))
        if n == 0:
            link(dve.tensor_scalar(key, hot, -4.0, None, ALU.mult))
            link(dve.tensor_tensor(probs, probs, key, ALU.add))


TOP_STEPS = 14


def slot_rows(dve, link, mem, t, row_id):
    pos, picked, slot_f = mem["pos"][:, 0:t, :], mem["eq"][:, 0:t, :], mem["slot_f"]
    for n in range(2):
        link(dve.tensor_tensor(picked, mem["hot"][:, 0:t, n, :], pos, ALU.mult))
        link(dve.tensor_reduce(slot_f[:, 0:t, n], picked, AX.X, ALU.add))
        link(dve.tensor_copy(mem["pay"][:, 0:t, n, 0], row_id))
        link(dve.tensor_copy(mem["pay"][:, 0:t, n, 1].bitcast(FP32), mem["best"][:, 0:t, n]))


SLOT_STEPS = 8


POOL_CUTS = ((0, 1, 2), (11, 14))
DVE_CUTS = ((3, 4), (5, 6, 7, 8, 9, 10, 12, 13, 15))


def shorten_weights(act, mem, n):
    w, part = (mem[("wg_" if n < E else "wu_") + name] for name in ("e", "short"))
    act.activation(short(part[:, n % E, :, :]), w[:, n % E, :, :], ACT.Copy).then_inc(mem["ev_cut"]["shortened"], 1)


def cut_weights(eng, mem, n):
    w, part, rest = (mem[("wg_" if n < E else "wu_") + name] for name in ("e", "short", "rest"))
    eng.wait_ge(mem["ev_cut"]["shortened"], n + 1)
    return eng.tensor_tensor(short(rest[:, n % E, :, :]), w[:, n % E, :, :], part[:, n % E, :, :], ALU.subtract)


def stage_mix(nc, mem, dram):
    ident = mem["ident"]
    with ExitStack() as ctx:
        sb, pb, sem = places(nc, ctx)
        heads = mem["heads_in"]
        h, u, ud = (mem["mix_" + n] for n in ("h", "u", "ud"))
        by_feature = "p (c t) n -> p c (t n)"
        heads_T, u_T, state, hidden = (mem["mix_" + n][:, :, :].rearrange(by_feature, c=DC)
                                       for n in ("heads_T", "u_T", "state", "hidden"))
        h2 = sb("mix_h2", [P, 2, TT, D], FP32)
        u2_T = sb("mix_u2_T", [P, DC, S], FP32)
        back = sb("mix_back", [P, 4, S], FP32)
        gate = sb("mix_gate", [P, FC, S], FP32)
        act_T = sb("mix_act_T", [P, FC, S], FP32)
        stats = sb("mix_stats", [P, TT, 6], FP32)
        mv = sb("mix_mv", [P, TT, 2], FP32)
        rstd = sb("mix_rstd", [P, TT], FP32)
        probs = sb("mix_probs", [P, TT, E], FP32)
        for name, shape in (("counts", [P, E]), ("need", [P, E]), ("ends", [P, E]), ("tile_f", [P, 2, TILES])):
            mem[name] = sb(name, shape, FP32)
        chosen = sb("mix_chosen", [P, TT + 1, E], BF16)
        cls_moments = sb("cls_moments", [P, 2, 6], FP32)
        cls_mv = sb("cls_mv", [P, 2, 2], FP32)
        cls_rstd = sb("cls_rstd", [P, 2], FP32)
        cls_probs = sb("cls_probs", [P, 1, E], FP32)
        cls_h = mem["cls_h"][:, :]
        cls_u, cls_ud, cls_u2 = (h2[:, 1, n, :] for n in range(3))
        cls_u_T, cls_state, cls_u2_T = gate[:, 0:2, P:2 * P], gate[:, 2:4, P:2 * P], gate[:, 0:2, 2 * P:3 * P]
        cls_gate, cls_act_T = gate[:, :, 0:P], act_T[:, :, 0:P]
        turn = pb("mix_turn", [P, DC, S], FP32)
        made = pb("mix_made", [P, 2, S], FP32)
        pairs = pb("mix_pairs", [P, 2, 2, S], FP32)
        cls_ps = [pairs[:, n // 2, n % 2, :] for n in range(4)]
        names = ("heads_in heads_turned hT_copied out_made h_done stats1 pow1 u_done ud_done u_turned uT_copied "
                 "bu_made state_done y_made h2_done stats2 pow2 u2_done u2_turned u2T_copied logits_made "
                 "logits_biased sigmoid chosen_done counts_made counts_read slots_ready slots_out "
                 "gate_made gate_done act_done down_made acc_done u2_stored "
                 "cls_stats cls_pow cls_u cls_turned cls_copied cls_y cls_h2 cls_logits cls_biased cls_sigmoid "
                 "cls_up cls_silu cls_act cls_down cls_done cls_slots cls_stored "
                 "cls_steps tile_steps scatter_begun stats_ready ln_steps scan_steps top_steps slot_steps")
        ev = {n: sem("mix_" + n) for n in names.split()}
        ev["acc_stored"] = mem["acc_stored"]
        block = ctx.enter_context(nc.Block())
        cos, sin = mem["cos"][:, 1:T1], mem["sin"][:, 1:T1]
        out_rows = dram["out"]

        def batches(eng, step):
            step(0, 0, False, True, True)
            with eng.Fori(0, (B - 2) // 2) as i:
                for par in range(2):
                    step(2 * i + par + 1, 1 - par, True, True, True)
            step(B - 1, 1, True, True, False)
            step(B, 0, True, False, False)

        @block.sync
        def _(sp):

            def step(b, par, prev, this, nxt):
                if nxt:
                    sp.wait_ge(mem["heads_stored"], 16 * B)
                    sp.wait_ge(ev["heads_turned"], b + 1)
                    sp.dma_start(heads[:, :, :].rearrange("p t n -> p (t n)"),
                                 dram["heads"][bass.ds(b + 1, 1), :, :].rearrange("b p n -> p (b n)")
                                 ).then_inc(ev["heads_in"], 16)
                if not prev:
                    for name, rows, done in (("x_rows", cls_u2, "cls_h2"), ("out", cls_h, "cls_done")):
                        sp.wait_ge(ev[done], 2 if name == "x_rows" else 1)
                        sp.dma_start(dram[name][0:ROWS, :].rearrange("(b t) n -> b t n", t=T1)[:, 0, :],
                                     rows[0:B, :]).then_inc(ev["cls_stored"], 16)
                if this:
                    for name in ("wg_e", "wu_e", "wd_e"):
                        sp.dma_start(mem[name][:, bass.ds(b, 1), :, :], dram[name][:, bass.ds(b, 1), :, :]
                                     ).then_inc(mem["experts_in"], 16)
                    sp.wait_ge(ev["u2_done"], b + 1)
                    sp.dma_start(dram["x_rows"][bass.ds(T1 * b + 1, S), :].rearrange("(t p) n -> p t n", p=P),
                                 u[:, :, :]).then_inc(ev["u2_stored"], 16)
                if prev:
                    sp.wait_ge(ev["acc_done"], 2 * b)
                    sp.dma_start(out_rows[bass.ds(T1 * b - T1 + 1, S), :].rearrange("(t p) n -> p t n", p=P),
                                 h2[:, 1 - par, :, :]).then_inc(ev["acc_stored"], 16)

            batches(sp, step)
            sp.wait_ge(ev["u2_stored"], 16 * B)

        @block.gpsimd
        def _(pool):
            def inverse_deviation(b, which):
                pool.wait_ge(ev[f"stats{which}"], b + 1)
                pool.tensor_tensor(rstd[:, :], mv[:, :, 1], mem["minus_half"][:, 0:TT], ALU.pow).then_inc(ev[f"pow{which}"], 1)

            def step(b, par, prev, this, nxt):
                if this:
                    pool.wait_ge(ev["u_done"], b + 1)
                    pool.tensor_tensor(ud[:, :, :], u[:, :, :], mem["d_row"][:, :].unsqueeze(1).to_broadcast([P, TT, D]),
                                       ALU.mult).then_inc(ev["ud_done"], 1)
                    pool.wait_ge(ev["ud_done"], 2 * b + 1)
                    if prev:
                        pool.wait_ge(ev["acc_stored"], 16 * (b - 1))
                        pool.wait_ge(ev["cls_stored"], 32)
                    pool.tensor_tensor(h2[:, par, :, :], ud[:, :, :], h[:, :, :], ALU.add).then_inc(ev["ud_done"], 1)
                    inverse_deviation(b, 2)
                if not prev:
                    pool.wait_ge(ev["cls_slots"], 1)
                    for n in range(2):
                        pool.indirect_dma_start(
                            out=dram["table"], in_=mem["pay"][:, 0, n, :], in_offset=None,
                            out_offset=bass.IndirectOffsetOnAxis(ap=mem["slot_i"][:, 0, n:n + 1].bitcast(U32), axis=0)
                        ).then_inc(ev["slots_out"], 16)
                if prev:
                    pool.wait_ge(ev["slots_ready"], b)
                    pool.sem_inc(ev["scatter_begun"])
                    for t in range(TT):
                        for n in range(2):
                            pool.indirect_dma_start(
                                out=dram["table"], in_offset=None, in_=mem["pay"][:, t, n, :],
                                out_offset=bass.IndirectOffsetOnAxis(
                                    ap=mem["slot_i"][:, t, n:n + 1].bitcast(U32), axis=0)).then_inc(ev["slots_out"], 16)
                if nxt:
                    inverse_deviation(b + 1, 1)
                if not this:
                    for n in POOL_CUTS[0]:
                        cut_weights(pool, mem, n).then_inc(mem["ev_cut"]["pool"], 1)
                        pool.wait_ge(mem["ev_cut"]["pool"], n + 1)

            def class_deviation(n):
                pool.wait_ge(ev["cls_stats"], n + 1)
                pool.tensor_tensor(cls_rstd[:, n:n + 1], cls_mv[:, n, 1:2], mem["minus_half"][:, 0:1],
                                   ALU.pow).then_inc(ev["cls_pow"], 1)

            class_deviation(0)
            class_deviation(1)
            inverse_deviation(0, 1)
            batches(pool, step)
            pool.wait_ge(ev["slots_out"], 16 * (2 + 2 * TT * B))

        @block.scalar
        def _(act):
            def silu(j, m):
                act.wait_ge(ev["gate_made"], FC * j + m + 1)
                act.wait_ge(ev["act_done"], FC * j)
                act.activation(gate[:, m, :], pairs[:, m % 2, 0, :], ACT.Silu).then_inc(ev["gate_done"], 1)

            def copy_turned(to, b, turned, copied):
                act.wait_ge(ev[turned], b + 1)
                act.activation(to[:, :, :], turn[:, :, :], ACT.Copy).then_inc(ev[copied], 1)

            def class_copy(n, to, bank):
                act.wait_ge(ev["cls_turned"], n + 1)
                act.activation(to, cls_ps[bank][:, 0:D].rearrange("p (c n) -> p c n", c=2), ACT.Copy).then_inc(ev["cls_copied"], 1)

            def step(b, par, prev, this, nxt):
                if this:
                    copy_turned(u_T, b, "u_turned", "uT_copied")
                if prev:
                    silu(b - 1, 1)
                    if not this:
                        act.wait_ge(mem["experts_in"], 16 * 3 * E)
                        for n in range(3):
                            shorten_weights(act, mem, n)
                    silu(b - 1, 2)
                    if not this:
                        for n in range(3, 6):
                            shorten_weights(act, mem, n)
                if nxt:
                    copy_turned(heads_T, b + 1, "heads_turned", "hT_copied")
                if prev:
                    silu(b - 1, 3)
                    if not this:
                        act.wait_ge(ev["u2_stored"], 16 * B)
                        for n in range(6, E):
                            shorten_weights(act, mem, n)
                if this:
                    copy_turned(u2_T, b, "u2_turned", "u2T_copied")
                    act.wait_ge(ev["logits_biased"], b + 1)
                    act.activation(probs[:, :, :], probs[:, :, :], ACT.Sigmoid).then_inc(ev["sigmoid"], 1)
                    silu(b, 0)

            class_copy(0, cls_u_T, 0)
            class_copy(1, cls_state, 1)
            copy_turned(heads_T, 0, "heads_turned", "hT_copied")
            class_copy(2, cls_u2_T, 3)
            act.wait_ge(ev["cls_biased"], 1)
            act.activation(cls_probs[:, :, :], cls_probs[:, :, :], ACT.Sigmoid).then_inc(ev["cls_sigmoid"], 1)
            act.wait_ge(ev["cls_up"], 1)
            act.activation(cls_gate, cls_ps[1].rearrange("p (m n) -> p m n", m=FC), ACT.Silu).then_inc(ev["cls_silu"], 1)
            batches(act, step)

        @block.tensor
        def _(pe):
            def turn_rows(rows, done):
                for c in range(DC):
                    for t in range(TT):
                        mm = pe.transpose(turn[:, c, t * P:(t + 1) * P], rows[:, t, c * P:(c + 1) * P], ident[:, :])
                mm.then_inc(ev[done], 1)

            def turn_heads(b):
                if not (isinstance(b, int) and b == 0):
                    pe.wait_ge(ev["heads_in"], 16 * b)
                turn_rows(heads, "heads_turned")

            def by_token(lhs, w, done):
                for t in range(TT):
                    for c in range(DC):
                        mm = pe.matmul(made[:, t // 2, (t % 2) * D:(t % 2 + 1) * D], lhs[:, c, t * P:(t + 1) * P],
                                       w[:, c, :], start=(c == 0), stop=(c == DC - 1))
                    if t % 2:
                        mm.then_inc(ev[done], 1)

            def project_out(b):
                pe.wait_ge(ev["hT_copied"], b + 1)
                pe.wait_ge(ev["h2_done"], 2 * b)
                by_token(heads_T, mem["wo_T"], "out_made")

            def shared_up(j, m):
                if m == 0:
                    pe.wait_ge(ev["acc_done"], 2 * j)
                elif m >= 2:
                    pe.wait_ge(ev["act_done"], FC * j + m - 1)
                for n, w in enumerate((mem["wg_s"], mem["wu_s"])):
                    for c in range(DC):
                        mm = pe.matmul(pairs[:, m % 2, n, :], w[:, c, m * P:(m + 1) * P], u2_T[:, c, :],
                                       start=(c == 0), stop=(c == DC - 1))
                mm.then_inc(ev["gate_made"], 1)

            def shared_down(j, half):
                pe.wait_ge(ev["act_done"], FC * j + FC)
                for t in (2 * half, 2 * half + 1):
                    for m in range(FC):
                        mm = pe.matmul(pairs[:, 0, half, (t % 2) * D:(t % 2 + 1) * D], act_T[:, m, t * P:(t + 1) * P],
                                       mem["wd_s"][:, m, :], start=(m == 0), stop=(m == FC - 1))
                mm.then_inc(ev["down_made"], 1)

            def count(j, nxt):
                pe.wait_ge(ev["chosen_done"], j + 1)
                if nxt:
                    pe.wait_ge(ev["hT_copied"], j + 3)
                pos = turn[:, 1, 0:(TT + 1) * E].rearrange("p (t e) -> p t e", e=E)
                pe.matmul(pos, mem["before"][:, :], chosen[:, :, :], start=True, stop=False)
                for k in range(1, TT + 1):
                    mm = pe.matmul(pos[:, k:TT + 1, :], mem["all_ones"][:, :], chosen[:, 0:TT + 1 - k, :],
                                   start=False, stop=(k == TT))
                mm.then_inc(ev["counts_made"], 1)

            def step(b, par, prev, this, nxt):
                if this:
                    pe.wait_ge(ev["u_done"], b + 1)
                    pe.wait_ge(ev["logits_biased"], b)
                    turn_rows(u, "u_turned")
                if prev:
                    if not this:
                        count(b - 1, nxt)
                    shared_up(b - 1, 1)
                if this:
                    pe.wait_ge(ev["uT_copied"], b + 1)
                    for m in range(2):
                        for c in range(DC):
                            mm = pe.matmul(made[:, m, :], mem["m1_T"][:, c, m * P:(m + 1) * P], u_T[:, c, :],
                                           start=(c == 0), stop=(c == DC - 1))
                    mm.then_inc(ev["bu_made"], 1)
                if prev:
                    shared_up(b - 1, 2)
                if not prev:
                    class_down()
                if nxt:
                    turn_heads(b + 1)
                if prev:
                    shared_up(b - 1, 3)
                    if this:
                        count(b - 1, nxt)
                if this:
                    pe.wait_ge(ev["state_done"], b + 1)
                    by_token(hidden, mem["m2_T"], "y_made")
                if prev:
                    shared_down(b - 1, 0)
                    shared_down(b - 1, 1)
                if this:
                    pe.wait_ge(ev["u2_done"], b + 1)
                    pe.wait_ge(ev["counts_read"], b)
                    if nxt:
                        pe.wait_ge(ev["hT_copied"], b + 2)
                    turn_rows(u, "u2_turned")
                if nxt:
                    project_out(b + 1)
                if this:
                    pe.wait_ge(ev["u2T_copied"], b + 1)
                    for t in range(TT):
                        for c in range(DC):
                            mm = pe.matmul(turn[:, 0, t * E:(t + 1) * E], u2_T[:, c, t * P:(t + 1) * P],
                                           mem["wr_T"][:, c, :], start=(c == 0), stop=(c == DC - 1))
                    mm.then_inc(ev["logits_made"], 1)
                    if not prev:
                        pe.wait_ge(ev["cls_done"], 1)
                    shared_up(b, 0)

            def class_product(bank, lhs, w, width, done):
                for c in range(2):
                    mm = pe.matmul(cls_ps[bank][:, 0:width], lhs[:, c, :], w[:, c, :], start=(c == 0), stop=(c == 1))
                mm.then_inc(ev[done], 1)

            def class_turn(bank, rows):
                for c in range(2):
                    mm = pe.transpose(cls_ps[bank][:, c * P:(c + 1) * P], rows[:, c * P:(c + 1) * P], ident[:, :])
                mm.then_inc(ev["cls_turned"], 1)

            def class_mix():
                pe.wait_ge(ev["cls_u"], 1)
                class_turn(0, cls_u)
                pe.wait_ge(ev["cls_copied"], 1)
                for m in range(2):
                    for c in range(2):
                        mm = pe.matmul(cls_ps[1][:, m * P:(m + 1) * P], mem["m1_T"][:, c, m * P:(m + 1) * P], cls_u_T[:, c, :],
                                       start=(c == 0), stop=(c == 1))
                mm.then_inc(ev["cls_turned"], 1)
                pe.wait_ge(ev["cls_copied"], 2)
                class_product(2, cls_state, mem["m2_T"], D, "cls_y")

            def class_up():
                pe.wait_ge(ev["cls_h2"], 2)
                class_turn(3, cls_u2)
                pe.wait_ge(ev["cls_copied"], 3)
                class_product(0, cls_u2_T, mem["wr_T"], E, "cls_logits")
                for bank, w in ((1, mem["wg_s"]), (2, mem["wu_s"])):
                    for m in range(FC):
                        for c in range(2):
                            mm = pe.matmul(cls_ps[bank][:, m * P:(m + 1) * P], w[:, c, m * P:(m + 1) * P], cls_u2_T[:, c, :],
                                           start=(c == 0), stop=(c == 1))
                mm.then_inc(ev["cls_up"], 1)

            def class_down():
                pe.wait_ge(ev["cls_act"], 1)
                for m in range(FC):
                    mm = pe.matmul(cls_ps[3][:, 0:D], cls_act_T[:, m, :], mem["wd_s"][:, m, :], start=(m == 0), stop=(m == FC - 1))
                mm.then_inc(ev["cls_down"], 1)

            class_mix()
            turn_heads(0)
            project_out(0)
            class_up()
            batches(pe, step)

        @block.vector
        def _(dve):
            def shared_act(j, m):
                dve.wait_ge(ev["gate_done"], FC * j + m + 1)
                dve.wait_ge(ev["down_made"], 2 * j)
                dve.tensor_tensor(act_T[:, m, :], gate[:, m, :], pairs[:, m % 2, 1, :], ALU.mult).then_inc(ev["act_done"], 1)

            def shared_add(j, par, half):
                dve.wait_ge(ev["down_made"], 2 * j + half + 1)
                rows = h2[:, par, 2 * half:2 * half + 2, :]
                dve.tensor_tensor(rows, pairs[:, 0, half, :].rearrange("p (t n) -> p t n", t=2), rows,
                                  ALU.add).then_inc(ev["acc_done"], 1)

            def sum_and_statistics(b, rows, term, which, link):
                product, done = (("out_made", "h_done"), ("y_made", "h2_done"))[which - 1]
                for n in range(2):
                    dve.wait_ge(ev[product], 2 * b + n + 1)
                    pair = rows[:, 2 * n:2 * n + 2, :]
                    dve.tensor_tensor(pair, made[:, n, :].rearrange("p (t n) -> p t n", t=2),
                                      pair if term is None else term, ALU.add).then_inc(ev[done], 1)
                    dve.wait_ge(ev[done], 2 * b + n + 1)
                    for t in (2 * n, 2 * n + 1):
                        link(dve.bn_stats(stats[:, t, :], rows[:, t, :]), wait=(t == TT - 1))
                dve.sem_inc(ev["stats_ready"])
                for t in range(TT):
                    link(dve.bn_aggr(mv[:, t, :], stats[:, t, :]), wait=(t == TT - 1))
                dve.tensor_scalar(mv[:, :, 1], mv[:, :, 1], EPS, None, ALU.add).then_inc(ev[f"stats{which}"], 1)

            def normalise(b, rows, which):
                dve.wait_ge(ev[f"pow{which}"], b + 1)
                for t in range(TT):
                    last = dve.tensor_scalar(u[:, t, :], rows[:, t, :], mv[:, t, 0:1], rstd[:, t:t + 1],
                                             ALU.subtract, ALU.mult)
                last.then_inc(ev["u_done" if which == 1 else "u2_done"], 1)

            def place(j):
                link = chain(dve, ev["slot_steps"], (SLOT_STEPS + 2) * j)
                pos = turn[:, 1, 0:TT * E].rearrange("p (t e) -> p t e", e=E)
                dve.wait_ge(ev["counts_made"], j + 1)
                dve.wait_ge(ev["counts_read"], j)
                dve.wait_ge(ev["slots_out"], 16 * (2 * TT * j + 2))
                link(dve.tensor_tensor(mem["pos"][:, :, :], pos, mem["next_slot"][:, :].unsqueeze(1).to_broadcast([P, TT, E]),
                                       ALU.add))
                dve.tensor_tensor(mem["next_slot"][:, :], turn[:, 1, TT * E:(TT + 1) * E], mem["next_slot"][:, :],
                                  ALU.add).then_inc(ev["counts_read"], 1)
                slot_rows(dve, link, mem, TT, mem["row_id"][:, :])
                link(dve.tensor_scalar(mem["row_id"][:, :], mem["row_id"][:, :], float(T1), None, ALU.add))
                dve.tensor_copy(mem["slot_i"][:, :, :], mem["slot_f"][:, :, :]).then_inc(ev["slots_ready"], 1)

            def first_sum(b):
                dve.wait_ge(ev["ud_done"], 2 * b)
                sum_and_statistics(b, h, mem["bo_row"][:, :].unsqueeze(1).to_broadcast([P, 2, D]), 1,
                                   chain(dve, ev["ln_steps"], 4 * TT * b))

            def step(b, par, prev, this, nxt):
                scan = chain(dve, ev["scan_steps"], 7 * b)
                if prev:
                    dve.wait_ge(ev["sigmoid"], b)
                    top_two(dve, chain(dve, ev["top_steps"], TOP_STEPS * (b - 1)), mem, probs[:, :, :], TT)
                    dve.tensor_tensor(chosen[:, 0:TT, :], mem["hot"][:, :, 0, :], mem["hot"][:, :, 1, :],
                                      ALU.add).then_inc(ev["chosen_done"], 1)
                    shared_act(b - 1, 0)
                    if not this:
                        place(b - 1)
                    shared_act(b - 1, 1)
                    if not this:
                        cut_weights(dve, mem, DVE_CUTS[0][0]).then_inc(mem["ev_cut"]["dve"], 1)
                if this:
                    dve.wait_ge(ev["bu_made"], b + 1)
                    dve.tensor_tensor(back[:, 0, :], made[:, 0, :], cos, ALU.mult)
                    scan(dve.tensor_tensor(back[:, 1, :], made[:, 1, :], sin, ALU.mult), wait=False)
                    dve.tensor_tensor(back[:, 2, :], made[:, 1, :], cos, ALU.mult)
                    scan(dve.tensor_tensor(back[:, 3, :], made[:, 0, :], sin, ALU.mult))
                    scan(dve.tensor_tensor_scan(state[:, 0, :], back[:, 0, :], back[:, 1, :], mem["state0"][:, 0:1],
                                                ALU.add, ALU.add), wait=False)
                    scan(dve.tensor_tensor_scan(state[:, 1, :], back[:, 2, :], back[:, 3, :], mem["state0"][:, 1:2],
                                                ALU.add, ALU.subtract))
                if this:
                    dve.tensor_tensor(back[:, 0, :], state[:, 0, :], cos, ALU.mult)
                    scan(dve.tensor_tensor(back[:, 1, :], state[:, 1, :], sin, ALU.mult), wait=False)
                    dve.tensor_tensor(back[:, 2, :], state[:, 0, :], sin, ALU.mult)
                    scan(dve.tensor_tensor(back[:, 3, :], state[:, 1, :], cos, ALU.mult))
                    dve.wait_ge(ev["y_made"], 2 * b)
                    scan(dve.tensor_tensor(hidden[:, 0, :], back[:, 0, :], back[:, 1, :], ALU.subtract), wait=False)
                    dve.tensor_tensor(hidden[:, 1, :], back[:, 2, :], back[:, 3, :], ALU.add).then_inc(ev["state_done"], 1)
                if not prev:
                    class_choose()
                if prev:
                    shared_act(b - 1, 2)
                    if not this:
                        cut_weights(dve, mem, DVE_CUTS[0][1]).then_inc(mem["ev_cut"]["dve"], 1)
                    shared_act(b - 1, 3)
                    if this:
                        place(b - 1)
                    else:
                        dve.wait_ge(ev["counts_read"], b)
                        list_tiles(dve, chain(dve, ev["tile_steps"], 0), mem,
                                   back[:, :, :].rearrange("p n s -> p (n s)"))
                if this:
                    dve.wait_ge(ev["ud_done"], 2 * b + 2)
                    sum_and_statistics(b, h2[:, par, :, :], None, 2, chain(dve, ev["ln_steps"], 4 * TT * b + 2 * TT))
                if prev:
                    shared_add(b - 1, 1 - par, 0)
                if this:
                    normalise(b, h2[:, par, :, :], 2)
                if prev:
                    shared_add(b - 1, 1 - par, 1)
                else:
                    class_place()
                    class_add()
                if nxt:
                    first_sum(b + 1)
                if this:
                    dve.wait_ge(ev["logits_made"], b + 1)
                    dve.tensor_tensor(probs[:, :, :], turn[:, 0, 0:TT * E].rearrange("p (t e) -> p t e", e=E),
                                      mem["rb_row"][:, :].unsqueeze(1).to_broadcast([P, TT, E]),
                                      ALU.add).then_inc(ev["logits_biased"], 1)
                if nxt:
                    dve.wait_ge(ev["u2_stored"], 16 * b + 16)
                    normalise(b + 1, h, 1)

            cls_link = chain(dve, ev["cls_steps"], 0)
            cls_link(dve.memset(chosen[:, TT, :], 0.0))

            def class_norm(n, to, done):
                cls_link(dve.bn_stats(cls_moments[:, n, :], cls_h))
                cls_link(dve.bn_aggr(cls_mv[:, n, :], cls_moments[:, n, :]))
                dve.tensor_scalar(cls_mv[:, n, 1:2], cls_mv[:, n, 1:2], EPS, None, ALU.add).then_inc(ev["cls_stats"], 1)
                dve.wait_ge(ev["cls_pow"], n + 1)
                dve.tensor_scalar(to, cls_h, cls_mv[:, n, 0:1], cls_rstd[:, n:n + 1], ALU.subtract, ALU.mult).then_inc(ev[done], 1)

            def class_mix():
                class_norm(0, cls_u, "cls_u")
                dve.wait_ge(ev["cls_u"], 1)
                cls_link(dve.tensor_tensor(cls_ud, cls_u, mem["d_row"][:, :], ALU.mult))
                cls_link(dve.tensor_tensor(cls_h, cls_h, cls_ud, ALU.add))
                dve.wait_ge(ev["cls_copied"], 2)
                dve.tensor_copy(mem["state0"][:, :], cls_state[:, :, 0])
                dve.wait_ge(ev["cls_y"], 1)
                dve.tensor_tensor(cls_h, cls_h, cls_ps[2][:, 0:D], ALU.add).then_inc(ev["cls_h2"], 1)
                dve.wait_ge(ev["cls_h2"], 1)
                class_norm(1, cls_u2, "cls_h2")

            def class_bias():
                dve.wait_ge(ev["cls_logits"], 1)
                dve.tensor_tensor(cls_probs[:, 0, :], cls_ps[0][:, 0:E], mem["rb_row"][:, :], ALU.add).then_inc(ev["cls_biased"], 1)

            def class_act():
                dve.wait_ge(ev["cls_silu"], 1)
                dve.tensor_tensor(cls_act_T, cls_gate, cls_ps[2].rearrange("p (m n) -> p m n", m=FC),
                                  ALU.mult).then_inc(ev["cls_act"], 1)

            def class_choose():
                dve.wait_ge(ev["cls_sigmoid"], 1)
                top_two(dve, cls_link, mem, cls_probs[:, :, :], 1)

            def class_place():
                cls_link(dve.tensor_copy(mem["pos"][:, 0, :], mem["slot0"][:, :]))
                slot_rows(dve, cls_link, mem, 1, mem["cls_ids"][:, :])
                next_slot, slot_f = mem["next_slot"][:, :], mem["slot_f"][:, 0, :]
                cls_link(dve.tensor_tensor(next_slot, mem["hot"][:, 0, 0, :], mem["hot"][:, 0, 1, :], ALU.add))
                cls_link(dve.tensor_scalar(next_slot, next_slot, float(B), None, ALU.mult))
                cls_link(dve.tensor_tensor(next_slot, next_slot, mem["slot0"][:, :], ALU.add))
                cls_link(dve.tensor_scalar(slot_f, slot_f, mem["first"][:, 0:1], None, ALU.mult))
                cls_link(dve.tensor_tensor(slot_f, slot_f, mem["spare"][:, :], ALU.add))
                dve.tensor_copy(mem["slot_i"][:, 0, :], slot_f).then_inc(ev["cls_slots"], 1)

            def class_add():
                dve.wait_ge(ev["cls_down"], 1)
                dve.tensor_tensor(cls_h, cls_h, cls_ps[3][:, 0:D], ALU.add).then_inc(ev["cls_done"], 1)

            class_mix()
            first_sum(0)
            normalise(0, h, 1)
            class_bias()
            class_act()
            batches(dve, step)


def list_tiles(dve, link, mem, scratch):
    counts, need, ends, tile_f = (mem[n] for n in ("counts", "need", "ends", "tile_f"))
    over = scratch[:, 0:E * CAP].rearrange("p (e n) -> p e n", e=E)
    passed, skipped = (scratch[:, n:n + TILES * E].rearrange("p (n e) -> p n e", e=E) for n in (0, 2 * S))
    index = mem["tile_index"][:, 0:TILES]
    link(dve.tensor_tensor(counts[:, :], mem["next_slot"][:, :], mem["slot0"][:, :], ALU.subtract))
    link(dve.tensor_tensor(over, counts[:, :].unsqueeze(2).to_broadcast([P, E, CAP]),
                           mem["tile_rows"][:, 0:CAP].unsqueeze(1).to_broadcast([P, E, CAP]), ALU.is_gt))
    link(dve.tensor_reduce(need[:, :], over, AX.X, ALU.add))
    link(dve.tensor_tensor_scan(ends[:, :], mem["ones_e"][:, :], need[:, :], 0.0, ALU.mult, ALU.add))
    link(dve.tensor_scalar(need[:, :], need[:, :], -1.0, float(CAP), ALU.mult, ALU.add))
    link(dve.tensor_tensor(passed, index.unsqueeze(2).to_broadcast([P, TILES, E]),
                           ends[:, :].unsqueeze(1).to_broadcast([P, TILES, E]), ALU.is_ge))
    link(dve.tensor_reduce(tile_f[:, 1, :], passed, AX.X, ALU.add))
    link(dve.tensor_scalar(tile_f[:, 1, :], tile_f[:, 1, :], float(E - 1), None, ALU.min))
    link(dve.tensor_tensor(skipped, passed, need[:, :].unsqueeze(1).to_broadcast([P, TILES, E]), ALU.mult))
    link(dve.tensor_reduce(tile_f[:, 0, :], skipped, AX.X, ALU.add))
    link(dve.tensor_tensor(tile_f[:, 0, :], tile_f[:, 0, :], index, ALU.add))
    dve.tensor_copy(mem["tile_i"][:, :, :], tile_f[:, :, :])


def stage_experts(nc, mem, dram):
    ident = mem["ident"]
    R = RING
    X = 4
    with ExitStack() as ctx:
        sb, pb, sem = places(nc, ctx)
        tile_i = mem["tile_i"]
        sb("weights_place", [P, 4, E, DC, F], FP32)
        wg_rest, wu_rest, wg_short, wu_short = (mem[n] for n in ("wg_rest", "wu_rest", "wg_short", "wu_short"))
        slot = sb("slot", [P, R, 2], I32)
        x_in = sb("x_in", [P, X, D], FP32)
        x_T = sb("x_T2", [P, 2, DC, P], FP32)
        x_rest = sb("x_rest", [P, 2, DC, P], FP32)
        gate = sb("gate", [P, 2, F], FP32)
        acts = sb("acts", [P, 2, F], FP32)
        acts_T = sb("acts_T", [P, FC, P], FP32)
        y = sb("y", [P, 2, D], FP32)
        ps_up = pb("ps_up", [P, 2, 2, F], FP32)
        ps_x = pb("ps_x", [P, S], FP32)
        ps_a = pb("ps_a", [P, S], FP32)
        ps_y = pb("ps_y", [P, 2, S], FP32)
        slot_in = [sem(f"slot_in{r}") for r in range(R)]
        y_added = sem("y_added")
        x_gathered = [sem(f"x_gathered{r}") for r in range(X)]
        names = ("x_turned xT_copied x_cut gate_made up_made silu acts_done acts_turned aT_copied down_made y_done "
                 "dma_begun")
        ev = {n: sem("x_" + n) for n in names.split()}
        block = ctx.enter_context(nc.Block())
        LOOPS = TILES // R
        @block.sync
        def _(sp):
            def load_slot(i, r):
                q = sp.value_load(tile_i[0:1, 0, bass.ds(R * i + r, 1)], min_val=0, max_val=SLOTS // P - 1)
                sp.dma_start(slot[:, r, :], dram["table"][bass.ds(q * P, P), :]).then_inc(slot_in[r], 16)

            for r in range(R):
                load_slot(0, r)
            with sp.Fori(0, LOOPS - 1) as i:
                for r in range(R):
                    sp.wait_ge(y_added, 16 * (R * i + r + 1))
                    load_slot(i + 1, r)
            sp.wait_ge(y_added, 16 * TILES)

        @block.gpsimd
        def _(pool):
            def gather(i, r):
                pool.wait_ge(slot_in[r % R], 16 * (i + r // R) + 16)
                if not (isinstance(i, int) and i == 0 and r < X):
                    pool.wait_ge(ev["x_turned"], R * i + r - X + 1)
                pool.sem_inc(ev["dma_begun"])
                pool.indirect_dma_start(
                    out=x_in[:, r % X, :], out_offset=None, in_=dram["x_rows"],
                    in_offset=bass.IndirectOffsetOnAxis(ap=slot[:, r % R, 0:1].bitcast(U32), axis=0)
                ).then_inc(x_gathered[r % X], 16)

            def add(i, r):
                pool.wait_ge(ev["y_done"], R * i + r + 1)
                pool.wait_ge(y_added, 16 * (R * i + r))
                pool.sem_inc(ev["dma_begun"])
                pool.indirect_dma_start(
                    out=dram["out"], in_=y[:, r % 2, :], in_offset=None, compute_op=ALU.add,
                    out_offset=bass.IndirectOffsetOnAxis(ap=slot[:, r, 0:1].bitcast(U32), axis=0)
                ).then_inc(y_added, 16)

            pool.wait_ge(mem["acc_stored"], 16 * B)
            for r in range(X):
                gather(0, r)
            for n in POOL_CUTS[1]:
                cut_weights(pool, mem, n).then_inc(mem["ev_cut"]["pool"], 1)
                pool.wait_ge(mem["ev_cut"]["pool"], len(POOL_CUTS[0]) + POOL_CUTS[1].index(n) + 1)
            with pool.Fori(0, LOOPS - 1) as i:
                for r in range(R):
                    add(i, r)
                    gather(i, r + X)
            for r in range(R):
                add(LOOPS - 1, r)
                if r < R - X:
                    gather(LOOPS - 1, r + X)

        @block.tensor
        def _(pe):
            def turn_x(i, r):
                t = R * i + r
                pe.wait_ge(x_gathered[r % X], 16 * (R // X * i + r // X) + 16)
                pe.wait_ge(ev["x_cut"], t)
                for c in range(DC):
                    mm = pe.transpose(ps_x[:, c * P:(c + 1) * P], x_in[:, r % X, c * P:(c + 1) * P], ident[:, :])
                mm.then_inc(ev["x_turned"], 1)

            def up(t, par, which, e):
                w = (wg_short, wg_rest) if which == 0 else (wu_short, wu_rest)
                if which == 0:
                    pe.wait_ge(ev["x_cut"], t + 1)
                    if not (isinstance(t, int) and t == 0):
                        pe.wait_ge(ev["acts_done"], t - 1)
                for c in range(DC):
                    mm = split_products(pe, ps_up[:, par, which, :], (x_T[:, par, c, :], x_rest[:, par, c, :]),
                                        [part[:, bass.ds(e, 1), c, :] for part in w], start=(c == 0), stop=(c == DC - 1))
                mm.then_inc(ev["gate_made" if which == 0 else "up_made"], 1)

            def turn_acts(t, par):
                pe.wait_ge(ev["acts_done"], t + 1)
                pe.wait_ge(ev["aT_copied"], t)
                for m in range(FC):
                    mm = pe.transpose(ps_a[:, m * P:(m + 1) * P], acts[:, par, m * P:(m + 1) * P], ident[:, :])
                mm.then_inc(ev["acts_turned"], 1)

            def down(i, r, e):
                pe.wait_ge(ev["aT_copied"], R * i + r + 1)
                pe.wait_ge(ev["y_done"], R * i + max(r - 1, 0))
                for m in range(FC):
                    mm = pe.matmul(ps_y[:, r % 2, 0:D], acts_T[:, m, :], mem["wd_e"][:, bass.ds(e, 1), m, :],
                                   start=(m == 0), stop=(m == FC - 1))
                mm.then_inc(ev["down_made"], 1)

            def expert(t):
                return pe.value_load(tile_i[0:1, 1, bass.ds(t, 1)], min_val=0, max_val=E - 1)

            pe.wait_ge(mem["experts_in"], 16 * 3 * E)
            for t in range(2):
                turn_x(0, t)
            pe.wait_ge(mem["ev_cut"]["dve"], sum(map(len, DVE_CUTS)))
            pe.wait_ge(mem["ev_cut"]["pool"], sum(map(len, POOL_CUTS)))
            first = expert(0)
            for which in range(2):
                up(0, 0, which, first)

            def body(i, last):
                for r in range(R):
                    t, par = R * i + r, r % 2
                    more = not (last and r == R - 1)
                    if more:
                        following = expert(t + 1)
                        up(t + 1, 1 - par, 0, following)
                    turn_acts(t, par)
                    if not (last and r >= R - 2):
                        turn_x(i, r + 2)
                    if more:
                        up(t + 1, 1 - par, 1, following)
                    down(i, r, expert(t))

            with pe.Fori(0, LOOPS - 1) as i:
                body(i, False)
            body(LOOPS - 1, True)

        @block.scalar
        def _(act):
            def silu(t, par):
                act.wait_ge(ev["gate_made"], t + 1)
                if not (isinstance(t, int) and t == 0):
                    act.wait_ge(ev["acts_done"], t - 1)
                act.activation(gate[:, par, :], ps_up[:, par, 0, :], ACT.Silu).then_inc(ev["silu"], 1)

            def body(i, last):
                for r in range(R):
                    t, par = R * i + r, r % 2
                    if not (last and r == R - 1):
                        silu(t + 1, 1 - par)
                    act.wait_ge(ev["acts_turned"], t + 1)
                    act.wait_ge(ev["down_made"], t)
                    act.activation(acts_T[:, :, :], ps_a[:, :].rearrange("p (m n) -> p m n", m=FC),
                                   ACT.Copy).then_inc(ev["aT_copied"], 1)

            for n in range(E, 2 * E):
                if n == 2 * E - 1:
                    act.wait_ge(mem["acc_stored"], 16 * B)
                shorten_weights(act, mem, n)
            silu(0, 0)
            with act.Fori(0, LOOPS - 1) as i:
                body(i, False)
            body(LOOPS - 1, True)

        @block.vector
        def _(dve):
            def copy_x(t, par):
                dve.wait_ge(ev["x_turned"], t + 1)
                if not (isinstance(t, int) and t < 2):
                    dve.wait_ge(ev["up_made"], t - 1)
                turned = ps_x[:, 0:D].rearrange("p (c n) -> p c n", c=DC)
                dve.tensor_copy(short(x_T[:, par, :, :]), turned).then_inc(ev["xT_copied"], 1)
                dve.wait_ge(ev["xT_copied"], t + 1)
                dve.tensor_tensor(short(x_rest[:, par, :, :]), turned, x_T[:, par, :, :], ALU.subtract).then_inc(ev["x_cut"], 1)

            def act(t, par):
                dve.wait_ge(ev["silu"], t + 1)
                dve.wait_ge(ev["up_made"], t + 1)
                if not (isinstance(t, int) and t == 0):
                    dve.wait_ge(ev["acts_turned"], t - 1)
                dve.tensor_tensor(acts[:, par, :], gate[:, par, :], ps_up[:, par, 1, :], ALU.mult).then_inc(ev["acts_done"], 1)

            def weigh(i, r):
                dve.wait_ge(ev["down_made"], R * i + r + 1)
                if not (isinstance(i, int) and i == 0 and r < 2):
                    dve.wait_ge(y_added, 16 * (R * i + r - 1))
                dve.tensor_scalar(y[:, r % 2, :], ps_y[:, r % 2, 0:D], slot[:, r, 1:2].bitcast(FP32), None,
                                  ALU.mult).then_inc(ev["y_done"], 1)

            def body(i, last):
                for r in range(R):
                    t, par = R * i + r, r % 2
                    if not (last and r >= R - 2):
                        copy_x(t + 2, par)
                    if not (last and r == R - 1):
                        act(t + 1, 1 - par)
                    weigh(i, r)

            for n in DVE_CUTS[1]:
                cut_weights(dve, mem, n).then_inc(mem["ev_cut"]["dve"], 1)
            copy_x(0, 0)
            copy_x(1, 1)
            act(0, 0)
            body(0, False)
            with dve.Fori(1, LOOPS - 1) as i:
                body(i, False)
            body(LOOPS - 1, True)


INPUTS = ("x", "cls_tok", "L0_tok_w_qkv", "L0_tok_b_qkv", "L0_tok_w_out", "L0_tok_b_out", "L0_attn_a_params",
          "L0_attn_B_w", "L0_attn_C_w", "L0_attn_D", "L0_ffn_Wg_s", "L0_ffn_Wu_s", "L0_ffn_Wd_s", "L0_ffn_Wg",
          "L0_ffn_Wu", "L0_ffn_Wd", "L0_ffn_Wr", "L0_ffn_rb")


def laid_out(x, cls_tok, w_qkv, b_qkv, w_out, b_out, a_params, b_w, c_w, d, wg_s, wu_s, wd_s, wg, wu, wd, wr, rb):
    def chunks(w):
        return w.reshape(-1, P, w.shape[-1]).transpose(1, 0, 2)

    def experts(w):
        return w.transpose(0, 2, 1).reshape(E, -1, P, w.shape[1]).transpose(2, 0, 1, 3)

    w = w_qkv.reshape(H, 3, HD, D).transpose(3, 1, 0, 2).reshape(D, 3 * D)
    bias = b_qkv.reshape(H, 3, HD).transpose(1, 0, 2).reshape(3, D)
    return {
        "xT": x.reshape(B, S, D).transpose(0, 2, 1).reshape(B, DC, P, S), "cls": cls_tok.reshape(1, D),
        "wqkv": chunks(w), "bqk": bias[:2].reshape(4, P).T, "bv": bias[2:3], "wo_T": chunks(w_out.T),
        "bo": b_out.reshape(1, D), "a_params": a_params.reshape(P, 1), "b_w": chunks(b_w), "c_T": chunks(c_w.T),
        "d": d.reshape(1, D), "wg_s": chunks(wg_s.T), "wu_s": chunks(wu_s.T), "wd_s": chunks(wd_s.T),
        "wg_e": experts(wg), "wu_e": experts(wu), "wd_e": experts(wd), "wr_T": chunks(wr.T), "rb": rb.reshape(1, E),
    }


def constants():
    f32, n = np.float32, np.arange(D)
    k = np.arange(P)
    angle = 2 * np.pi / D * (np.outer(n, k) % D)
    nyquist = np.where(n % 2, -1.0, 1.0)
    to_planes = np.concatenate([np.cos(angle), -np.sin(angle)], 1)
    to_planes[:, P] = nyquist
    from_planes = 2.0 / D * to_planes
    from_planes[:, 0] /= 2
    from_planes[:, P] /= 2
    sine = -2 * np.sin(2 * np.pi / D * (np.outer(k + 1, k) % D))
    sine[P - 1] = 0
    rows = np.arange(SLOTS)
    p = np.arange(P)
    return {
        "ident": np.eye(P, dtype=f32),
        "before": (p[:, None] < p[None, :]).astype(f32),
        "sine": sine.astype(f32),
        "to_planes": to_planes.reshape(2, P, D).transpose(1, 0, 2).astype(f32),
        "from_planes": from_planes.reshape(2, P, D).transpose(1, 0, 2).astype(f32),
        "table_init": np.stack([ROWS + rows % P, 0 * rows], 1).astype(np.int32),
        "iota_e": np.tile(np.arange(E, dtype=f32), (P, 1)),
        "slot0": np.tile(np.arange(E, dtype=f32) * CAP * P, (P, 1)),
        "first": (p < B).astype(f32)[:, None],
        "spare": np.where(p[:, None] < B, p[:, None], SLOTS + p[:, None] + [[0, P]]).astype(f32),
        "cls_ids": np.where(p < B, T1 * p, 0).astype(f32)[:, None],
        "row_first": (1 + p[:, None] + P * np.arange(TT)[None, :]).astype(f32),
        "tile_index": np.tile(np.arange(TILES, dtype=f32), (P, 1)),
        "tile_rows": np.tile(np.arange(TILES, dtype=f32) * P, (P, 1)),
    }


def program(nc, dram):
    with ExitStack() as ctx:
        sb, _, sem = places(nc, ctx)
        mem = {"experts_in": sem("experts_in"), "heads_stored": sem("heads_stored"), "acc_stored": sem("acc_stored"),
               "ev_cut": {n: sem("weights_" + n) for n in ("shortened", "dve", "pool")}}

        def row(name):
            return dram[name].to_broadcast([P, dram[name].shape[1]])

        kept = {
            "ident": ([P, P], dram["ident"]), "bo_row": ([P, D], row("bo")), "d_row": ([P, D], row("d")),
            "wo_T": ([P, DC, D], dram["wo_T"]), "wr_T": ([P, DC, E], dram["wr_T"]), "rb_row": ([P, E], row("rb")),
            "wg_s": ([P, DC, F], dram["wg_s"]), "wu_s": ([P, DC, F], dram["wu_s"]), "wd_s": ([P, FC, D], dram["wd_s"]),
            "iota_e": ([P, E], dram["iota_e"]), "slot0": ([P, E], dram["slot0"]), "first": ([P, 1], dram["first"]),
            "spare": ([P, 2], dram["spare"]), "cls_ids": ([P, 1], dram["cls_ids"]),
            "cls_h": ([P, D], row("cls")), "row_id": ([P, TT], dram["row_first"]),
            "tile_index": ([P, TILES], dram["tile_index"]), "tile_rows": ([P, TILES], dram["tile_rows"]),
        }
        others = (
                ("identb", [P, P], BF16), ("before", [P, P], BF16), ("all_ones", [P, P], BF16), ("ones_e", [P, E], FP32),
                ("m1_T", [P, DC, D], FP32), ("m2_T", [P, 2, D], FP32), ("cos", [P, T1], FP32), ("sin", [P, T1], FP32),
                ("power", [P, 11, 2], FP32), ("state0", [P, 2], FP32), ("zeros", [P, D], FP32),
                ("minus_half", [P, TT], FP32),
                ("best", [P, TT, 2], FP32), ("hot", [P, TT, 2, E], FP32), ("eq", [P, TT, E], FP32), ("key", [P, TT, E], FP32),
                ("least", [P, TT], FP32), ("pos", [P, TT, E], FP32), ("slot_f", [P, TT, 2], FP32),
                ("slot_i", [P, TT, 2], I32), ("pay", [P, TT, 2, 2], I32), ("next_slot", [P, E], FP32),
                ("max_parts", [P, P // (G * TT), G * TT], BF16))
        for name, shape, dtype in (("ident", [P, P], FP32), ("wd_e", [P, E, FC, D], FP32), ("tile_i", [P, 2, TILES], I32)):
            mem[name] = sb("k_" + name, shape, dtype)
        with ExitStack() as later:
            for name in ("wg_rest", "wu_rest", "wg_short", "wu_short"):
                mem[name] = later.enter_context(nc.sbuf_tensor(name, [P, E, DC, F], FP32))
        until_cut = ctx.enter_context(ExitStack())
        for name in ("wg_e", "wu_e"):
            mem[name] = until_cut.enter_context(nc.sbuf_tensor("k_" + name, [P, E, DC, F], FP32))
        until_mixed = ctx.enter_context(ExitStack())
        sb2, _, _ = places(nc, until_mixed)
        for name in ("heads_in", "mix_heads_T", "mix_h", "mix_u_T", "mix_state", "mix_hidden", "mix_ud", "mix_u"):
            mem[name] = sb2("k_" + name, [P, TT, D], FP32)
        for name, shape, dtype in [(name, shape, FP32) for name, (shape, _) in kept.items()] + list(others):
            if name not in mem:
                mem[name] = sb2("k_" + name, shape, dtype)
        rows = mem["wg_e"][:, :, :, :].bitcast(BF16).rearrange("p g c (a s) -> p g (c a) s", s=S)
        mem["q_rows"], mem["k_rows"] = rows[:, 0:NG, :, :], rows[:, NG:2 * NG, :, :]
        mem["probs"] = mem["wu_e"][:, :, :, :]
        mem["heads"] = mem["wd_e"][:, 2, :, :]
        mem["v_unit"] = mem["wd_e"][:, 0:2, :, :].rearrange("p e m n -> p (e m n)").rearrange(
            "p (g t h w) -> p g t h w", g=NG, t=TT, h=G)
        loads = [(mem[name][tuple(slice(None) for _ in shape)], src) for name, (shape, src) in kept.items()]
        mem["later_loads"] = loads
        with ExitStack() as first:
            sb1, _, _ = places(nc, first)
            for name, shape in (("wqkv", [P, DC, 3 * D]), ("bqk", [P, 4]), ("bv", [P, D])):
                mem[name] = sb1("k_" + name, shape, FP32)
            mem["unit_in"] = [sem(f"unit_in{n}") for n in range(NG)]
            mem["first_loads"] = [(mem["wqkv"][:, :, :], dram["wqkv"]), (mem["bqk"][:, :], dram["bqk"]),
                                  (mem["bv"][:, :], row("bv"))]
            stage_qkv(nc, mem, dram)
        stage_attention(nc, mem, dram)
        stage_mix(nc, mem, dram)
        until_mixed.close()
        until_cut.close()
        stage_experts(nc, mem, dram)


def kernel(**inputs):
    import concourse.bacc as _bacc
    from concourse.bass_utils import run_bass_kernel_spmd as _run

    arrays = dict(constants(), **laid_out(*(np.asarray(inputs[name]) for name in INPUTS)))
    arrays = {name: np.ascontiguousarray(a) for name, a in arrays.items()}
    nc = _bacc.Bacc("TRN2", target_bir_lowering=False, num_devices=1)
    dram = {name: nc.dram_tensor("in_" + name, a.shape, mybir.dt.from_np(a.dtype), kind="ExternalInput").ap()
            for name, a in arrays.items()}
    for name, shape, dtype in (
            ("qk", (B, 2, PARTS, D, S), BF16), ("v", (B, P, TT * H * VW), FP32), ("heads", (B, P, TT * D), FP32),
            ("x_rows", (ROWS + P, D), FP32), ("table", (SLOTS + 2 * P, 2), I32)):
        dram[name] = nc.dram_tensor("kept_" + name, shape, dtype, kind="Internal").ap()
    dram["out"] = nc.dram_tensor("out_rows", (ROWS + P, D), FP32, kind="ExternalOutput").ap()
    program(nc, dram)
    result = _run(nc, [{"in_" + name: a for name, a in arrays.items()}], core_ids=[0])
    return result.results[0]["out_rows"][:ROWS].reshape(B, T1, D)
```
